# Optimizing a Trainium2 kernel written in Bass

```python
import numpy as np
import jax
import jax.numpy as jnp

def _softmax(x, axis=-1):
    return jax.nn.softmax(x, axis=axis)

def _gelu(x):
    return jax.nn.gelu(x, approximate=True)

def _silu(x):
    return jax.nn.silu(x)

def _sigmoid(x):
    return jax.nn.sigmoid(x)

def _layernorm(x, axis=-1, eps=1e-05):
    m = jnp.mean(x, axis=axis, keepdims=True)
    v = jnp.var(x, axis=axis, keepdims=True)
    return (x - m) / jnp.sqrt(v + eps)

def _scatter_add(tgt, idx, src, axis=0):
    return tgt.at[idx].add(src)

def _segment_sum(src, seg, n):
    return jax.ops.segment_sum(src, seg, n)
kernel_name = 'mk_gnn_preln_d1_gnn_r64_4ef14d'

def setup_inputs(seed: int=0):
    np.random.seed(seed)
    _w = jnp.asarray

    def _rec_inputs():
        import jax
        import jax.numpy as jnp
        _gk = jax.random.key(seed)
        x = -0.000202 + 1 * jax.random.normal(jax.random.fold_in(_gk, 1), (100000, 64), jnp.float32)
        src = jax.random.randint(jax.random.fold_in(_gk, 2), (50000,), 0, 100000, jnp.int32)
        dst = jax.random.randint(jax.random.fold_in(_gk, 3), (50000,), 0, 100000, jnp.int32)
        _o = jnp.argsort(dst, stable=True)
        src = src[_o]
        dst = dst[_o]
        edge_attr_32 = 0.000189758 + 1.00013 * jax.random.normal(jax.random.fold_in(_gk, 11), (50000, 32), jnp.float32)
        return (x, src, dst, edge_attr_32)
    x, src, dst, edge_attr_32 = _rec_inputs()

    def _L0_gnn_setup():
        import jax, jax.numpy as jnp
        import numpy as np
        N_NODES = 100000
        N_EDGES = 25000
        D_IN = 64
        D_LAT = 64
        D_EDGE = 32
        N_ACT = 64
        NEG_SLOPE = 0.2

        def _leaky(x):
            return jnp.where(x > 0, x, NEG_SLOPE * x)

        def _gatv2(x, src, dst, eattr, W, b, We, att, bias, n_nodes):
            xl = x @ W + b
            m = _leaky(xl[src] + xl[dst] + eattr @ We)
            logits = m @ att
            mx = jax.ops.segment_max(logits, dst, num_segments=n_nodes)
            e = jnp.exp(logits - mx[dst])
            denom = jax.ops.segment_sum(e, dst, num_segments=n_nodes)
            alpha = e / denom[dst]
            out = jax.ops.segment_sum(xl[src] * alpha[:, None], dst, num_segments=n_nodes)
            return out + bias
        key = jax.random.key(seed)
        ks = jax.random.split(key, 13)
        s = 0.05
        x = jax.random.normal(ks[0], (N_NODES, D_IN), dtype=jnp.float32)
        edge_index = jax.random.randint(ks[1], (2, N_EDGES), 0, N_NODES, dtype=jnp.int32)
        edge_attr = jax.random.normal(ks[2], (N_EDGES, D_EDGE), dtype=jnp.float32)
        return {'x': x, 'edge_index': edge_index, 'edge_attr': edge_attr, 'W1': jax.random.normal(ks[3], (D_IN, D_LAT), dtype=jnp.float32) * s, 'b1': jax.random.normal(ks[4], (D_LAT,), dtype=jnp.float32) * s, 'We1': jax.random.normal(ks[5], (D_EDGE, D_LAT), dtype=jnp.float32) * s, 'att1': jax.random.normal(ks[6], (D_LAT,), dtype=jnp.float32) * s, 'bias1': jax.random.normal(ks[7], (D_LAT,), dtype=jnp.float32) * s, 'W2': jax.random.normal(ks[8], (D_LAT, N_ACT), dtype=jnp.float32) * s, 'b2': jax.random.normal(ks[9], (N_ACT,), dtype=jnp.float32) * s, 'We2': jax.random.normal(ks[10], (D_EDGE, N_ACT), dtype=jnp.float32) * s, 'att2': jax.random.normal(ks[11], (N_ACT,), dtype=jnp.float32) * s, 'bias2': jax.random.normal(ks[12], (N_ACT,), dtype=jnp.float32) * s}
    _L0_gnn_all = _L0_gnn_setup()
    _L0_gnn_in = {k: v for k, v in _L0_gnn_all.items() if k in ('W1', 'b1', 'We1', 'att1', 'bias1', 'W2', 'b2', 'We2', 'att2', 'bias2')}
    del _L0_gnn_all
    return {'x': x, 'src': src, 'dst': dst, 'edge_attr_32': edge_attr_32, 'L0_gnn_W1': _L0_gnn_in['W1'], 'L0_gnn_b1': _L0_gnn_in['b1'], 'L0_gnn_We1': _L0_gnn_in['We1'], 'L0_gnn_att1': _L0_gnn_in['att1'], 'L0_gnn_bias1': _L0_gnn_in['bias1'], 'L0_gnn_W2': _L0_gnn_in['W2'], 'L0_gnn_b2': _L0_gnn_in['b2'], 'L0_gnn_We2': _L0_gnn_in['We2'], 'L0_gnn_att2': _L0_gnn_in['att2'], 'L0_gnn_bias2': _L0_gnn_in['bias2']}

def reference(x, src, dst, edge_attr_32, L0_gnn_W1, L0_gnn_b1, L0_gnn_We1, L0_gnn_att1, L0_gnn_bias1, L0_gnn_W2, L0_gnn_b2, L0_gnn_We2, L0_gnn_att2, L0_gnn_bias2):
    import jax
    import jax.numpy as jnp

    def _L0_gnn_ref(x, edge_index, edge_attr, W1, b1, We1, att1, bias1, W2, b2, We2, att2, bias2):
        import jax, jax.numpy as jnp
        import numpy as np
        N_NODES = 100000
        N_EDGES = 25000
        D_IN = 64
        D_LAT = 64
        D_EDGE = 32
        N_ACT = 64
        NEG_SLOPE = 0.2

        def _leaky(x):
            return jnp.where(x > 0, x, NEG_SLOPE * x)

        def _gatv2(x, src, dst, eattr, W, b, We, att, bias, n_nodes):
            xl = x @ W + b
            m = _leaky(xl[src] + xl[dst] + eattr @ We)
            logits = m @ att
            mx = jax.ops.segment_max(logits, dst, num_segments=n_nodes)
            e = jnp.exp(logits - mx[dst])
            denom = jax.ops.segment_sum(e, dst, num_segments=n_nodes)
            alpha = e / denom[dst]
            out = jax.ops.segment_sum(xl[src] * alpha[:, None], dst, num_segments=n_nodes)
            return out + bias
        n = x.shape[0]
        src, dst = (edge_index[0], edge_index[1])
        deg = jax.ops.segment_sum(jnp.ones_like(dst, dtype=edge_attr.dtype), dst, num_segments=n)
        loop_attr = jax.ops.segment_sum(edge_attr, dst, num_segments=n) / jnp.maximum(deg, 1.0)[:, None]
        ar = jnp.arange(n, dtype=src.dtype)
        src_a = jnp.concatenate([src, ar])
        dst_a = jnp.concatenate([dst, ar])
        ea_a = jnp.concatenate([edge_attr, loop_attr], axis=0)
        h = _gatv2(x, src_a, dst_a, ea_a, W1, b1, We1, att1, bias1, n)
        action_logits = _gatv2(h, src_a, dst_a, ea_a, W2, b2, We2, att2, bias2, n)
        return action_logits
    edge_index = jnp.stack([src, dst])
    h = jnp.maximum(_layernorm(x, axis=-1), 0.0)
    x = x + _L0_gnn_ref(h, edge_index, edge_attr_32, L0_gnn_W1, L0_gnn_b1, L0_gnn_We1, L0_gnn_att1, L0_gnn_bias1, L0_gnn_W2, L0_gnn_b2, L0_gnn_We2, L0_gnn_att2, L0_gnn_bias2)
    return x

_drawn_inputs = setup_inputs


def setup_inputs(seed=0):
    import zlib

    import numpy as np

    out = dict(_drawn_inputs(seed))
    spreads = {}
    factors = {'edge_attr_32': 22.176,
     'L0_gnn_We1': 40.426,
     'L0_gnn_att1': 31.553,
     'L0_gnn_We2': 21.696,
     'L0_gnn_att2': 24.158}
    for name, (base, spread) in spreads.items():
        noise = np.random.default_rng([zlib.crc32(name.encode()), seed]).standard_normal(out[name].shape)
        drawn = base * np.exp(spread * noise) if base else spread * noise
        out[name] = jnp.asarray(drawn.astype(out[name].dtype))
    for name, factor in factors.items():
        out[name] = (out[name] * factor).astype(out[name].dtype)
    return out
```

```python
from contextlib import ExitStack

import concourse.bass as bass
from concourse import mybir

F32 = mybir.dt.float32
I32 = mybir.dt.int32
ALU = mybir.AluOpType
ACT = mybir.ActivationFunctionType
AX_X = mybir.AxisListType.X

P = 128
T = 8
D = 64
DE = 32
W = D + DE
NEG_SLOPE = 0.2
EPS = 1e-5
FAR = -1e30
SKIP = 200000.0
RSQRT_MAGIC = float(0x5F3759DF)
LN_STEPS = 19
SM_STEPS = 7
AG_STEPS = 11
AT_STEPS = 4


def gnn_kernel(nc, x, src, dst, ea, W1, b1, We1, att1, bias1, W2, b2, We2, att2, bias2, out):
    N = x.shape[0]
    E = src.shape[0]
    C = -(-E // (P * T)) * T
    U = C // T
    EP = P * C
    ROWS = E - (P - 1) * C
    DB = P * T
    NDB = -(-N // DB)
    TAILP = (N - (NDB - 1) * DB) // T
    assert 0 < ROWS <= C and NDB == 2 * U and (N - (NDB - 1) * DB) % T == 0 and U % 2 == 1
    F = T * D

    ea_pad = nc.dram_tensor("ea_pad", (EP, DE), F32, kind="Internal").ap()
    z_tab = nc.dram_tensor("z_tab", (N, D), F32, kind="Internal").ap()
    st_all = nc.dram_tensor("st_all", (U * P, W * T), F32, kind="Internal").ap()
    xd_all = nc.dram_tensor("xd_all", (U * P, F), F32, kind="Internal").ap()
    el_all = nc.dram_tensor("el_all", (U * P, F), F32, kind="Internal").ap()
    z_all = nc.dram_tensor("z_all", (U * P * T, D), F32, kind="Internal").ap()
    zd_all = nc.dram_tensor("zd_all", (U * P, F), F32, kind="Internal").ap()
    z_blk = z_all.rearrange("(u p t) d -> (u p) (t d)", p=P, t=T)
    ea_cols = ea_pad.rearrange("(p c) f -> p (c f)", p=P)

    with ExitStack() as ctx:
        def sb(name, shape, dt=F32):
            return ctx.enter_context(nc.sbuf_tensor(name, shape, dt))

        def ps(name, shape):
            return ctx.enter_context(nc.psum_tensor(name, shape, F32))

        def sem(name):
            return ctx.enter_context(nc.semaphore(name))

        src_i = sb("src_i", [P, C], I32)
        dst_i = sb("dst_i", [P, C], I32)
        gat_i = sb("gat_i", [P, U, 2, T], I32)
        sca_i = sb("sca_i", [P, C], I32)
        dext = sb("dext", [P, C + 2])
        edge_i = sb("edge_i", [P, 2], I32)
        same = sb("same", [P, C + 1])
        lastm = sb("lastm", [P, C])
        notlast = sb("notlast", [P, C])
        far = sb("far", [P, C])
        rcnt = sb("rcnt", [P, C])
        cnt = sb("cnt", [P, C])
        hend = sb("hend", [P, C])
        eq0 = sb("eq0", [P, C])
        tmpc = sb("tmpc", [P, C])
        tmpd = sb("tmpd", [P, C])
        iota_c = sb("iota_c", [P, C])
        iota_p = sb("iota_p", [P, 1])
        m_all = sb("m_all", [P, C + 1])
        den_all = sb("den_all", [P, C + 1])
        gidx = sb("gidx", [P, 2, 2 * T], I32)
        sidx = sb("sidx", [P, 2, T], I32)

        ident = sb("ident", [P, P])
        ident2 = sb("ident2", [P, P])
        w1d = sb("w1d", [P, P])
        w1d2 = sb("w1d2", [P, P])
        w1t = sb("w1t", [P, P])
        w2d = sb("w2d", [P, P])
        w12 = sb("w12", [P, P])
        we = sb("we", [P, 2, 2, P])
        attp = sb("attp", [P, 2, 2])
        attr = sb("attr", [P, 2, 2, 2])
        vecs = sb("vecs", [P, 4])
        vsum = sb("vsum", [P, 1])
        vrep = sb("vrep", [P, P])
        zb = sb("zb", [P, 2])
        rows = sb("rows", [P, 2, D])
        cb = sb("cb", [P, D])
        ones = sb("ones", [P, P])

        X = sb("X", [P, 2, 4 * T, D])
        XC = sb("XC", [P, 2, 2 * T, D])
        H = sb("H", [P, 2, 2 * T, D])
        HD = sb("HD", [P, 2, 2 * T, D])
        EA = sb("EA", [P, 2, T, DE])
        LA = sb("LA", [P, 2, T, DE])
        ST = sb("ST", [P, 2, W, T])
        H1 = sb("H1", [P, 2, T, D])
        ZE = sb("ZE", [P, 2, F])
        TD = sb("TD", [P, 2, 2, F])
        OD = sb("OD", [P, 2, 2 * T, D])
        EL = sb("EL", [P, 2, F])
        DX = sb("DX", [P, 2, 4 * T])
        EX = sb("EX", [P, 2, 4 * T])
        stats = sb("stats", [P, 4 * T, 6])
        lnb = sb("lnb", [P, 8, 4 * T])
        rstd = sb("rstd", [P, 2, 4 * T])
        nmr = sb("nmr", [P, 2, 2 * T])
        htd = sb("htd", [P, 2, F])
        hts = sb("hts", [P, 2, F])
        mz = sb("mz", [P, 4, F])
        V = sb("V", [P, W, T])
        RM = sb("RM", [P, W, T])
        h1t = sb("h1t", [P, F])
        tmpf = sb("tmpf", [P, 2, T, D])
        fin = sb("fin", [P, 4, T])

        pT = [ps(f"pT{i}", [P, F]) for i in range(2)]
        pM = ps("pM", [P, F])
        pS = ps("pS", [P, F])
        pY = ps("pY", [P, 2, F])
        pZ = ps("pZ", [P, F])
        pL = ps("pL", [P, F])

        HB = sb("HB", [P, W * T])
        HS = sb("HS", [P, W + 2])
        TS = sb("TS", [P, W + 2])
        sm = sb("sm", [P, 24])
        smi = sb("smi", [P, 6], I32)
        mask8 = sb("mask8", [P, T])
        xh = sb("xh", [P, D])
        hh = sb("hh", [P, D])
        zh = sb("zh", [P, D])
        row = sb("row", [1, 12, P + 1])
        sel = sb("sel", [1, 2, P])
        OT = sb("OT", [P, P + 1])
        QT = sb("QT", [P, P])
        CS = sb("CS", [P, P])
        loopm = sb("loopm", [P, DE])
        hht = sb("hht", [P, P])
        lpt = sb("lpt", [DE, P])
        srz = sb("srz", [D, 2, P])
        fixv = sb("fixv", [P, 2, D])
        fixt = sb("fixt", [D, P])
        zfix = sb("zfix", [P, D])
        tailc = sb("tailc", [P, D])

        ZS = sb("ZS", [P, 2, T, D])
        ZD = sb("ZD", [P, 2, T, D])
        XR = sb("XR", [P, 2, T, D])
        XRC = sb("XRC", [P, 2, T, D])
        OE = sb("OE", [P, 2, T, D])
        ZL = sb("ZL", [P, 2, T, D])
        ZB = sb("ZB", [P, 2, T, D])

        names = {}

        class Sems:

            def __getitem__(self, name):
                if name not in names:
                    names[name] = sem(name)
                return names[name]

        s = Sems()

        def turns(eng, first, peeled, end, body):
            for t in range(first, first + peeled):
                body(t, t % 2)
            t0 = first + peeled
            pairs = (end - t0) // 2
            with eng.Fori(0, pairs) as i:
                body(i * 2 + t0, t0 % 2)
                body(i * 2 + (t0 + 1), (t0 + 1) % 2)
            for t in range(t0 + 2 * pairs, end):
                body(t, t % 2)

        def known(k, n):
            return not isinstance(k, int) or k >= n

        def gathered(k, r):
            return (k - r) // 2 * (32 * T) + 32 * T if isinstance(k, int) else (k - r) * (16 * T) + 32 * T

        def scattered(k, r):
            return (k - r) // 2 * (16 * T) + 16 * T if isinstance(k, int) else (k - r) * (8 * T) + 16 * T

        def dma_uses(k, r, n=16):
            return (k - r) // 2 * n + n if isinstance(k, int) else (k - r) * (n // 2) + n

        def wait(eng, signal, value, went_on):
            eng.wait_ge(signal, value)
            if not isinstance(value, int):
                eng.sem_inc(went_on, 1)

        block = ctx.enter_context(nc.Block())

        @block.sync
        def _(sp):
            wait(sp, s["pads_set"], 1, s["sp_went_on"])
            full = (P - 1) * C
            sp.dma_start(src_i[0:P - 1, :], src[0:full].rearrange("(p c) -> p c", c=C)).then_inc(s["idx_in"], 16)
            sp.dma_start(src_i[P - 1:P, 0:ROWS], src[full:E].rearrange("(p c) -> p c", p=1)).then_inc(s["idx_in"], 16)
            sp.dma_start(dst_i[0:P - 1, :], dst[0:full].rearrange("(p c) -> p c", c=C)).then_inc(s["idx_in"], 16)
            sp.dma_start(dst_i[P - 1:P, 0:ROWS], dst[full:E].rearrange("(p c) -> p c", p=1)).then_inc(s["idx_in"], 16)
            sp.dma_start(edge_i[1:P, 0:1], dst[0:full].rearrange("(p c) -> p c", c=C)[:, C - 1:C],
                         allow_slow_non_contiguous=True).then_inc(s["idx_in"], 16)
            sp.dma_start(edge_i[0:P - 2, 1:2], dst[C:full].rearrange("(p c) -> p c", c=C)[:, 0:1],
                         allow_slow_non_contiguous=True).then_inc(s["idx_in"], 16)
            sp.dma_start(edge_i[P - 2:P - 1, 1:2], dst[full:full + 1].rearrange("(p c) -> p c", p=1)).then_inc(s["idx_in"], 16)

            sp.dma_start(ea_pad[0:E, :].rearrange("(a b) f -> a (b f)", a=16),
                         ea.rearrange("(a b) f -> a (b f)", a=16)).then_inc(s["ea_padded"], 16)
            padr = EP - E
            sp.dma_start(ea_pad[E:EP, :].rearrange("(a b) f -> a (b f)", a=16),
                         ZB[0:16, 0, :, :].rearrange("p t d -> p (t d)")[:, 0:padr // 16 * DE]).then_inc(s["ea_padded"], 16)

            for g in range(2):
                q = slice(g * D, (g + 1) * D)
                sp.dma_start(w1d[q, q], W1).then_inc(s["weights_in"], 16)
                sp.dma_start(w2d[q, q], W2).then_inc(s["weights_in"], 16)
                for l, (we_l, att_l) in enumerate(((We1, att1), (We2, att2))):
                    sp.dma_start(attp[q, l, g:g + 1], att_l.rearrange("(p c) -> p c", c=1)).then_inc(s["weights_in"], 16)
                    for v in range(2):
                        q2 = slice(v * D + g * DE, v * D + (g + 1) * DE)
                        sp.dma_start(we[q2, l, v, q], we_l).then_inc(s["weights_in"], 16)
                for c, v in enumerate((b1, bias1, b2)):
                    sp.dma_start(vecs[q, c:c + 1], v.rearrange("(p c) -> p c", c=1)).then_inc(s["weights_in"], 16)
            for c, v in enumerate((b2, bias2)):
                sp.dma_start(rows[:, c, :], v.rearrange("(p c) -> p c", p=1).to_broadcast([P, D])).then_inc(s["weights_in"], 16)

            def load_unit(k, r):
                if known(k, 2):
                    wait(sp, s["stats_read"], k - 1, s["sp_went_on"])
                    wait(sp, s["dense_normed"], k - 1, s["sp_went_on"])
                    wait(sp, s["xc_ready"], k - 1, s["sp_went_on"])
                n0 = k * (2 * DB)
                if isinstance(k, int) and k == U - 1:
                    sp.dma_start(X[:, r, 2 * T:3 * T, :], x[n0:n0 + DB, :].rearrange("(p t) d -> p t d", p=P)
                                 ).then_inc(s[f"dense_in{r}"], 16)
                    sp.dma_start(X[0:TAILP, r, 3 * T:4 * T, :], x[n0 + DB:N, :].rearrange("(p t) d -> p t d", p=TAILP)
                                 ).then_inc(s[f"dense_in{r}"], 16)
                else:
                    for b in range(2):
                        sp.dma_start(X[:, r, (2 + b) * T:(3 + b) * T, :],
                                     x[bass.ds(n0 + b * DB, DB), :].rearrange("(p t) d -> p t d", p=P)
                                     ).then_inc(s[f"dense_in{r}"], 16)
                if not known(k, 2):
                    wait(sp, s["ea_padded"], 32, s["sp_went_on"])
                else:
                    wait(sp, s["ea_turned"], k - 1, s["sp_went_on"])
                    wait(sp, s["attr_step"], (k - 1) * AT_STEPS, s["sp_went_on"])
                sp.dma_start(EA[:, r, :, :].rearrange("p t f -> p (t f)"),
                             ea_cols[:, bass.ds(k * (T * DE), T * DE)]).then_inc(s[f"ea_in{r}"], 16)

            def turn(k, r):
                if not isinstance(k, int) or k + 1 < U:
                    load_unit(k + 1, 1 - r)
                if not isinstance(k, int) or k < U:
                    wait(sp, s[f"gathered{r}"], gathered(k, r), s["sp_went_on"])
                    sp.dma_start(xd_all[bass.ds(k * P, P), :],
                                 X[:, r, T:2 * T, :].rearrange("p t d -> p (t d)")).then_inc(s[f"xd_saved{r}"], 16)
                    wait(sp, s["el_ready"], k + 1, s["sp_went_on"])
                    sp.dma_start(el_all[bass.ds(k * P, P), :], EL[:, r, :]).then_inc(s[f"el_saved{r}"], 16)
                    wait(sp, s["z_dense_ready"], k + 1, s["sp_went_on"])
                    n0 = k * (2 * DB)
                    for b in range(2):
                        if isinstance(k, int) and k == U - 1 and b == 1:
                            sp.dma_start(z_tab[n0 + DB:N, :].rearrange("(p t) d -> p (t d)", p=TAILP),
                                         TD[0:TAILP, r, b, :]).then_inc(s[f"z_dense_saved{r}"], 16)
                        else:
                            sp.dma_start(z_tab[bass.ds(n0 + b * DB, DB), :].rearrange("(p t) d -> p (t d)", p=P),
                                         TD[:, r, b, :]).then_inc(s[f"z_dense_saved{r}"], 16)
                if known(k, 1):
                    q = 1 - r
                    j = k - 1
                    wait(sp, s["out_dense_done"], k, s["sp_went_on"])
                    n0 = j * (2 * DB)
                    for b in range(2):
                        if isinstance(k, int) and j == U - 1 and b == 1:
                            sp.dma_start(out[n0 + DB:N, :].rearrange("(p t) d -> p t d", p=TAILP),
                                         OD[0:TAILP, q, T:2 * T, :]).then_inc(s[f"out_dense_saved{q}"], 16)
                        else:
                            sp.dma_start(out[bass.ds(n0 + b * DB, DB), :].rearrange("(p t) d -> p t d", p=P),
                                         OD[:, q, b * T:(b + 1) * T, :]).then_inc(s[f"out_dense_saved{q}"], 16)
                    wait(sp, s["h1_ready"], k, s["sp_went_on"])
                    sp.dma_start(st_all[bass.ds(j * P, P), :],
                                 ST[:, q, :, :].rearrange("p f t -> p (f t)")).then_inc(s[f"state_saved{q}"], 16)
                    wait(sp, s["z_edge_ready"], k, s["sp_went_on"])
                    sp.dma_start(z_blk[bass.ds(j * P, P), :], ZE[:, q, :]).then_inc(s[f"z_edge_saved{q}"], 16)

            load_unit(0, 0)
            turns(sp, 0, 3, U - 1, turn)
            turn(U - 1, 0)
            turn(U, 1)

            wait(sp, s["z_patched"], 16, s["sp_went_on"])

            def turn2(k, r):
                u = (U - 1) - k
                if known(k, 2):
                    wait(sp, s[f"z_scattered{r}"], scattered(k - 2, r), s["sp_went_on"])
                    wait(sp, s["zd_ready"], k - 1, s["sp_went_on"])
                sp.dma_start(ZL[:, r, :, :].rearrange("p t d -> p (t d)"),
                             z_blk[bass.ds(u * P, P), :]).then_inc(s[f"z_back{r}"], 16)
                if known(k, 1):
                    store_zd(k - 1, 1 - r)

            def store_zd(k, r):
                u = (U - 1) - k
                wait(sp, s["zd_ready"], k + 1, s["sp_went_on"])
                sp.dma_start(zd_all[bass.ds(u * P, P), :],
                             ZB[:, r, :, :].rearrange("p t d -> p (t d)")).then_inc(s[f"zd_saved{r}"], 16)

            turns(sp, 0, 3, U, turn2)
            store_zd(U - 1, 0)

            for r in range(2):
                wait(sp, s[f"zd_saved{r}"], 16 * ((U + 1 - r) // 2), s["sp_went_on"])
                wait(sp, s[f"xd_saved{r}"], 16 * ((U + 1 - r) // 2), s["sp_went_on"])
                wait(sp, s[f"el_saved{r}"], 16 * ((U + 1 - r) // 2), s["sp_went_on"])

            def turn3(k, r):
                if known(k, 2):
                    wait(sp, s["agg2_done"], k - 1, s["sp_went_on"])
                    wait(sp, s["rows2_done"], k - 1, s["sp_went_on"])
                sp.dma_start(ZD[:, r, :, :].rearrange("p t d -> p (t d)"),
                             zd_all[bass.ds(k * P, P), :]).then_inc(s[f"dst2_in{r}"], 16)
                sp.dma_start(XR[:, r, :, :].rearrange("p t d -> p (t d)"),
                             xd_all[bass.ds(k * P, P), :]).then_inc(s[f"dst2_in{r}"], 16)
                sp.dma_start(EL[:, r, :], el_all[bass.ds(k * P, P), :]).then_inc(s[f"dst2_in{r}"], 16)
                if known(k, 1):
                    store_st(k - 1, 1 - r)

            def store_st(k, r):
                wait(sp, s["agg2_done"], k + 1, s["sp_went_on"])
                sp.dma_start(st_all[bass.ds(k * P, P), 0:F],
                             ST[:, r, 0:D, :].rearrange("p f t -> p (f t)")).then_inc(s[f"state2_saved{r}"], 16)

            turns(sp, 0, 3, U, turn3)
            store_st(U - 1, 0)

            for r in range(2):
                wait(sp, s[f"out_dense_saved{r}"], 32 * ((U + 1 - r) // 2), s["sp_went_on"])
                wait(sp, s[f"state2_saved{r}"], 16 * ((U + 1 - r) // 2), s["sp_went_on"])
            wait(sp, s["out_fixed"], 16, s["sp_went_on"])

        @block.gpsimd
        def _(pool):
            pool.memset(ident[:, :], 0.0).then_inc(s["ident_zero"], 1)
            wait(pool, s["ident_zero"], 1, s["pool_went_on"])
            pool.affine_select(out=ident[:, :], in_=ident[:, :], compare_op=ALU.not_equal, fill=1.0, base=0,
                               pattern=[[-1, P]], channel_multiplier=1).then_inc(s["ident_ready"], 1)
            pool.iota(iota_c[:, :], pattern=[[1, C]], base=0, channel_multiplier=0,
                      allow_small_or_imprecise_dtypes=True).then_inc(s["iotas"], 1)
            pool.iota(iota_p[:, :], pattern=[[0, 1]], base=0, channel_multiplier=1,
                      allow_small_or_imprecise_dtypes=True).then_inc(s["iotas"], 1)

            def gather(to, table, index, signal):
                pool.indirect_dma_start(out=to, out_offset=None, in_=table,
                                        in_offset=bass.IndirectOffsetOnAxis(ap=index, axis=0)).then_inc(signal, 16)

            def scatter(table, index, frm, signal, limit):
                pool.indirect_dma_start(out=table, out_offset=bass.IndirectOffsetOnAxis(ap=index, axis=0), in_=frm,
                                        in_offset=None, bounds_check=limit, oob_is_err=False).then_inc(signal, 16)

            def turn(k, r):
                if known(k, 2):
                    wait(pool, s["stats_read"], k - 1, s["pool_went_on"])
                    wait(pool, s["edges_centred"], k - 1, s["pool_went_on"])
                    wait(pool, s[f"xd_saved{r}"], dma_uses(k - 2, r), s["pool_went_on"])
                pool.tensor_copy(gidx[:, r, :], gat_i[:, bass.ds(k, 1), :, :].rearrange("p u s t -> p (u s t)")
                                 ).then_inc(s["gidx_ready"], 1)
                wait(pool, s["gidx_ready"], k + 1, s["pool_went_on"])
                for t in range(2 * T):
                    gather(X[:, r, t, :], x, gidx[:, r, t:t + 1], s[f"gathered{r}"])

            wait(pool, s["gat_i_ready"], 2, s["pool_went_on"])
            turns(pool, 0, 3, U, turn)

            for r in range(2):
                wait(pool, s[f"state_saved{r}"], 16 * ((U + 1 - r) // 2), s["pool_went_on"])
            wait(pool, s["head_idx"], 1, s["pool_went_on"])
            gather(HB[:, :], st_all, smi[:, 0:1], s["head_in"])
            gather(xh[:, :], x, smi[:, 1:2], s["head_in"])
            for r in range(2):
                wait(pool, s[f"z_dense_saved{r}"], 32 * ((U + 1 - r) // 2), s["pool_went_on"])
                wait(pool, s[f"z_edge_saved{r}"], 16 * ((U + 1 - r) // 2), s["pool_went_on"])
            wait(pool, s["zfix_ready"], 1, s["pool_went_on"])
            scatter(z_all, smi[:, 3:4], zfix[:, :], s["z_patched"], U * P * T - 1)
            scatter(z_tab, smi[:, 2:3], zfix[:, :], s["z_fixed"], N - 1)
            wait(pool, s["z_fixed"], 16, s["pool_went_on"])
            gather(tailc[:, :], z_tab, smi[:, 4:5], s["tail_in"])
            gather(zh[:, :], z_tab, smi[:, 1:2], s["zh_in"])

            def turn2(k, r):
                u = (U - 1) - k
                if known(k, 2):
                    wait(pool, s[f"z_scattered{r}"], scattered(k - 2, r), s["pool_went_on"])
                pool.tensor_copy(sidx[:, r, :], sca_i[:, bass.ds(u * T, T)]).then_inc(s["sidx_ready"], 1)
                wait(pool, s["sidx_ready"], k + 1, s["pool_went_on"])
                wait(pool, s[f"z_back{r}"], dma_uses(k, r), s["pool_went_on"])
                for t in range(T):
                    scatter(z_tab, sidx[:, r, t:t + 1], ZL[:, r, t, :], s[f"z_scattered{r}"], N - 1)

            turns(pool, 0, 3, U, turn2)

            for r in range(2):
                wait(pool, s[f"z_scattered{r}"], 16 * T * ((U + 1 - r) // 2), s["pool_went_on"])
                wait(pool, s[f"out_dense_saved{r}"], 32 * ((U + 1 - r) // 2), s["pool_went_on"])
            wait(pool, s["tail_in"], 16, s["pool_went_on"])

            def fetch(k, r):
                if known(k, 2):
                    wait(pool, s["agg2_done"], k - 1, s["pool_went_on"])
                    wait(pool, s["rows2_done"], k - 1, s["pool_went_on"])
                pool.tensor_copy(gidx[:, r, 0:T], gat_i[:, bass.ds(k, 1), 0, :].rearrange("p u t -> p (u t)")
                                 ).then_inc(s["gidx_ready"], 1)
                wait(pool, s["gidx_ready"], k + (U + 1), s["pool_went_on"])
                for t in range(T):
                    gather(ZS[:, r, t, :], z_tab, gidx[:, r, t:t + 1], s[f"src2_in{r}"])

            def put(k, r):
                if known(k, 2):
                    wait(pool, s[f"out_scattered{r}"], scattered(k - 2, r), s["pool_went_on"])
                pool.tensor_copy(sidx[:, r, :], sca_i[:, bass.ds(k * T, T)]).then_inc(s["sidx_ready"], 1)
                wait(pool, s["sidx_ready"], k + (U + 1), s["pool_went_on"])
                wait(pool, s["agg2_done"], k + 1, s["pool_went_on"])
                for t in range(T):
                    scatter(out, sidx[:, r, t:t + 1], OE[:, r, t, :], s[f"out_scattered{r}"], N - 1)

            def turn3(k, r):
                fetch(k, r)
                if known(k, 2):
                    put(k - 2, r)

            turns(pool, 0, 4, U, turn3)
            put(U - 2, (U - 2) % 2)
            put(U - 1, (U - 1) % 2)

            for r in range(2):
                wait(pool, s[f"state2_saved{r}"], 16 * ((U + 1 - r) // 2), s["pool_went_on"])
            gather(HB[:, :], st_all, smi[:, 0:1], s["head_in"])
            wait(pool, s["outfix_ready"], 1, s["pool_went_on"])
            scatter(out, smi[:, 2:3], zfix[:, :], s["out_fixed"], N - 1)
            for r in range(2):
                wait(pool, s[f"out_scattered{r}"], 16 * T * ((U + 1 - r) // 2), s["pool_went_on"])

        def link(eng, name, ins, also=None, n=1):
            links[name] = links.get(name, 0) + 1
            ins.then_inc(s[name], 1)
            eng.wait_ge(s[name], links[name])
            if also is not None:
                eng.sem_inc(also, n)

        links = {}

        def bc(ap, n):
            return ap.unsqueeze(2).to_broadcast([P, ap.shape[1], n])

        def softmax_logits(dve, k, q, n):
            a = bass.ds(k * T, T)
            b = bass.ds(k * T + 1, T)
            m = m_all[:, b]
            L = pL[:, q * 2 * T:q * 2 * T + T]
            Ls = pL[:, q * 2 * T + T:(q + 1) * 2 * T]
            dx = [DX[:, q, i * T:(i + 1) * T] for i in range(4)]
            step = s["soft_step"]
            base = n * SM_STEPS
            dve.wait_ge(s["logits_ready"], n + 1)
            dve.tensor_tensor_scan(m, far[:, a], L, m_all[:, bass.ds(k * T, 1)], ALU.add, ALU.max).then_inc(step, 1)
            dve.wait_ge(step, base + 1)
            dve.tensor_tensor(dx[0], m_all[:, a], far[:, a], ALU.add).then_inc(step, 1)
            dve.tensor_tensor(dx[1], L, m, ALU.subtract).then_inc(step, 1)
            dve.tensor_tensor(fin[:, 3, :], m, Ls, ALU.max).then_inc(step, 1)
            dve.wait_ge(step, base + 4)
            dve.tensor_tensor(dx[0], dx[0], m, ALU.subtract).then_inc(step, 1)
            dve.tensor_tensor(dx[2], m, fin[:, 3, :], ALU.subtract).then_inc(step, 1)
            dve.tensor_tensor(dx[3], Ls, fin[:, 3, :], ALU.subtract).then_inc(step, 1)

        def aggregate(dve, k, q, n, hs, hd, to, first_of_layer, ready, done):
            b = bass.ds(k * T + 1, T)
            ex = [EX[:, q, i * T:(i + 1) * T] for i in range(4)]
            step = s["agg_step"]
            base = n * AG_STEPS
            acc = ST[:, q, 0:D, :]
            prev = ST[:, 1 - q, 0:D, T - 1]
            dve.wait_ge(s["exps_ready"], n + 1)
            dve.tensor_tensor(V[:, 0:D, :].rearrange("p f t -> p t f"), hs, bc(ex[1], D), ALU.mult).then_inc(step, 1)
            dve.tensor_tensor_scan(den_all[:, b], ex[0], ex[1], den_all[:, bass.ds(k * T, 1)],
                                   ALU.mult, ALU.add).then_inc(step, 1)
            dve.wait_ge(step, base + 2)
            dve.scalar_tensor_tensor(out=V[:, 0:D, 0], in0=prev, scalar=EX[:, q, 0:1], in1=V[:, 0:D, 0],
                                     op0=ALU.mult, op1=ALU.add).then_inc(step, 1)
            dve.tensor_tensor(fin[:, 0, :], den_all[:, b], ex[2], ALU.mult).then_inc(step, 1)
            dve.wait_ge(step, base + 4)
            dve.wait_ge(s["decay_ready"], n + 1)
            if known(n, 2):
                ready(n)
            dve.tensor_tensor_scan(acc.rearrange("p f t -> p (f t)"), RM[:, 0:D, :].rearrange("p f t -> p (f t)"),
                                   V[:, 0:D, :].rearrange("p f t -> p (f t)"), 0.0, ALU.mult, ALU.add
                                   ).then_inc(step, 1)
            dve.tensor_tensor(fin[:, 0, :], fin[:, 0, :], ex[3], ALU.add).then_inc(step, 1)
            dve.wait_ge(step, base + 6)
            dve.reciprocal(fin[:, 1, :], fin[:, 0, :]).then_inc(step, 1)
            dve.wait_ge(step, base + 7)
            dve.tensor_tensor(fin[:, 2, :], ex[2], fin[:, 1, :], ALU.mult).then_inc(step, 1)
            dve.tensor_tensor(fin[:, 3, :], ex[3], fin[:, 1, :], ALU.mult).then_inc(step, 1)
            dve.wait_ge(step, base + 9)
            dve.tensor_tensor(tmpf[:, 0, :, :], acc.rearrange("p f t -> p t f"), bc(fin[:, 2, :], D),
                              ALU.mult).then_inc(step, 1)
            dve.tensor_tensor(tmpf[:, 1, :, :], hd, bc(fin[:, 3, :], D), ALU.mult).then_inc(step, 1)
            dve.wait_ge(step, base + 11)
            done()

        @block.vector
        def _(dve):
            link(dve, "setup", dve.memset(src_i[:, :], 0))
            link(dve, "setup", dve.memset(dst_i[:, :], N))
            link(dve, "setup", dve.memset(edge_i[:, :], -1))
            link(dve, "setup", dve.memset(ZB[:, :, :, :], 0.0))
            link(dve, "setup", dve.memset(w1d[:, :], 0.0))
            link(dve, "setup", dve.memset(w2d[:, :], 0.0))
            link(dve, "setup", dve.memset(attp[:, :, :], 0.0))
            link(dve, "setup", dve.memset(we[:, :, :, :], 0.0), s["pads_set"], 1)
            link(dve, "setup", dve.memset(ones[:, :], 1.0))
            link(dve, "setup", dve.memset(ST[:, :, :, :], 0.0))
            link(dve, "setup", dve.memset(RM[:, :, :], 0.0))
            link(dve, "setup", dve.memset(m_all[:, 0:1], FAR))
            link(dve, "setup", dve.memset(den_all[:, 0:1], 0.0))
            link(dve, "setup", dve.memset(same[:, C:C + 1], 0.0))
            link(dve, "setup", dve.memset(sel[:, 0, :], 1.0))
            link(dve, "setup", dve.memset(sel[:, 1, :], 0.0))
            link(dve, "setup", dve.memset(row[:, :, :], 0.0))
            link(dve, "setup", dve.memset(OT[:, :], 0.0))
            link(dve, "setup", dve.memset(sel[:, 0, D:W], 0.0))
            link(dve, "setup", dve.memset(sel[:, 0, W + 1:W + 2], 0.0))
            link(dve, "setup", dve.memset(sel[:, 1, D:W], 1.0))
            link(dve, "setup", dve.memset(sel[:, 1, W + 1:W + 2], 1.0))
            link(dve, "setup", dve.memset(row[:, 1, 0:1], FAR))

            dve.wait_ge(s["idx_in"], 16 * 7)
            link(dve, "setup", dve.tensor_copy(dext[:, 1:C + 1], dst_i[:, :]))
            link(dve, "setup", dve.tensor_copy(dext[:, 0:1], edge_i[:, 0:1]))
            link(dve, "setup", dve.tensor_copy(dext[:, C + 1:C + 2], edge_i[:, 1:2]))
            link(dve, "setup", dve.tensor_copy(gat_i[:, :, 0, :], src_i[:, :].rearrange("p (u t) -> p u t", t=T)))
            link(dve, "setup", dve.tensor_scalar(gat_i[:, :, 1, :], dext[:, 1:C + 1].rearrange("p (u t) -> p u t", t=T),
                              float(N - 1), None, ALU.min), s["gat_i_ready"], 2)
            link(dve, "setup", dve.tensor_tensor(same[:, 0:C], dext[:, 1:C + 1], dext[:, 0:C], ALU.is_equal))
            link(dve, "setup", dve.tensor_tensor(notlast[:, :], dext[:, 1:C + 1], dext[:, 2:C + 2], ALU.is_equal))
            link(dve, "setup", dve.tensor_scalar(eq0[:, :], dext[:, 1:C + 1], dext[:, 1:2], None, ALU.is_equal))
            link(dve, "setup", dve.tensor_copy(sm[:, 0:1], same[:, 0:1]))
            link(dve, "setup", dve.tensor_copy(sm[:, 1:2], eq0[:, C - 1:C]))
            link(dve, "setup", dve.tensor_scalar(lastm[:, :], notlast[:, :], -1.0, 1.0, ALU.mult, ALU.add))
            link(dve, "setup", dve.memset(same[:, 0:1], 0.0))
            link(dve, "setup", dve.tensor_scalar(far[:, :], same[:, 0:C], 1.0, -FAR, ALU.subtract, ALU.mult))
            link(dve, "setup", dve.tensor_scalar(tmpc[:, :], same[:, 1:C + 1], -1.0, 1.0, ALU.mult, ALU.add))
            link(dve, "setup", dve.tensor_scalar(tmpd[:, :], eq0[:, :], sm[:, 0:1], None, ALU.mult))
            link(dve, "setup", dve.tensor_tensor_scan(cnt[:, :], same[:, 0:C], ones[:, 0:1].to_broadcast([P, C]), 0.0,
                                                      ALU.mult, ALU.add))
            link(dve, "setup", dve.reciprocal(rcnt[:, :], cnt[:, :]))
            link(dve, "setup", dve.tensor_scalar(tmpd[:, :], tmpd[:, :], -1.0, 1.0, ALU.mult, ALU.add))
            link(dve, "setup", dve.tensor_tensor(hend[:, :], eq0[:, :], tmpc[:, :], ALU.mult))
            link(dve, "setup", dve.tensor_tensor(tmpd[:, :], tmpd[:, :], lastm[:, :], ALU.mult))
            link(dve, "setup", dve.scalar_tensor_tensor(out=tmpd[:, :], in0=dext[:, 1:C + 1], scalar=SKIP,
                                                        in1=tmpd[:, :], op0=ALU.subtract, op1=ALU.mult))
            link(dve, "setup", dve.tensor_scalar(sca_i[:, :], tmpd[:, :], SKIP, None, ALU.add))
            dve.wait_ge(s["iotas"], 2)
            link(dve, "setup", dve.tensor_tensor(tmpc[:, :], hend[:, :], iota_c[:, :], ALU.mult))
            link(dve, "setup", dve.tensor_reduce(sm[:, 2:3], tmpc[:, :], AX_X, ALU.add))
            link(dve, "setup", dve.tensor_tensor(tmpc[:, :], hend[:, :], lastm[:, :], ALU.mult))
            link(dve, "setup", dve.tensor_reduce(sm[:, 3:4], tmpc[:, :], AX_X, ALU.add))
            link(dve, "setup", dve.tensor_copy(smi[:, 5:6], sm[:, 2:3]))
            link(dve, "setup", dve.tensor_scalar(smi[:, 0:1], smi[:, 5:6], 3, None, ALU.logical_shift_right))
            link(dve, "setup", dve.tensor_copy(sm[:, 4:5], smi[:, 0:1]))
            link(dve, "setup", dve.scalar_tensor_tensor(out=sm[:, 5:6], in0=sm[:, 4:5], scalar=-float(T),
                                                        in1=sm[:, 2:3], op0=ALU.mult, op1=ALU.add))
            link(dve, "setup", dve.tensor_scalar(mask8[:, :], iota_c[:, 0:T], sm[:, 5:6], None, ALU.is_equal))
            link(dve, "setup", dve.scalar_tensor_tensor(out=sm[:, 6:7], in0=sm[:, 4:5], scalar=float(P),
                                                        in1=iota_p[:, :], op0=ALU.mult, op1=ALU.add))
            link(dve, "setup", dve.tensor_copy(smi[:, 0:1], sm[:, 6:7]))
            link(dve, "setup", dve.scalar_tensor_tensor(out=sm[:, 7:8], in0=sm[:, 6:7], scalar=float(T), in1=sm[:, 5:6],
                                     op0=ALU.mult, op1=ALU.add))
            link(dve, "setup", dve.tensor_tensor(sm[:, 8:9], sm[:, 3:4], sm[:, 0:1], ALU.mult))
            link(dve, "setup", dve.scalar_tensor_tensor(out=sm[:, 9:10], in0=dext[:, 1:2], scalar=SKIP,
                                                        in1=sm[:, 8:9], op0=ALU.subtract, op1=ALU.mult))
            link(dve, "setup", dve.tensor_scalar(smi[:, 2:3], sm[:, 9:10], SKIP, None, ALU.add))
            link(dve, "setup", dve.scalar_tensor_tensor(out=sm[:, 9:10], in0=sm[:, 7:8], scalar=SKIP,
                                                        in1=sm[:, 8:9], op0=ALU.subtract, op1=ALU.mult))
            link(dve, "setup", dve.tensor_scalar(smi[:, 3:4], sm[:, 9:10], SKIP, None, ALU.add))
            link(dve, "setup", dve.tensor_scalar(smi[:, 1:2], dext[:, 1:2], float(N - 1), None, ALU.min))
            link(dve, "setup", dve.tensor_scalar(smi[:, 4:5], dext[:, C:C + 1], float(N - 1), None, ALU.min))
            link(dve, "setup", dve.tensor_tensor(sm[:, 10:11], sm[:, 0:1], sm[:, 1:2], ALU.mult))
            link(dve, "setup", dve.tensor_scalar(sm[:, 11:12], sm[:, 10:11], 1.0, -FAR, ALU.subtract, ALU.mult))
            link(dve, "setup", dve.tensor_scalar(sm[:, 12:13], sm[:, 0:1], 1.0, -FAR, ALU.subtract, ALU.mult), s["head_idx"], 1)

            dve.wait_ge(s["weights_in"], 16 * (2 * (2 + 2 + 4 + 3) + 2))
            dve.wait_ge(s["ident_ready"], 1)
            link(dve, "setup", dve.tensor_scalar(w1d2[:, :], w1d[:, :], 2.0, None, ALU.mult))
            link(dve, "setup", dve.tensor_scalar(ident2[:, :], ident[:, :], 2.0, None, ALU.mult))
            for l in range(2):
                link(dve, "setup", dve.tensor_scalar(attr[:, l, 0, :], attp[:, l, :], 1.0 - NEG_SLOPE, None, ALU.mult))
                link(dve, "setup", dve.tensor_scalar(attr[:, l, 1, :], attp[:, l, :], NEG_SLOPE, None, ALU.mult))
            link(dve, "setup", dve.tensor_scalar(zb[:, 0:1], vecs[:, 0:1], 2.0, None, ALU.mult))
            link(dve, "setup", dve.tensor_tensor(cb[:, :], rows[:, 0, :], rows[:, 1, :], ALU.add))
            link(dve, "setup", dve.tensor_tensor(vsum[:, :], vecs[:, 0:1], vecs[:, 1:2], ALU.add))
            link(dve, "setup", dve.tensor_scalar(vrep[:, :], ones[:, :], vsum[:, 0:1], None, ALU.mult), s["weights_made"], 1)
            dve.wait_ge(s["w1_turned"], 1)
            link(dve, "setup", dve.tensor_copy(w1t[:, :], pT[0][:, 0:P]), s["w1t_ready"], 1)
            dve.wait_ge(s["w12_made"], 1)
            link(dve, "setup", dve.tensor_copy(w12[:, :], pT[1][:, 0:P]))
            link(dve, "setup", dve.tensor_scalar(zb[:, 1:2], pM[:, 0:1], vecs[:, 2:3], 2.0, ALU.add, ALU.mult))
            link(dve, "setup", dve.tensor_tensor(cb[:, :], cb[:, :], pS[:, 0:D], ALU.add), s["consts_ready"], 1)
            dve.wait_ge(s["consts_ready"], 1)

            def edges_and_dense(k, r):
                step = s["attr_step"]
                base = k * AT_STEPS
                dve.wait_ge(s[f"ea_in{r}"], dma_uses(k, r))
                Va = V[:, D:W, :]
                dve.tensor_copy(Va.rearrange("p f t -> p t f"), EA[:, r, :, :]).then_inc(step, 1)
                dve.wait_ge(step, base + 1)
                dve.scalar_tensor_tensor(out=V[:, D:W, 0], in0=ST[:, 1 - r, D:W, T - 1],
                                         scalar=same[:, bass.ds(k * T, 1)], in1=V[:, D:W, 0],
                                         op0=ALU.mult, op1=ALU.add).then_inc(step, 1)
                dve.wait_ge(step, base + 2)
                dve.wait_ge(s["mask_spread"], k + 1)
                if known(k, 2):
                    dve.wait_ge(s[f"state_saved{r}"], dma_uses(k - 2, r))
                dve.tensor_tensor_scan(ST[:, r, D:W, :].rearrange("p f t -> p (f t)"),
                                       RM[:, D:W, :].rearrange("p f t -> p (f t)"),
                                       Va.rearrange("p f t -> p (f t)"), 0.0, ALU.mult, ALU.add).then_inc(step, 1)
                dve.wait_ge(step, base + 3)
                if known(k, 2):
                    dve.wait_ge(s["ea_turned"], k - 1)
                dve.tensor_tensor(LA[:, r, :, :], ST[:, r, D:W, :].rearrange("p f t -> p t f"),
                                  bc(rcnt[:, bass.ds(k * T, T)], DE), ALU.mult).then_inc(step, 1)

            def norm_unit(k, r):
                dve.wait_ge(s[f"dense_in{r}"], dma_uses(k, r, 32))
                base = k * LN_STEPS
                step = s["stats_step"]
                for t in range(2 * T, 4 * T):
                    dve.bn_stats(stats[:, t, :], X[:, r, t, :])
                if known(k, 2):
                    dve.wait_ge(s["out_dense_done"], k - 1)
                dve.tensor_tensor(XC[:, r, :, :], X[:, r, 2 * T:4 * T, :],
                                  cb[:, :].unsqueeze(1).to_broadcast([P, 2 * T, D]), ALU.add
                                  ).then_inc(s["xc_ready"], 1)
                dve.wait_ge(s[f"gathered{r}"], gathered(k, r))
                for t in range(2 * T):
                    last = dve.bn_stats(stats[:, t, :], X[:, r, t, :])
                last.then_inc(s["stats_read"], 1)
                dve.wait_ge(s["stats_read"], k + 1)
                me, ve, mo, vo = (stats[:, :, c] for c in (1, 2, 4, 5))
                rs = rstd[:, r, :]
                dve.tensor_tensor(lnb[:, 0, :], me, mo, ALU.add).then_inc(step, 1)
                dve.tensor_tensor(lnb[:, 1, :], me, mo, ALU.subtract).then_inc(step, 1)
                dve.tensor_tensor(lnb[:, 2, :], ve, vo, ALU.add).then_inc(step, 1)
                dve.wait_ge(step, base + 3)
                dve.scalar_tensor_tensor(out=lnb[:, 3, :], in0=lnb[:, 1, :], scalar=0.25, in1=lnb[:, 1, :],
                                         op0=ALU.mult, op1=ALU.mult).then_inc(step, 1)
                dve.tensor_scalar(lnb[:, 4, :], lnb[:, 2, :], 1.0 / D, EPS, ALU.mult, ALU.add).then_inc(step, 1)
                dve.tensor_scalar(lnb[:, 7, :], lnb[:, 0, :], 0.5, None, ALU.mult).then_inc(step, 1)
                dve.wait_ge(step, base + 6)
                dve.tensor_tensor(lnb[:, 5, :], lnb[:, 3, :], lnb[:, 4, :], ALU.add).then_inc(step, 1)
                dve.wait_ge(step, base + 7)
                dve.tensor_scalar(lnb[:, 6, :].bitcast(I32), lnb[:, 5, :].bitcast(I32), 1, None,
                                  ALU.logical_shift_right).then_inc(step, 1)
                dve.wait_ge(step, base + 8)
                dve.tensor_scalar(rs.bitcast(I32), lnb[:, 6, :].bitcast(I32), -1.0, RSQRT_MAGIC,
                                  ALU.mult, ALU.add).then_inc(step, 1)
                n = 9
                for _ in range(3):
                    dve.wait_ge(step, base + n)
                    dve.scalar_tensor_tensor(out=lnb[:, 0, :], in0=rs, scalar=-0.5, in1=rs,
                                             op0=ALU.mult, op1=ALU.mult).then_inc(step, 1)
                    dve.wait_ge(step, base + n + 1)
                    dve.tensor_tensor(lnb[:, 1, :], lnb[:, 0, :], lnb[:, 5, :], ALU.mult).then_inc(step, 1)
                    dve.wait_ge(step, base + n + 2)
                    dve.scalar_tensor_tensor(out=rs, in0=lnb[:, 1, :], scalar=1.5, in1=rs,
                                             op0=ALU.add, op1=ALU.mult).then_inc(step, 1)
                    n += 3
                dve.wait_ge(step, base + n)
                dve.scalar_tensor_tensor(out=nmr[:, r, :], in0=lnb[:, 7, 2 * T:4 * T], scalar=-1.0,
                                         in1=rs[:, 2 * T:4 * T], op0=ALU.mult, op1=ALU.mult).then_inc(step, 1)
                assert n + 1 == LN_STEPS
                if known(k, 2):
                    dve.wait_ge(s["hd_turned"], k - 1)
                dve.tensor_tensor(H[:, r, :, :], X[:, r, 0:2 * T, :], bc(lnb[:, 7, 0:2 * T], D), ALU.subtract
                                  ).then_inc(s["edges_centred"], 1)
                dve.wait_ge(s["edges_centred"], k + 1)
                dve.tensor_tensor(H[:, r, :, :], H[:, r, :, :], bc(rs[:, 0:2 * T], D), ALU.mult
                                  ).then_inc(s["edges_scaled"], 1)
                dve.wait_ge(s["edges_scaled"], k + 1)
                dve.tensor_scalar(H[:, r, :, :], H[:, r, :, :], 0.0, None, ALU.max).then_inc(s["h_ready"], 1)

            def out_dense(k, r):
                dve.wait_ge(s["z_dense_ready"], k + 1)
                if known(k, 2):
                    dve.wait_ge(s[f"out_dense_saved{r}"], dma_uses(k - 2, r, 32))
                dve.tensor_tensor(OD[:, r, :, :].rearrange("p t d -> p (t d)"),
                                  XC[:, r, :, :].rearrange("p t d -> p (t d)"),
                                  TD[:, r, :, :].rearrange("p b f -> p (b f)"), ALU.add).then_inc(s["out_dense_done"], 1)

            def finish1(k, r):
                def done():
                    if known(k, 2):
                        dve.wait_ge(s["h1_turned"], k - 1)
                    dve.tensor_tensor(H1[:, r, :, :], tmpf[:, 0, :, :], tmpf[:, 1, :, :], ALU.add
                                      ).then_inc(s["h1_ready"], 1)

                aggregate(dve, k, r, k, H[:, r, 0:T, :], H[:, r, T:2 * T, :], None, True,
                          lambda n: None, done)

            def turn(k, r):
                if known(k, 1):
                    softmax_logits(dve, k - 1, 1 - r, k - 1)
                    out_dense(k - 1, 1 - r)
                if not isinstance(k, int) or k < U:
                    norm_unit(k, r)
                    edges_and_dense(k, r)
                if known(k, 1):
                    finish1(k - 1, 1 - r)

            turns(dve, 0, 3, U - 1, turn)
            turn(U - 1, 0)
            turn(U, 1)

            def spread_states(layer, rT, width):
                dve.wait_ge(s["head_in"], 32 if layer == 0 else 48)
                hb = HB[:, 0:width * T].rearrange("p (f t) -> p f t", t=T)
                link(dve, "seam", dve.tensor_tensor(V[:, 0:width, :], hb,
                                                    mask8[:, :].unsqueeze(1).to_broadcast([P, width, T]), ALU.mult))
                link(dve, "seam", dve.tensor_reduce(HS[:, 0:width], V[:, 0:width, :], AX_X, ALU.add))
                link(dve, "seam", dve.tensor_copy(TS[:, 0:width], ST[:, rT, 0:width, T - 1]))
                link(dve, "seam", dve.tensor_tensor(tmpc[:, :], hend[:, :], m_all[:, 1:C + 1], ALU.mult))
                link(dve, "seam", dve.tensor_reduce(sm[:, 13:14], tmpc[:, :], AX_X, ALU.add))
                link(dve, "seam", dve.tensor_tensor(tmpd[:, :], hend[:, :], den_all[:, 1:C + 1], ALU.mult))
                link(dve, "seam", dve.tensor_reduce(HS[:, W:W + 1], tmpd[:, :], AX_X, ALU.add))
                link(dve, "seam", dve.tensor_copy(TS[:, W:W + 1], den_all[:, C:C + 1]))
                if layer == 0:
                    link(dve, "seam", dve.tensor_tensor(tmpc[:, :], hend[:, :], cnt[:, :], ALU.mult))
                    link(dve, "seam", dve.tensor_reduce(HS[:, W + 1:W + 2], tmpc[:, :], AX_X, ALU.add))
                    link(dve, "seam", dve.tensor_copy(TS[:, W + 1:W + 2], cnt[:, C - 1:C]))
                link(dve, "seam", dve.tensor_copy(sm[:, 14:15], m_all[:, C:C + 1]))
                dve.sem_inc(s["tails_ready"], 1)

            def seam(layer, rT):
                width = W if layer == 0 else D
                spread_states(layer, rT, width)
                dve.wait_ge(s["rows_turned"], layer + 1)
                link(dve, "seam", dve.tensor_copy(row[:, 2:5, 0:P], pS[0:1, 0:3 * P].rearrange("p (a b) -> p a b", a=3)))
                link(dve, "seam", dve.tensor_tensor_scan(row[:, 1, 1:P + 1], row[:, 3, 0:P], row[:, 2, 0:P], FAR,
                                                         ALU.add, ALU.max))
                link(dve, "seam", dve.tensor_tensor(row[:, 5, 0:P], row[:, 2, 0:P], row[:, 1, 1:P + 1], ALU.subtract))
                link(dve, "seam", dve.tensor_tensor(row[:, 6, 0:P], row[:, 1, 0:P], row[:, 3, 0:P], ALU.add))
                link(dve, "seam", dve.tensor_tensor(row[:, 6, 0:P], row[:, 6, 0:P], row[:, 1, 1:P + 1], ALU.subtract))
                dve.sem_inc(s["row_exps_asked"], 1)
                dve.wait_ge(s["decay_spread"], layer + 1)
                link(dve, "seam", dve.tensor_copy(QT[0:W + 2, :], pM[0:W + 2, 0:P]))
                dve.wait_ge(s["tails_turned"], layer + 1)
                link(dve, "seam", dve.tensor_tensor(QT[0:W + 2, :], QT[0:W + 2, :], pT[0][0:W + 2, 0:P], ALU.mult))
                link(dve, "seam", dve.tensor_tensor_scan(OT[0:W + 2, 1:P + 1], pM[0:W + 2, P:2 * P], QT[0:W + 2, :], 0.0,
                                                         ALU.mult, ALU.add))
                dve.sem_inc(s["carries_made"], 1)
                dve.wait_ge(s["carries_turned"], layer + 1)
                link(dve, "seam", dve.tensor_copy(CS[:, 0:W + 2], pT[1][:, 0:W + 2]))
                link(dve, "seam", dve.tensor_scalar(sm[:, 15:16], pS[:, 3 * P:3 * P + 1], sm[:, 12:13], None, ALU.add))
                link(dve, "seam", dve.tensor_tensor(sm[:, 16:17], sm[:, 15:16], sm[:, 13:14], ALU.max))
                link(dve, "seam", dve.tensor_tensor(sm[:, 17:18], sm[:, 13:14], sm[:, 16:17], ALU.subtract))
                link(dve, "seam", dve.tensor_tensor(sm[:, 18:19], sm[:, 15:16], sm[:, 16:17], ALU.subtract))
                dve.sem_inc(s["seam_exps_asked"], 1)
                dve.wait_ge(s["seam_exps"], 2 * layer + 1)
                for a, b in ((0, D), (W, W + 1)):
                    link(dve, "seam", dve.tensor_scalar(HS[:, a:b], HS[:, a:b], sm[:, 19:20], None, ALU.mult))
                    link(dve, "seam", dve.scalar_tensor_tensor(out=HS[:, a:b], in0=CS[:, a:b], scalar=sm[:, 20:21],
                                                               in1=HS[:, a:b], op0=ALU.mult, op1=ALU.add))
                if layer == 0:
                    for a, b in ((D, W), (W + 1, W + 2)):
                        link(dve, "seam", dve.scalar_tensor_tensor(out=HS[:, a:b], in0=CS[:, a:b], scalar=sm[:, 0:1],
                                                                   in1=HS[:, a:b], op0=ALU.mult, op1=ALU.add))
                    link(dve, "seam", dve.reciprocal(sm[:, 21:22], HS[:, W + 1:W + 2]))
                    link(dve, "seam", dve.tensor_scalar(loopm[:, :], HS[:, D:W], sm[:, 21:22], None, ALU.mult))
                    mean = lnb[:, 0, 0:1]
                    link(dve, "seam", dve.bn_stats(stats[:, 0, :], xh[:, :]))
                    link(dve, "seam", dve.tensor_tensor(lnb[:, 0, 0:1], stats[:, 0, 1:2], stats[:, 0, 4:5], ALU.add))
                    link(dve, "seam", dve.tensor_tensor(lnb[:, 1, 0:1], stats[:, 0, 1:2], stats[:, 0, 4:5], ALU.subtract))
                    link(dve, "seam", dve.tensor_tensor(lnb[:, 2, 0:1], stats[:, 0, 2:3], stats[:, 0, 5:6], ALU.add))
                    link(dve, "seam", dve.scalar_tensor_tensor(out=lnb[:, 3, 0:1], in0=lnb[:, 1, 0:1], scalar=0.25, in1=lnb[:, 1, 0:1],
                                             op0=ALU.mult, op1=ALU.mult))
                    link(dve, "seam", dve.tensor_scalar(lnb[:, 4, 0:1], lnb[:, 2, 0:1], 1.0 / D, EPS, ALU.mult, ALU.add))
                    link(dve, "seam", dve.tensor_scalar(lnb[:, 7, 0:1], mean, 0.5, None, ALU.mult))
                    v = lnb[:, 5, 0:1]
                    y = lnb[:, 6, 0:1]
                    link(dve, "seam", dve.tensor_tensor(v, lnb[:, 3, 0:1], lnb[:, 4, 0:1], ALU.add))
                    link(dve, "seam", dve.tensor_scalar(y.bitcast(I32), v.bitcast(I32), 1, None,
                                                        ALU.logical_shift_right))
                    link(dve, "seam", dve.tensor_scalar(y.bitcast(I32), y.bitcast(I32), -1.0, RSQRT_MAGIC,
                                                        ALU.mult, ALU.add))
                    for _ in range(3):
                        link(dve, "seam", dve.scalar_tensor_tensor(out=lnb[:, 0, 0:1], in0=y, scalar=-0.5, in1=y,
                                                                   op0=ALU.mult, op1=ALU.mult))
                        link(dve, "seam", dve.tensor_tensor(lnb[:, 1, 0:1], lnb[:, 0, 0:1], v, ALU.mult))
                        link(dve, "seam", dve.scalar_tensor_tensor(out=y, in0=lnb[:, 1, 0:1], scalar=1.5, in1=y,
                                                                   op0=ALU.add, op1=ALU.mult))
                    link(dve, "seam", dve.tensor_scalar(hh[:, :], xh[:, :], lnb[:, 7, 0:1], y, ALU.subtract, ALU.mult))
                    link(dve, "seam", dve.tensor_scalar(hh[:, :], hh[:, :], 0.0, None, ALU.max))
                node = hh if layer == 0 else zh
                if layer == 1:
                    dve.wait_ge(s["zh_in"], 16)
                dve.sem_inc(s["node_ready"], 1)
                dve.wait_ge(s["loop_logit"], layer + 1)
                ls = pL[:, 4 * T:4 * T + 1]
                link(dve, "seam", dve.tensor_tensor(sm[:, 15:16], ls, sm[:, 16:17], ALU.max))
                link(dve, "seam", dve.tensor_tensor(sm[:, 17:18], sm[:, 16:17], sm[:, 15:16], ALU.subtract))
                link(dve, "seam", dve.tensor_tensor(sm[:, 18:19], ls, sm[:, 15:16], ALU.subtract))
                dve.sem_inc(s["seam_exps_asked"], 1)
                dve.wait_ge(s["seam_exps"], 2 * layer + 2)
                link(dve, "seam", dve.scalar_tensor_tensor(out=sm[:, 21:22], in0=HS[:, W:W + 1], scalar=sm[:, 19:20],
                                                           in1=sm[:, 20:21], op0=ALU.mult, op1=ALU.add))
                link(dve, "seam", dve.reciprocal(sm[:, 22:23], sm[:, 21:22]))
                link(dve, "seam", dve.tensor_scalar(sm[:, 19:21], sm[:, 19:21], sm[:, 22:23], None, ALU.mult))
                link(dve, "seam", dve.tensor_scalar(fixv[:, 0, :], HS[:, 0:D], sm[:, 19:20], None, ALU.mult))
                link(dve, "seam", dve.scalar_tensor_tensor(out=fixv[:, 1, :], in0=node[:, :], scalar=sm[:, 20:21],
                                                           in1=fixv[:, 0, :], op0=ALU.mult, op1=ALU.add))

            seam(0, 0)
            dve.sem_inc(s["fixv_ready"], 1)
            dve.wait_ge(s["zfix_made"], 1)
            link(dve, "seam", dve.tensor_copy(zfix[:, :], pM[:, 0:D]), s["zfix_ready"], 1)
            link(dve, "seam", dve.memset(m_all[:, 0:1], FAR))

            dve.wait_ge(s["tail_in"], 16)

            def turn2(k, r):
                u = (U - 1) - k
                a = bass.ds(u * T, T)
                base = k * (T + 1)
                wait(dve, s[f"z_back{r}"], dma_uses(k, r), s["dve_went_on"])
                if known(k, 2):
                    wait(dve, s[f"zd_saved{r}"], dma_uses(k - 2, r), s["dve_went_on"])
                dve.tensor_tensor(ZB[:, r, :, :], ZL[:, r, :, :], bc(lastm[:, a], D), ALU.mult
                                  ).then_inc(s["back_step"], 1)
                for n, t in enumerate(reversed(range(T))):
                    prev = ZB[:, r, t + 1, :] if t + 1 < T else (ZB[:, 1 - r, 0, :] if known(k, 1) else tailc[:, :])
                    wait(dve, s["back_step"], base + n + 1, s["dve_went_on"])
                    ins = dve.scalar_tensor_tensor(out=ZB[:, r, t, :], in0=prev,
                                                   scalar=notlast[:, bass.ds(u * T + t, 1)], in1=ZB[:, r, t, :],
                                                   op0=ALU.mult, op1=ALU.add).then_inc(s["back_step"], 1)
                wait(dve, s["back_step"], base + T + 1, s["dve_went_on"])
                dve.sem_inc(s["zd_ready"], 1)

            turns(dve, 0, 3, U, turn2)

            def turn3(k, r):
                n = k + U
                dve.wait_ge(s[f"dst2_in{r}"], dma_uses(k, r, 48))
                dve.tensor_tensor(XRC[:, r, :, :], XR[:, r, :, :], cb[:, :].unsqueeze(1).to_broadcast([P, T, D]),
                                  ALU.add).then_inc(s["xrc_ready"], 1)
                softmax_logits(dve, k, r, n)

                def ready(_):
                    if known(k, 2):
                        dve.wait_ge(s[f"state2_saved{r}"], dma_uses(k - 2, r))

                def done():
                    dve.tensor_tensor(tmpf[:, 0, :, :], tmpf[:, 0, :, :], tmpf[:, 1, :, :], ALU.add
                                      ).then_inc(s["mean2_ready"], 1)
                    dve.wait_ge(s["mean2_ready"], k + 1)
                    if known(k, 2):
                        dve.wait_ge(s[f"out_scattered{r}"], scattered(k - 2, r))
                    dve.tensor_tensor(OE[:, r, :, :], tmpf[:, 0, :, :], XRC[:, r, :, :], ALU.add
                                      ).then_inc(s["agg2_done"], 1)

                aggregate(dve, k, r, n, ZS[:, r, :, :], ZD[:, r, :, :], None, False, ready, done)

            turns(dve, 0, 3, U, turn3)
            seam(1, 0)
            link(dve, "seam", dve.tensor_tensor(zfix[:, :], fixv[:, 1, :], cb[:, :], ALU.add))
            dve.tensor_tensor(zfix[:, :], zfix[:, :], xh[:, :], ALU.add).then_inc(s["outfix_ready"], 1)

        @block.scalar
        def _(act):
            def exps(k, q, n):
                act.wait_ge(s["soft_step"], n * SM_STEPS + SM_STEPS)
                act.activation(EX[:, q, :], DX[:, q, :], ACT.Exp).then_inc(s["exps_ready"], 1)
                act.wait_ge(s["exps_ready"], n + 1)
                if known(n, 1):
                    act.wait_ge(s["agg_step"], (n - 1) * AG_STEPS + 5)
                act.activation(RM[:, 0:D, 1:T], EX[:, q, 1:T].unsqueeze(1).to_broadcast([P, D, T - 1]),
                               ACT.Copy).then_inc(s["decay_ready"], 1)

            def leaky_rows(n, layer, done_m, done_s):
                for i, (ps_i, made) in enumerate(((pM, "rows_m"), (pS, "rows_s"))):
                    act.wait_ge(s[made], n + 1)
                    if known(n, 1):
                        act.wait_ge(s["logits_ready"], n)
                    act.activation(mz[:, 2 * i, :], ps_i[:, :], ACT.Relu, bias=zb[:, layer:layer + 1])
                    act.activation(mz[:, 2 * i + 1, :], ps_i[:, :], ACT.Identity, bias=zb[:, layer:layer + 1]
                                   ).then_inc(s[(done_m, done_s)[i]], 1)

            def unit(k, r):
                if known(k, 1):
                    act.wait_ge(s["attr_step"], (k - 1) * AT_STEPS + 3)
                act.activation(RM[:, D:W, 1:T],
                               same[:, bass.ds(k * T + 1, T - 1)].unsqueeze(1).to_broadcast([P, DE, T - 1]),
                               ACT.Copy).then_inc(s["mask_spread"], 1)
                act.wait_ge(s["stats_step"], k * LN_STEPS + LN_STEPS)
                if known(k, 2):
                    act.wait_ge(s["dense1_turned"], k - 1)
                for t in range(2 * T):
                    last = act.activation(HD[:, r, t, :], X[:, r, 2 * T + t, :], ACT.Relu,
                                          bias=nmr[:, r, t:t + 1], scale=rstd[:, r, 2 * T + t:2 * T + t + 1])
                last.then_inc(s["dense_normed"], 1)
                for b in range(2):
                    act.wait_ge(s[f"dense{b}_turned"], k + 1)
                    if known(k, 1):
                        act.wait_ge(s["z_dense_made"], k)
                    act.activation(htd[:, b, :], pT[b][:, :], ACT.Copy).then_inc(s[f"dense{b}_out"], 1)
                for b, nm in enumerate(("hs", "hd")):
                    act.wait_ge(s[f"{nm}_turned"], k + 1)
                    if known(k, 1):
                        act.wait_ge(s["rows_s"], k)
                    act.activation(hts[:, b, :], pT[b][:, :], ACT.Copy).then_inc(s[f"{nm}_out"], 1)
                act.wait_ge(s["ea_turned"], k + 1)
                if known(k, 2):
                    act.wait_ge(s[f"el_saved{r}"], dma_uses(k - 2, r))
                    act.wait_ge(s["rows_s"], k - 1)
                act.activation(EL[:, r, :], pT[0][:, :], ACT.Copy).then_inc(s["el_ready"], 1)
                leaky_rows(k, 0, "mz_m", "mz_s")
                act.wait_ge(s["z_dense_made"], k + 1)
                if known(k, 2):
                    act.wait_ge(s[f"z_dense_saved{r}"], dma_uses(k - 2, r, 32))
                    act.wait_ge(s["out_dense_done"], k - 1)
                act.activation(TD[:, r, :, :].rearrange("p b f -> p (b f)"), pY[:, :, :].rearrange("p b f -> p (b f)"),
                               ACT.Copy).then_inc(s["z_dense_ready"], 1)

            def edges_out(k, r):
                act.wait_ge(s["h1_turned"], k + 1)
                if known(k, 1):
                    act.wait_ge(s["z_edge_made"], k)
                act.activation(h1t[:, :], pT[1][:, :], ACT.Copy).then_inc(s["h1t_ready"], 1)
                act.wait_ge(s["z_edge_made"], k + 1)
                if known(k, 2):
                    act.wait_ge(s[f"z_edge_saved{r}"], dma_uses(k - 2, r))
                act.activation(ZE[:, r, :], pZ[:, :], ACT.Copy).then_inc(s["z_edge_ready"], 1)

            act.wait_ge(s["consts_ready"], 1)

            def turn(k, r):
                if known(k, 1):
                    exps(k - 1, 1 - r, k - 1)
                if not isinstance(k, int) or k < U:
                    unit(k, r)
                if known(k, 1):
                    edges_out(k - 1, 1 - r)

            turns(act, 0, 3, U - 1, turn)
            turn(U - 1, 0)
            turn(U, 1)

            def seam(layer):
                act.wait_ge(s["row_exps_asked"], layer + 1)
                act.activation(row[:, 7:9, 0:P], row[:, 5:7, 0:P], ACT.Exp).then_inc(s["row_exps"], 1)
                act.wait_ge(s["seam_exps_asked"], 2 * layer + 1)
                act.activation(sm[:, 19:21], sm[:, 17:19], ACT.Exp).then_inc(s["seam_exps"], 1)
                act.wait_ge(s["node_turned"], layer + 1)
                if layer == 0:
                    act.activation(lpt[:, :], pT[0][0:DE, P:2 * P], ACT.Copy)
                act.activation(hht[0:D, :], pT[0][0:D, 0:P], ACT.Copy).then_inc(s["node_out"], 1)
                act.wait_ge(s["loop_rows"], layer + 1)
                act.activation(srz[:, 0, :], pM[0:D, 0:P], ACT.Relu, bias=zb[0:D, layer:layer + 1])
                act.activation(srz[:, 1, :], pM[0:D, 0:P], ACT.Identity, bias=zb[0:D, layer:layer + 1]
                               ).then_inc(s["loop_leaky"], 1)
                act.wait_ge(s["seam_exps_asked"], 2 * layer + 2)
                act.activation(sm[:, 19:21], sm[:, 17:19], ACT.Exp).then_inc(s["seam_exps"], 1)

            seam(0)
            act.wait_ge(s["fix_turned"], 1)
            act.activation(fixt[:, :], pT[0][0:D, 0:P], ACT.Copy).then_inc(s["fixt_ready"], 1)

            def turn3(k, r):
                n = k + U
                leaky_rows(n, 1, "mz_m", "mz_s")
                exps(k, r, n)

            turns(act, 0, 1, U, turn3)
            seam(1)

        @block.tensor
        def _(pe):
            def turned(to, tile, signal):
                for j in range(F // P):
                    last = pe.transpose(to[:, j * P:(j + 1) * P], tile[:, j * P:(j + 1) * P], ident[:, :])
                last.then_inc(signal, 1)

            def flat(ap):
                return ap.rearrange("p t d -> p (t d)")

            def logits(n, q, layer):
                for i, ready in enumerate(("mz_m", "mz_s")):
                    pe.wait_ge(s[ready], n + 1)
                    if i == 0 and known(n, 1):
                        pe.wait_ge(s["soft_step"], (n - 1) * SM_STEPS + SM_STEPS)
                    for j in range(T // 2):
                        c = q * 2 * T + i * T + 2 * j
                        for h in range(2):
                            last = pe.matmul(pL[:, c:c + 2], mz[:, 2 * i + h, j * P:(j + 1) * P], attr[:, layer, h, :],
                                             start=(h == 0), stop=(h == 1))
                last.then_inc(s["logits_ready"], 1)

            pe.wait_ge(s["weights_made"], 1)
            pe.transpose(pT[0][:, 0:P], w1d[:, :], ident[:, :]).then_inc(s["w1_turned"], 1)
            pe.wait_ge(s["w1t_ready"], 1)
            pe.matmul(pM[:, 0:1], w2d[:, :], vsum[:, :], start=True, stop=True)
            pe.matmul(pS[:, 0:D], vrep[0:D, :], w2d[0:D, 0:D], start=True, stop=True)
            pe.matmul(pT[1][:, 0:P], w1t[:, :], w2d[:, :], start=True, stop=True).then_inc(s["w12_made"], 1)
            pe.wait_ge(s["consts_ready"], 1)

            def unit(k, r):
                pe.wait_ge(s["dense_normed"], k + 1)
                if known(k, 1):
                    pe.wait_ge(s["el_ready"], k)
                turned(pT[0], flat(HD[:, r, 0:T, :]), s["dense0_turned"])
                if known(k, 2):
                    pe.wait_ge(s["h1t_ready"], k - 1)
                turned(pT[1], flat(HD[:, r, T:2 * T, :]), s["dense1_turned"])
                pe.wait_ge(s["h_ready"], k + 1)
                pe.wait_ge(s["dense0_out"], k + 1)
                turned(pT[0], flat(H[:, r, 0:T, :]), s["hs_turned"])
                pe.wait_ge(s["dense1_out"], k + 1)
                turned(pT[1], flat(H[:, r, T:2 * T, :]), s["hd_turned"])
                pe.wait_ge(s["attr_step"], k * AT_STEPS + AT_STEPS)
                pe.wait_ge(s["hs_out"], k + 1)
                for i, tile in enumerate((EA, LA)):
                    tile = flat(tile[:, r, :, :])
                    for j in range(2):
                        last = pe.transpose(pT[0][:, (2 * i + j) * P:(2 * i + j + 1) * P],
                                            tile[:, j * P:(j + 1) * P], ident[:, :])
                last.then_inc(s["ea_turned"], 1)
                pe.wait_ge(s["hd_out"], k + 1)
                pe.wait_ge(s["el_ready"], k + 1)
                if known(k, 1):
                    pe.wait_ge(s["mz_m"], k)
                pe.matmul(pM[:, :], w1d[:, :], hts[:, 0, :], start=True, stop=False)
                pe.matmul(pM[:, :], w1d[:, :], hts[:, 1, :], start=False, stop=True)
                for j in range(T // 2):
                    last = pe.matmul(pM[:, j * P:(j + 1) * P], we[:, 0, j % 2, :],
                                     EL[:, r, j // 2 * P:(j // 2 + 1) * P], start=False, stop=True,
                                     skip_group_check=True)
                last.then_inc(s["rows_m"], 1)
                if known(k, 1):
                    pe.wait_ge(s["mz_s"], k)
                pe.matmul(pS[:, :], w1d2[:, :], hts[:, 1, :], start=True, stop=True)
                for j in range(T // 2):
                    last = pe.matmul(pS[:, j * P:(j + 1) * P], we[:, 0, j % 2, :],
                                     EL[:, r, (2 + j // 2) * P:(3 + j // 2) * P], start=False,
                                     stop=True, skip_group_check=True)
                last.then_inc(s["rows_s"], 1)
                if known(k, 1):
                    pe.wait_ge(s["z_dense_ready"], k)
                for b in range(2):
                    for j in range(T // 2):
                        last = pe.matmul(pY[:, b, j * P:(j + 1) * P], htd[:, b, j * P:(j + 1) * P], w12[:, :],
                                         start=True, stop=True)
                last.then_inc(s["z_dense_made"], 1)
                logits(k, r, 0)

            def edges(k, r, turns_ahead):
                pe.wait_ge(s["h1_ready"], k + 1)
                if turns_ahead:
                    pe.wait_ge(s["hd_out"], k + 2)
                turned(pT[1], flat(H1[:, r, :, :]), s["h1_turned"])
                pe.wait_ge(s["h1t_ready"], k + 1)
                if known(k, 1):
                    pe.wait_ge(s["z_edge_ready"], k)
                for j in range(T // 2):
                    last = pe.matmul(pZ[:, j * P:(j + 1) * P], h1t[:, j * P:(j + 1) * P], w12[:, :],
                                     start=True, stop=True)
                last.then_inc(s["z_edge_made"], 1)

            def turn(k, r):
                if not isinstance(k, int) or k < U:
                    unit(k, r)
                if known(k, 1):
                    edges(k - 1, 1 - r, not isinstance(k, int) or k < U)

            turns(pe, 0, 3, U - 1, turn)
            turn(U - 1, 0)
            turn(U, 1)

            def seam(layer):
                pe.wait_ge(s["tails_ready"], layer + 1)
                for i, c in enumerate((14, 11, 10)):
                    last = pe.transpose(pS[0:1, i * P:(i + 1) * P], sm[:, c:c + 1], ident[:, :])
                last.then_inc(s["rows_turned"], 1)
                pe.transpose(pT[0][0:W + 2, 0:P], TS[:, :], ident[:, :]).then_inc(s["tails_turned"], 1)
                pe.wait_ge(s["row_exps"], layer + 1)
                pe.matmul(pM[:, 0:P], sel[:, 0, :], row[:, 7, 0:P], start=True, stop=False)
                pe.matmul(pM[:, 0:P], sel[:, 1, :], ones[0:1, :], start=False, stop=True)
                pe.matmul(pM[:, P:2 * P], sel[:, 0, :], row[:, 8, 0:P], start=True, stop=False)
                pe.matmul(pM[:, P:2 * P], sel[:, 1, :], row[:, 4, 0:P], start=False, stop=True
                          ).then_inc(s["decay_spread"], 1)
                pe.wait_ge(s["carries_made"], layer + 1)
                pe.transpose(pT[1][:, 0:W + 2], OT[0:W + 2, 0:P], ident[0:W + 2, 0:W + 2])
                pe.transpose(pS[:, 3 * P:3 * P + 1], row[:, 1, 0:P], ident[0:1, 0:1]).then_inc(s["carries_turned"], 1)
                pe.wait_ge(s["node_ready"], layer + 1)
                node = hh if layer == 0 else zh
                if layer == 0:
                    pe.transpose(pT[0][0:DE, P:2 * P], loopm[:, :], ident[:, :])
                pe.transpose(pT[0][0:D, 0:P], node[:, :], ident[:, :]).then_inc(s["node_turned"], 1)
                pe.wait_ge(s["node_out"], layer + 1)
                wn = w1d2 if layer == 0 else ident2
                pe.matmul(pM[0:D, 0:P], wn[0:D, 0:D], hht[0:D, :], start=True, stop=False)
                pe.matmul(pM[0:D, 0:P], we[0:DE, layer, 0, 0:D], lpt[:, :], start=False, stop=True
                          ).then_inc(s["loop_rows"], 1)
                pe.wait_ge(s["loop_leaky"], layer + 1)
                for h in range(2):
                    last = pe.matmul(pL[:, 4 * T:4 * T + 1], srz[:, h, :], attr[0:D, layer, h, 0:1],
                                     start=(h == 0), stop=(h == 1))
                last.then_inc(s["loop_logit"], 1)

            seam(0)
            pe.wait_ge(s["fixv_ready"], 1)
            pe.transpose(pT[0][0:D, 0:P], fixv[:, 1, :], ident[:, :]).then_inc(s["fix_turned"], 1)
            pe.wait_ge(s["fixt_ready"], 1)
            pe.matmul(pM[:, 0:D], fixt[:, :], w12[0:D, 0:D], start=True, stop=True).then_inc(s["zfix_made"], 1)
            pe.wait_ge(s["zfix_ready"], 1)

            def turn3(k, r):
                n = k + U
                pe.wait_ge(s[f"src2_in{r}"], scattered(k, r))
                pe.wait_ge(s[f"dst2_in{r}"], dma_uses(k, r, 48))
                pe.wait_ge(s["mz_m"], n)
                zs, zd = flat(ZS[:, r, :, :]), flat(ZD[:, r, :, :])
                for j in range(T // 2):
                    c = slice(j * P, (j + 1) * P)
                    pe.matmul(pM[:, c], zs[:, c], ident[:, :], start=True, stop=False)
                    pe.matmul(pM[:, c], zd[:, c], ident[:, :], start=False, stop=False)
                    last = pe.matmul(pM[:, c], we[:, 1, j % 2, :], EL[:, r, j // 2 * P:(j // 2 + 1) * P],
                                     start=False, stop=True)
                last.then_inc(s["rows_m"], 1)
                pe.wait_ge(s["mz_s"], n)
                for j in range(T // 2):
                    c = slice(j * P, (j + 1) * P)
                    pe.matmul(pS[:, c], zd[:, c], ident2[:, :], start=True, stop=False)
                    last = pe.matmul(pS[:, c], we[:, 1, j % 2, :], EL[:, r, (2 + j // 2) * P:(3 + j // 2) * P],
                                     start=False, stop=True)
                last.then_inc(s["rows_s"], 1)
                pe.wait_ge(s["rows_s"], n + 1)
                pe.nop().then_inc(s["rows2_done"], 1)
                logits(n, r, 1)

            turns(pe, 0, 3, U, turn3)
            seam(1)


_INS = ["x", "src", "dst", "edge_attr_32"] + [f"L0_gnn_{n}" for n in
        ("W1", "b1", "We1", "att1", "bias1", "W2", "b2", "We2", "att2", "bias2")]


def kernel(**inputs):
    import numpy as np
    import concourse.bacc as bacc
    from concourse.bass_utils import run_bass_kernel_spmd

    nc = bacc.Bacc("TRN2", target_bir_lowering=False, num_devices=1)
    arrays, args = {}, []
    for name in _INS:
        a = np.ascontiguousarray(inputs[name])
        arrays[f"in_{name}"] = a
        args.append(nc.dram_tensor(f"in_{name}", a.shape, mybir.dt.from_np(a.dtype), kind="ExternalInput").ap())
    out = nc.dram_tensor("out_0", tuple(inputs["x"].shape), F32, kind="ExternalOutput").ap()
    gnn_kernel(nc, *args, out)
    r = run_bass_kernel_spmd(nc, [arrays], core_ids=[0])
    return r.results[0]["out_0"]
```

```python
from contextlib import ExitStack

import concourse.bass as bass
from concourse import mybir

F32 = mybir.dt.float32
I32 = mybir.dt.int32
BF16 = mybir.dt.bfloat16
ALU = mybir.AluOpType
ACT = mybir.ActivationFunctionType
AX_X = mybir.AxisListType.X

P = 128
T = 8
D = 64
DE = 32
W = D + DE
NEG_SLOPE = 0.2
EPS = 1e-5
FAR = -1e30
SKIP = 200000.0
RSQRT_MAGIC = float(0x5F3759DF)
LN_STEPS = 19
SM_STEPS = 7
AG_STEPS = 11
AT_STEPS = 4


def gnn_kernel(nc, x, src, dst, ea, W1, b1, We1, att1, bias1, W2, b2, We2, att2, bias2, out):
    N = x.shape[0]
    E = src.shape[0]
    C = -(-E // (P * T)) * T
    U = C // T
    EP = P * C
    ROWS = E - (P - 1) * C
    DB = P * T
    NDB = -(-N // DB)
    TAILP = (N - (NDB - 1) * DB) // T
    assert 0 < ROWS <= C and NDB == 2 * U and (N - (NDB - 1) * DB) % T == 0 and U % 2 == 1
    F = T * D

    ea_pad = nc.dram_tensor("ea_pad", (EP, DE), F32, kind="Internal").ap()
    z_tab = nc.dram_tensor("z_tab", (N, D), F32, kind="Internal").ap()
    st_all = nc.dram_tensor("st_all", (U * P, W * T), F32, kind="Internal").ap()
    xd_all = nc.dram_tensor("xd_all", (U * P, F), F32, kind="Internal").ap()
    el_all = nc.dram_tensor("el_all", (U * P, F), F32, kind="Internal").ap()
    z_all = nc.dram_tensor("z_all", (U * P * T, D), F32, kind="Internal").ap()
    zd_all = nc.dram_tensor("zd_all", (U * P, F), F32, kind="Internal").ap()
    z_blk = z_all.rearrange("(u p t) d -> (u p) (t d)", p=P, t=T)
    ea_cols = ea_pad.rearrange("(p c) f -> p (c f)", p=P)

    with ExitStack() as ctx:
        def sb(name, shape, dt=F32):
            return ctx.enter_context(nc.sbuf_tensor(name, shape, dt))

        def ps(name, shape):
            return ctx.enter_context(nc.psum_tensor(name, shape, F32))

        def sem(name):
            return ctx.enter_context(nc.semaphore(name))

        src_i = sb("src_i", [P, C], I32)
        dst_i = sb("dst_i", [P, C], I32)
        gat_i = sb("gat_i", [P, U, 2, T], I32)
        sca_i = sb("sca_i", [P, C], I32)
        dext = sb("dext", [P, C + 2])
        edge_i = sb("edge_i", [P, 2], I32)
        same = sb("same", [P, C + 1])
        lastm = sb("lastm", [P, C])
        notlast = sb("notlast", [P, C])
        far = sb("far", [P, C])
        rcnt = sb("rcnt", [P, C])
        cnt = sb("cnt", [P, C])
        hend = sb("hend", [P, C])
        eq0 = sb("eq0", [P, C])
        tmpc = sb("tmpc", [P, C])
        tmpd = sb("tmpd", [P, C])
        iota_c = sb("iota_c", [P, C])
        iota_p = sb("iota_p", [P, 1])
        m_all = sb("m_all", [P, C + 1])
        den_all = sb("den_all", [P, C + 1])
        gidx = sb("gidx", [P, 2, 2 * T], I32)
        sidx = sb("sidx", [P, 2, T], I32)

        ident = sb("ident", [P, P])
        ident2 = sb("ident2", [P, P])
        w1d = sb("w1d", [P, P])
        w1d2 = sb("w1d2", [P, P])
        w1t = sb("w1t", [P, P])
        w2d = sb("w2d", [P, P])
        w12 = sb("w12", [P, P])
        we = sb("we", [P, 2, 2, P])
        attp = sb("attp", [P, 2, 2])
        attr = sb("attr", [P, 2, 2, 2])
        vecs = sb("vecs", [P, 4])
        vsum = sb("vsum", [P, 1])
        vrep = sb("vrep", [P, P])
        zb = sb("zb", [P, 2])
        rows = sb("rows", [P, 2, D])
        cb = sb("cb", [P, D])
        ones = sb("ones", [P, P])
        ones_h = sb("ones_h", [P, P], BF16)
        cb3 = sb("cb3", [P, F], BF16)
        part = sb("part", [P, 3, D], BF16)
        rest = sb("rest", [P, 3, D])
        third = sb("third", [P, 3])

        X = sb("X", [P, 2, 2 * T, D])
        XD = sb("XD", [P, 4, 2 * T, D])
        H = sb("H", [P, 2, 2 * T, D])
        HD = sb("HD", [P, 2, 2 * T, D])
        EA = sb("EA", [P, 2, T, DE])
        LA = sb("LA", [P, 2, T, DE])
        ST = sb("ST", [P, 2, W, T])
        H1 = sb("H1", [P, 2, T, D])
        ZE = sb("ZE", [P, 2, F])
        TD = sb("TD", [P, 2, 2, F])
        OD = sb("OD", [P, 2, 2 * T, D])
        EL = sb("EL", [P, 2, F])
        DX = sb("DX", [P, 2, 4 * T])
        EX = sb("EX", [P, 2, 4 * T])
        stats = sb("stats", [P, 4 * T, 6])
        lnb = sb("lnb", [P, 8, 4 * T])
        meanb = sb("meanb", [P, 2, 4 * T])
        mx8 = sb("mx8", [P, T])
        rstd = sb("rstd", [P, 2, 4 * T])
        nmr = sb("nmr", [P, 2, 4 * T])
        htd = sb("htd", [P, 2, F])
        hts = sb("hts", [P, 2, F])
        mz = sb("mz", [P, 4, F])
        V = sb("V", [P, W, T])
        RM = sb("RM", [P, W, T])
        h1t = sb("h1t", [P, F])
        tmpf = sb("tmpf", [P, 2, T, D])
        fin = sb("fin", [P, 4, T])

        pT = [ps(f"pT{i}", [P, F]) for i in range(2)]
        pM = ps("pM", [P, F])
        pS = ps("pS", [P, F])
        pY = ps("pY", [P, 2, F])
        pZ = ps("pZ", [P, F])
        pL = ps("pL", [P, F])

        HB = sb("HB", [P, W * T])
        HS = sb("HS", [P, W + 2])
        TS = sb("TS", [P, W + 2])
        sm = sb("sm", [P, 24])
        smi = sb("smi", [P, 6], I32)
        mask8 = sb("mask8", [P, T])
        xh = sb("xh", [P, D])
        hh = sb("hh", [P, D])
        zh = sb("zh", [P, D])
        row = sb("row", [1, 12, P + 1])
        sel = sb("sel", [1, 2, P])
        OT = sb("OT", [P, P + 1])
        QT = sb("QT", [P, P])
        CS = sb("CS", [P, P])
        loopm = sb("loopm", [P, DE])
        hht = sb("hht", [P, P])
        lpt = sb("lpt", [DE, P])
        srz = sb("srz", [D, 2, P])
        fixv = sb("fixv", [P, 2, D])
        fixt = sb("fixt", [D, P])
        zfix = sb("zfix", [P, D])
        tailc = sb("tailc", [P, D])

        ZS = sb("ZS", [P, 2, T, D])
        ZD = sb("ZD", [P, 2, T, D])
        XR = sb("XR", [P, 2, T, D])
        OE = sb("OE", [P, 2, T, D])
        ZL = sb("ZL", [P, 2, T, D])
        ZB = sb("ZB", [P, 2, T, D])

        names = {}

        class Sems:

            def __getitem__(self, name):
                if name not in names:
                    names[name] = sem(name)
                return names[name]

        s = Sems()

        def turns(eng, first, peeled, end, body, by=2):
            for t in range(first, first + peeled):
                body(t, t % by)
            t0 = first + peeled
            rounds = (end - t0) // by
            with eng.Fori(0, rounds) as i:
                for t in range(t0, t0 + by):
                    body(i * by + t, t % by)
            for t in range(t0 + by * rounds, end):
                body(t, t % by)

        def known(k, n):
            return not isinstance(k, int) or k >= n

        def gathered(k, r):
            return (k - r) // 2 * (32 * T) + 32 * T if isinstance(k, int) else (k - r) * (16 * T) + 32 * T

        def scattered(k, r):
            return (k - r) // 2 * (16 * T) + 16 * T if isinstance(k, int) else (k - r) * (8 * T) + 16 * T

        def dma_uses(k, r, n=16, ring=2):
            return (k - r) // ring * n + n if isinstance(k, int) else (k - r) * (n // ring) + n

        def wait(eng, signal, value, went_on):
            eng.wait_ge(signal, value)
            if not isinstance(value, int):
                eng.sem_inc(went_on, 1)

        block = ctx.enter_context(nc.Block())

        @block.sync
        def _(sp):
            wait(sp, s["pads_set"], 1, s["sp_went_on"])
            full = (P - 1) * C
            sp.dma_start(src_i[0:P - 1, :], src[0:full].rearrange("(p c) -> p c", c=C)).then_inc(s["idx_in"], 16)
            sp.dma_start(src_i[P - 1:P, 0:ROWS], src[full:E].rearrange("(p c) -> p c", p=1)).then_inc(s["idx_in"], 16)
            sp.dma_start(dst_i[0:P - 1, :], dst[0:full].rearrange("(p c) -> p c", c=C)).then_inc(s["idx_in"], 16)
            sp.dma_start(dst_i[P - 1:P, 0:ROWS], dst[full:E].rearrange("(p c) -> p c", p=1)).then_inc(s["idx_in"], 16)
            sp.dma_start(edge_i[1:P, 0:1], dst[0:full].rearrange("(p c) -> p c", c=C)[:, C - 1:C],
                         allow_slow_non_contiguous=True).then_inc(s["idx_in"], 16)
            sp.dma_start(edge_i[0:P - 2, 1:2], dst[C:full].rearrange("(p c) -> p c", c=C)[:, 0:1],
                         allow_slow_non_contiguous=True).then_inc(s["idx_in"], 16)
            sp.dma_start(edge_i[P - 2:P - 1, 1:2], dst[full:full + 1].rearrange("(p c) -> p c", p=1)).then_inc(s["idx_in"], 16)

            sp.dma_start(ea_pad[0:E, :].rearrange("(a b) f -> a (b f)", a=16),
                         ea.rearrange("(a b) f -> a (b f)", a=16)).then_inc(s["ea_padded"], 16)
            padr = EP - E
            sp.dma_start(ea_pad[E:EP, :].rearrange("(a b) f -> a (b f)", a=16),
                         ZB[0:16, 0, :, :].rearrange("p t d -> p (t d)")[:, 0:padr // 16 * DE]).then_inc(s["ea_padded"], 16)

            for g in range(2):
                q = slice(g * D, (g + 1) * D)
                sp.dma_start(w1d[q, q], W1).then_inc(s["weights_in"], 16)
                sp.dma_start(w2d[q, q], W2).then_inc(s["weights_in"], 16)
                for l, (we_l, att_l) in enumerate(((We1, att1), (We2, att2))):
                    sp.dma_start(attp[q, l, g:g + 1], att_l.rearrange("(p c) -> p c", c=1)).then_inc(s["weights_in"], 16)
                    for v in range(2):
                        q2 = slice(v * D + g * DE, v * D + (g + 1) * DE)
                        sp.dma_start(we[q2, l, v, q], we_l).then_inc(s["weights_in"], 16)
                for c, v in enumerate((b1, bias1, bias2)):
                    sp.dma_start(vecs[q, c:c + 1], v.rearrange("(p c) -> p c", c=1)).then_inc(s["weights_in"], 16)
            for c, v in enumerate((b2, bias2)):
                sp.dma_start(rows[:, c, :], v.rearrange("(p c) -> p c", p=1).to_broadcast([P, D])).then_inc(s["weights_in"], 16)

            def load_dense(k, r):
                if known(k, 4):
                    wait(sp, s["dense_stats"], k - 3, s["sp_went_on"])
                    wait(sp, s["dense_normed"], k - 3, s["sp_went_on"])
                    wait(sp, s["out_dense_done"], k - 3, s["sp_went_on"])
                n0 = k * (2 * DB)
                if isinstance(k, int) and k == U - 1:
                    sp.dma_start(XD[:, r, 0:T, :], x[n0:n0 + DB, :].rearrange("(p t) d -> p t d", p=P)
                                 ).then_inc(s[f"dense_in{r}"], 16)
                    sp.dma_start(XD[0:TAILP, r, T:2 * T, :], x[n0 + DB:N, :].rearrange("(p t) d -> p t d", p=TAILP)
                                 ).then_inc(s[f"dense_in{r}"], 16)
                else:
                    for b in range(2):
                        sp.dma_start(XD[:, r, b * T:(b + 1) * T, :],
                                     x[bass.ds(n0 + b * DB, DB), :].rearrange("(p t) d -> p t d", p=P)
                                     ).then_inc(s[f"dense_in{r}"], 16)

            def load_edge_features(k, r):
                if not known(k, 2):
                    wait(sp, s["ea_padded"], 32, s["sp_went_on"])
                else:
                    wait(sp, s["ea_turned"], k - 1, s["sp_went_on"])
                    wait(sp, s["attr_step"], (k - 1) * AT_STEPS, s["sp_went_on"])
                sp.dma_start(EA[:, r, :, :].rearrange("p t f -> p (t f)"),
                             ea_cols[:, bass.ds(k * (T * DE), T * DE)]).then_inc(s[f"ea_in{r}"], 16)

            def store_z_dense(k, r):
                wait(sp, s["z_dense_ready"], k + 1, s["sp_went_on"])
                n0 = k * (2 * DB)
                for b in range(2):
                    if isinstance(k, int) and k == U - 1 and b == 1:
                        sp.dma_start(z_tab[n0 + DB:N, :].rearrange("(p t) d -> p (t d)", p=TAILP),
                                     TD[0:TAILP, r, b, :]).then_inc(s[f"z_dense_saved{r}"], 16)
                    else:
                        sp.dma_start(z_tab[bass.ds(n0 + b * DB, DB), :].rearrange("(p t) d -> p (t d)", p=P),
                                     TD[:, r, b, :]).then_inc(s[f"z_dense_saved{r}"], 16)

            def store_out_dense(k, r):
                wait(sp, s["out_dense_done"], k + 1, s["sp_went_on"])
                n0 = k * (2 * DB)
                for b in range(2):
                    if isinstance(k, int) and k == U - 1 and b == 1:
                        sp.dma_start(out[n0 + DB:N, :].rearrange("(p t) d -> p t d", p=TAILP),
                                     OD[0:TAILP, r, T:2 * T, :]).then_inc(s[f"out_dense_saved{r}"], 16)
                    else:
                        sp.dma_start(out[bass.ds(n0 + b * DB, DB), :].rearrange("(p t) d -> p t d", p=P),
                                     OD[:, r, b * T:(b + 1) * T, :]).then_inc(s[f"out_dense_saved{r}"], 16)

            def turn(k, r4):
                r = r4 % 2
                late = isinstance(k, int) and k >= U
                if not late:
                    wait(sp, s[f"gathered{r}"], gathered(k, r), s["sp_went_on"])
                    sp.dma_start(xd_all[bass.ds(k * P, P), :],
                                 X[:, r, T:2 * T, :].rearrange("p t d -> p (t d)")).then_inc(s[f"xd_saved{r}"], 16)
                if known(k, 2) and not (late and k - 2 >= U):
                    wait(sp, s["h1_ready"], k - 1, s["sp_went_on"])
                    sp.dma_start(st_all[bass.ds((k - 2) * P, P), 0:F],
                                 ST[:, r, 0:D, :].rearrange("p f t -> p (f t)")).then_inc(s[f"state_saved{r}"], 16)
                    store_out_dense(k - 2, r)
                if not isinstance(k, int) or k + 2 < U:
                    load_dense(k + 2, (r4 + 2) % 4)
                if not late:
                    wait(sp, s["attr_step"], k * AT_STEPS + 3, s["sp_went_on"])
                    sp.dma_start(st_all[bass.ds(k * P, P), F:W * T],
                                 ST[:, r, D:W, :].rearrange("p f t -> p (f t)")).then_inc(s[f"sums_saved{r}"], 16)
                if known(k, 3):
                    wait(sp, s["z_edge_ready"], k - 2, s["sp_went_on"])
                    sp.dma_start(z_blk[bass.ds((k - 3) * P, P), :], ZE[:, 1 - r, :]).then_inc(s[f"z_edge_saved{1 - r}"], 16)
                if not late:
                    wait(sp, s["el_ready"], k + 1, s["sp_went_on"])
                    sp.dma_start(el_all[bass.ds(k * P, P), :], EL[:, r, :]).then_inc(s[f"el_saved{r}"], 16)
                if not isinstance(k, int) or k + 1 < U:
                    load_edge_features(k + 1, 1 - r)
                if known(k, 1) and not (late and k - 1 >= U):
                    store_z_dense(k - 1, 1 - r)

            load_dense(0, 0)
            load_edge_features(0, 0)
            load_dense(1, 1)
            turns(sp, 0, 4, U - 3, turn, 4)
            for k in range(U - 3, U + 3):
                turn(k, k % 4)

            wait(sp, s["z_patched"], 16, s["sp_went_on"])

            def turn2(k, r):
                u = (U - 1) - k
                if known(k, 2):
                    wait(sp, s[f"z_scattered{r}"], scattered(k - 2, r), s["sp_went_on"])
                    wait(sp, s["zd_ready"], k - 1, s["sp_went_on"])
                sp.dma_start(ZL[:, r, :, :].rearrange("p t d -> p (t d)"),
                             z_blk[bass.ds(u * P, P), :]).then_inc(s[f"z_back{r}"], 16)
                if known(k, 1):
                    store_zd(k - 1, 1 - r)

            def store_zd(k, r):
                u = (U - 1) - k
                wait(sp, s["zd_ready"], k + 1, s["sp_went_on"])
                sp.dma_start(zd_all[bass.ds(u * P, P), :],
                             ZB[:, r, :, :].rearrange("p t d -> p (t d)")).then_inc(s[f"zd_saved{r}"], 16)

            turns(sp, 0, 3, U, turn2)
            store_zd(U - 1, 0)

            for r in range(2):
                wait(sp, s[f"zd_saved{r}"], 16 * ((U + 1 - r) // 2), s["sp_went_on"])
                wait(sp, s[f"xd_saved{r}"], 16 * ((U + 1 - r) // 2), s["sp_went_on"])
                wait(sp, s[f"el_saved{r}"], 16 * ((U + 1 - r) // 2), s["sp_went_on"])

            def turn3(k, r):
                if known(k, 2):
                    wait(sp, s["agg2_done"], k - 1, s["sp_went_on"])
                    wait(sp, s["rows2_done"], k - 1, s["sp_went_on"])
                sp.dma_start(ZD[:, r, :, :].rearrange("p t d -> p (t d)"),
                             zd_all[bass.ds(k * P, P), :]).then_inc(s[f"dst2_in{r}"], 16)
                sp.dma_start(XR[:, r, :, :].rearrange("p t d -> p (t d)"),
                             xd_all[bass.ds(k * P, P), :]).then_inc(s[f"dst2_in{r}"], 16)
                sp.dma_start(EL[:, r, :], el_all[bass.ds(k * P, P), :]).then_inc(s[f"dst2_in{r}"], 16)
                if known(k, 1):
                    store_st(k - 1, 1 - r)

            def store_st(k, r):
                wait(sp, s["agg2_done"], k + 1, s["sp_went_on"])
                sp.dma_start(st_all[bass.ds(k * P, P), 0:F],
                             ST[:, r, 0:D, :].rearrange("p f t -> p (f t)")).then_inc(s[f"state2_saved{r}"], 16)

            turns(sp, 0, 3, U, turn3)
            store_st(U - 1, 0)

            for r in range(2):
                wait(sp, s[f"out_dense_saved{r}"], 32 * ((U + 1 - r) // 2), s["sp_went_on"])
                wait(sp, s[f"state2_saved{r}"], 16 * ((U + 1 - r) // 2), s["sp_went_on"])
            wait(sp, s["out_fixed"], 16, s["sp_went_on"])

        @block.gpsimd
        def _(pool):
            pool.memset(ident[:, :], 0.0).then_inc(s["ident_zero"], 1)
            wait(pool, s["ident_zero"], 1, s["pool_went_on"])
            pool.affine_select(out=ident[:, :], in_=ident[:, :], compare_op=ALU.not_equal, fill=1.0, base=0,
                               pattern=[[-1, P]], channel_multiplier=1).then_inc(s["ident_ready"], 1)
            pool.iota(iota_c[:, :], pattern=[[1, C]], base=0, channel_multiplier=0,
                      allow_small_or_imprecise_dtypes=True).then_inc(s["iotas"], 1)
            pool.iota(iota_p[:, :], pattern=[[0, 1]], base=0, channel_multiplier=1,
                      allow_small_or_imprecise_dtypes=True).then_inc(s["iotas"], 1)

            def gather(to, table, index, signal):
                pool.indirect_dma_start(out=to, out_offset=None, in_=table,
                                        in_offset=bass.IndirectOffsetOnAxis(ap=index, axis=0)).then_inc(signal, 16)

            def scatter(table, index, frm, signal, limit):
                pool.indirect_dma_start(out=table, out_offset=bass.IndirectOffsetOnAxis(ap=index, axis=0), in_=frm,
                                        in_offset=None, bounds_check=limit, oob_is_err=False).then_inc(signal, 16)

            def turn(k, r):
                if known(k, 2):
                    wait(pool, s["stats_read"], k - 1, s["pool_went_on"])
                    wait(pool, s["edges_step"], (k - 1) * 4, s["pool_went_on"])
                    wait(pool, s[f"xd_saved{r}"], dma_uses(k - 2, r), s["pool_went_on"])
                pool.tensor_copy(gidx[:, r, :], gat_i[:, bass.ds(k, 1), :, :].rearrange("p u s t -> p (u s t)")
                                 ).then_inc(s["gidx_ready"], 1)
                wait(pool, s["gidx_ready"], k + 1, s["pool_went_on"])
                for t in range(2 * T):
                    gather(X[:, r, t, :], x, gidx[:, r, t:t + 1], s[f"gathered{r}"])

            wait(pool, s["gat_i_ready"], 2, s["pool_went_on"])
            turns(pool, 0, 3, U, turn)

            for r in range(2):
                wait(pool, s[f"state_saved{r}"], 16 * ((U + 1 - r) // 2), s["pool_went_on"])
                wait(pool, s[f"sums_saved{r}"], 16 * ((U + 1 - r) // 2), s["pool_went_on"])
            wait(pool, s["head_idx"], 1, s["pool_went_on"])
            gather(HB[:, :], st_all, smi[:, 0:1], s["head_in"])
            gather(xh[:, :], x, smi[:, 1:2], s["head_in"])
            for r in range(2):
                wait(pool, s[f"z_dense_saved{r}"], 32 * ((U + 1 - r) // 2), s["pool_went_on"])
                wait(pool, s[f"z_edge_saved{r}"], 16 * ((U + 1 - r) // 2), s["pool_went_on"])
            wait(pool, s["zfix_ready"], 1, s["pool_went_on"])
            scatter(z_all, smi[:, 3:4], zfix[:, :], s["z_patched"], U * P * T - 1)
            scatter(z_tab, smi[:, 2:3], zfix[:, :], s["z_fixed"], N - 1)
            wait(pool, s["z_fixed"], 16, s["pool_went_on"])
            gather(tailc[:, :], z_tab, smi[:, 4:5], s["tail_in"])
            gather(zh[:, :], z_tab, smi[:, 1:2], s["zh_in"])

            def turn2(k, r):
                u = (U - 1) - k
                if known(k, 2):
                    wait(pool, s[f"z_scattered{r}"], scattered(k - 2, r), s["pool_went_on"])
                pool.tensor_copy(sidx[:, r, :], sca_i[:, bass.ds(u * T, T)]).then_inc(s["sidx_ready"], 1)
                wait(pool, s["sidx_ready"], k + 1, s["pool_went_on"])
                wait(pool, s[f"z_back{r}"], dma_uses(k, r), s["pool_went_on"])
                for t in range(T):
                    scatter(z_tab, sidx[:, r, t:t + 1], ZL[:, r, t, :], s[f"z_scattered{r}"], N - 1)

            turns(pool, 0, 3, U, turn2)

            for r in range(2):
                wait(pool, s[f"z_scattered{r}"], 16 * T * ((U + 1 - r) // 2), s["pool_went_on"])
                wait(pool, s[f"out_dense_saved{r}"], 32 * ((U + 1 - r) // 2), s["pool_went_on"])
            wait(pool, s["tail_in"], 16, s["pool_went_on"])

            def fetch(k, r):
                if known(k, 2):
                    wait(pool, s["agg2_done"], k - 1, s["pool_went_on"])
                    wait(pool, s["rows2_done"], k - 1, s["pool_went_on"])
                pool.tensor_copy(gidx[:, r, 0:T], gat_i[:, bass.ds(k, 1), 0, :].rearrange("p u t -> p (u t)")
                                 ).then_inc(s["gidx_ready"], 1)
                wait(pool, s["gidx_ready"], k + (U + 1), s["pool_went_on"])
                for t in range(T):
                    gather(ZS[:, r, t, :], z_tab, gidx[:, r, t:t + 1], s[f"src2_in{r}"])

            def put(k, r):
                if known(k, 2):
                    wait(pool, s[f"out_scattered{r}"], scattered(k - 2, r), s["pool_went_on"])
                pool.tensor_copy(sidx[:, r, :], sca_i[:, bass.ds(k * T, T)]).then_inc(s["sidx_ready"], 1)
                wait(pool, s["sidx_ready"], k + (U + 1), s["pool_went_on"])
                wait(pool, s["agg2_done"], k + 1, s["pool_went_on"])
                for t in range(T):
                    scatter(out, sidx[:, r, t:t + 1], OE[:, r, t, :], s[f"out_scattered{r}"], N - 1)

            def turn3(k, r):
                fetch(k, r)
                if known(k, 2):
                    put(k - 2, r)

            turns(pool, 0, 4, U, turn3)
            put(U - 2, (U - 2) % 2)
            put(U - 1, (U - 1) % 2)

            for r in range(2):
                wait(pool, s[f"state2_saved{r}"], 16 * ((U + 1 - r) // 2), s["pool_went_on"])
            gather(HB[:, :], st_all, smi[:, 0:1], s["head_in"])
            wait(pool, s["outfix_ready"], 1, s["pool_went_on"])
            scatter(out, smi[:, 2:3], zfix[:, :], s["out_fixed"], N - 1)
            for r in range(2):
                wait(pool, s[f"out_scattered{r}"], 16 * T * ((U + 1 - r) // 2), s["pool_went_on"])

        def link(eng, name, ins, also=None, n=1):
            links[name] = links.get(name, 0) + 1
            ins.then_inc(s[name], 1)
            eng.wait_ge(s[name], links[name])
            if also is not None:
                eng.sem_inc(also, n)

        links = {}

        def bc(ap, n):
            return ap.unsqueeze(2).to_broadcast([P, ap.shape[1], n])

        def weave(*chains):
            chains = list(chains)
            while chains:
                for c in list(chains):
                    if next(c, "end") == "end":
                        chains.remove(c)

        def softmax_logits(dve, k, q, n):
            a = bass.ds(k * T, T)
            m = m_all[:, bass.ds(k * T + 1, T)]
            L = pL[:, q * 2 * T:q * 2 * T + T]
            Ls = pL[:, q * 2 * T + T:(q + 1) * 2 * T]
            dx = [DX[:, q, i * T:(i + 1) * T] for i in range(4)]
            step = s["soft_step"]
            base = n * SM_STEPS
            dve.wait_ge(s["logits_ready"], n + 1)
            dve.tensor_tensor_scan(m, far[:, a], L, m_all[:, bass.ds(k * T, 1)], ALU.add, ALU.max).then_inc(step, 1)
            yield
            dve.wait_ge(step, base + 1)
            dve.tensor_tensor(dx[0], m_all[:, a], far[:, a], ALU.add).then_inc(step, 1)
            dve.tensor_tensor(dx[1], L, m, ALU.subtract).then_inc(step, 1)
            dve.tensor_tensor(mx8[:, :], m, Ls, ALU.max).then_inc(step, 1)
            yield
            dve.wait_ge(step, base + 4)
            dve.tensor_tensor(dx[0], dx[0], m, ALU.subtract).then_inc(step, 1)
            dve.tensor_tensor(dx[2], m, mx8[:, :], ALU.subtract).then_inc(step, 1)
            dve.tensor_tensor(dx[3], Ls, mx8[:, :], ALU.subtract).then_inc(step, 1)
            yield

        def aggregate(dve, k, q, n, hs, hd, relu, before_state):
            b = bass.ds(k * T + 1, T)
            ex = [EX[:, q, i * T:(i + 1) * T] for i in range(4)]
            step = s["agg_step"]
            base = n * AG_STEPS
            acc = ST[:, q, 0:D, :]
            prev = ST[:, 1 - q, 0:D, T - 1]
            dve.wait_ge(s["exps_ready"], n + 1)
            if relu:
                dve.scalar_tensor_tensor(out=V[:, 0:D, :].rearrange("p f t -> p t f"), in0=hs, scalar=0.0,
                                         in1=bc(ex[1], D), op0=ALU.max, op1=ALU.mult).then_inc(step, 1)
            else:
                dve.tensor_tensor(V[:, 0:D, :].rearrange("p f t -> p t f"), hs, bc(ex[1], D), ALU.mult
                                  ).then_inc(step, 1)
            dve.tensor_tensor_scan(den_all[:, b], ex[0], ex[1], den_all[:, bass.ds(k * T, 1)],
                                   ALU.mult, ALU.add).then_inc(step, 1)
            yield
            dve.wait_ge(step, base + 2)
            dve.scalar_tensor_tensor(out=V[:, 0:D, 0], in0=prev, scalar=EX[:, q, 0:1], in1=V[:, 0:D, 0],
                                     op0=ALU.mult, op1=ALU.add).then_inc(step, 1)
            dve.tensor_tensor(fin[:, 0, :], den_all[:, b], ex[2], ALU.mult).then_inc(step, 1)
            yield
            dve.wait_ge(step, base + 4)
            dve.wait_ge(s["decay_ready"], n + 1)
            before_state()
            dve.tensor_tensor_scan(acc.rearrange("p f t -> p (f t)"), RM[:, 0:D, :].rearrange("p f t -> p (f t)"),
                                   V[:, 0:D, :].rearrange("p f t -> p (f t)"), 0.0, ALU.mult, ALU.add
                                   ).then_inc(step, 1)
            dve.tensor_tensor(fin[:, 0, :], fin[:, 0, :], ex[3], ALU.add).then_inc(step, 1)
            yield
            dve.wait_ge(step, base + 6)
            dve.reciprocal(fin[:, 1, :], fin[:, 0, :]).then_inc(step, 1)
            yield
            dve.wait_ge(step, base + 7)
            dve.tensor_tensor(fin[:, 2, :], ex[2], fin[:, 1, :], ALU.mult).then_inc(step, 1)
            dve.tensor_tensor(fin[:, 3, :], ex[3], fin[:, 1, :], ALU.mult).then_inc(step, 1)
            yield
            dve.wait_ge(step, base + 9)
            dve.tensor_tensor(tmpf[:, 0, :, :], acc.rearrange("p f t -> p t f"), bc(fin[:, 2, :], D),
                              ALU.mult).then_inc(step, 1)
            if relu:
                dve.scalar_tensor_tensor(out=tmpf[:, 1, :, :], in0=hd, scalar=0.0, in1=bc(fin[:, 3, :], D),
                                         op0=ALU.max, op1=ALU.mult).then_inc(step, 1)
            else:
                dve.tensor_tensor(tmpf[:, 1, :, :], hd, bc(fin[:, 3, :], D), ALU.mult).then_inc(step, 1)
            yield
            dve.wait_ge(step, base + 11)

        @block.vector
        def _(dve):
            link(dve, "setup", dve.memset(src_i[:, :], 0))
            link(dve, "setup", dve.memset(dst_i[:, :], N))
            link(dve, "setup", dve.memset(edge_i[:, :], -1))
            link(dve, "setup", dve.memset(ZB[:, :, :, :], 0.0))
            link(dve, "setup", dve.memset(w1d[:, :], 0.0))
            link(dve, "setup", dve.memset(w2d[:, :], 0.0))
            link(dve, "setup", dve.memset(attp[:, :, :], 0.0))
            link(dve, "setup", dve.memset(we[:, :, :, :], 0.0), s["pads_set"], 1)
            link(dve, "setup", dve.memset(ones[:, :], 1.0))
            link(dve, "setup", dve.memset(ST[:, :, :, :], 0.0))
            link(dve, "setup", dve.memset(RM[:, :, :], 0.0))
            link(dve, "setup", dve.memset(m_all[:, 0:1], FAR))
            link(dve, "setup", dve.memset(den_all[:, 0:1], 0.0))
            link(dve, "setup", dve.memset(same[:, C:C + 1], 0.0))
            link(dve, "setup", dve.memset(sel[:, 0, :], 1.0))
            link(dve, "setup", dve.memset(sel[:, 1, :], 0.0))
            link(dve, "setup", dve.memset(row[:, :, :], 0.0))
            link(dve, "setup", dve.memset(OT[:, :], 0.0))
            link(dve, "setup", dve.memset(sel[:, 0, D:W], 0.0))
            link(dve, "setup", dve.memset(sel[:, 0, W + 1:W + 2], 0.0))
            link(dve, "setup", dve.memset(sel[:, 1, D:W], 1.0))
            link(dve, "setup", dve.memset(sel[:, 1, W + 1:W + 2], 1.0))
            link(dve, "setup", dve.memset(row[:, 1, 0:1], FAR))

            dve.wait_ge(s["idx_in"], 16 * 7)
            link(dve, "setup", dve.tensor_copy(dext[:, 1:C + 1], dst_i[:, :]))
            link(dve, "setup", dve.tensor_copy(dext[:, 0:1], edge_i[:, 0:1]))
            link(dve, "setup", dve.tensor_copy(dext[:, C + 1:C + 2], edge_i[:, 1:2]))
            link(dve, "setup", dve.tensor_copy(gat_i[:, :, 0, :], src_i[:, :].rearrange("p (u t) -> p u t", t=T)))
            link(dve, "setup", dve.tensor_scalar(gat_i[:, :, 1, :], dext[:, 1:C + 1].rearrange("p (u t) -> p u t", t=T),
                              float(N - 1), None, ALU.min), s["gat_i_ready"], 2)
            link(dve, "setup", dve.tensor_tensor(same[:, 0:C], dext[:, 1:C + 1], dext[:, 0:C], ALU.is_equal))
            link(dve, "setup", dve.tensor_tensor(notlast[:, :], dext[:, 1:C + 1], dext[:, 2:C + 2], ALU.is_equal))
            link(dve, "setup", dve.tensor_scalar(eq0[:, :], dext[:, 1:C + 1], dext[:, 1:2], None, ALU.is_equal))
            link(dve, "setup", dve.tensor_copy(sm[:, 0:1], same[:, 0:1]))
            link(dve, "setup", dve.tensor_copy(sm[:, 1:2], eq0[:, C - 1:C]))
            link(dve, "setup", dve.tensor_scalar(lastm[:, :], notlast[:, :], -1.0, 1.0, ALU.mult, ALU.add))
            link(dve, "setup", dve.memset(same[:, 0:1], 0.0))
            link(dve, "setup", dve.tensor_scalar(far[:, :], same[:, 0:C], 1.0, -FAR, ALU.subtract, ALU.mult))
            link(dve, "setup", dve.tensor_scalar(tmpc[:, :], same[:, 1:C + 1], -1.0, 1.0, ALU.mult, ALU.add))
            link(dve, "setup", dve.tensor_scalar(tmpd[:, :], eq0[:, :], sm[:, 0:1], None, ALU.mult))
            link(dve, "setup", dve.tensor_tensor_scan(cnt[:, :], same[:, 0:C], ones[:, 0:1].to_broadcast([P, C]), 0.0,
                                                      ALU.mult, ALU.add))
            link(dve, "setup", dve.reciprocal(rcnt[:, :], cnt[:, :]))
            link(dve, "setup", dve.tensor_scalar(tmpd[:, :], tmpd[:, :], -1.0, 1.0, ALU.mult, ALU.add))
            link(dve, "setup", dve.tensor_tensor(hend[:, :], eq0[:, :], tmpc[:, :], ALU.mult))
            link(dve, "setup", dve.tensor_tensor(tmpd[:, :], tmpd[:, :], lastm[:, :], ALU.mult))
            link(dve, "setup", dve.scalar_tensor_tensor(out=tmpd[:, :], in0=dext[:, 1:C + 1], scalar=SKIP,
                                                        in1=tmpd[:, :], op0=ALU.subtract, op1=ALU.mult))
            link(dve, "setup", dve.tensor_scalar(sca_i[:, :], tmpd[:, :], SKIP, None, ALU.add))
            dve.wait_ge(s["iotas"], 2)
            link(dve, "setup", dve.tensor_tensor(tmpc[:, :], hend[:, :], iota_c[:, :], ALU.mult))
            link(dve, "setup", dve.tensor_reduce(sm[:, 2:3], tmpc[:, :], AX_X, ALU.add))
            link(dve, "setup", dve.tensor_tensor(tmpc[:, :], hend[:, :], lastm[:, :], ALU.mult))
            link(dve, "setup", dve.tensor_reduce(sm[:, 3:4], tmpc[:, :], AX_X, ALU.add))
            link(dve, "setup", dve.tensor_copy(smi[:, 5:6], sm[:, 2:3]))
            link(dve, "setup", dve.tensor_scalar(smi[:, 0:1], smi[:, 5:6], 3, None, ALU.logical_shift_right))
            link(dve, "setup", dve.tensor_copy(sm[:, 4:5], smi[:, 0:1]))
            link(dve, "setup", dve.scalar_tensor_tensor(out=sm[:, 5:6], in0=sm[:, 4:5], scalar=-float(T),
                                                        in1=sm[:, 2:3], op0=ALU.mult, op1=ALU.add))
            link(dve, "setup", dve.tensor_scalar(mask8[:, :], iota_c[:, 0:T], sm[:, 5:6], None, ALU.is_equal))
            link(dve, "setup", dve.scalar_tensor_tensor(out=sm[:, 6:7], in0=sm[:, 4:5], scalar=float(P),
                                                        in1=iota_p[:, :], op0=ALU.mult, op1=ALU.add))
            link(dve, "setup", dve.tensor_copy(smi[:, 0:1], sm[:, 6:7]))
            link(dve, "setup", dve.scalar_tensor_tensor(out=sm[:, 7:8], in0=sm[:, 6:7], scalar=float(T), in1=sm[:, 5:6],
                                     op0=ALU.mult, op1=ALU.add))
            link(dve, "setup", dve.tensor_tensor(sm[:, 8:9], sm[:, 3:4], sm[:, 0:1], ALU.mult))
            link(dve, "setup", dve.scalar_tensor_tensor(out=sm[:, 9:10], in0=dext[:, 1:2], scalar=SKIP,
                                                        in1=sm[:, 8:9], op0=ALU.subtract, op1=ALU.mult))
            link(dve, "setup", dve.tensor_scalar(smi[:, 2:3], sm[:, 9:10], SKIP, None, ALU.add))
            link(dve, "setup", dve.scalar_tensor_tensor(out=sm[:, 9:10], in0=sm[:, 7:8], scalar=SKIP,
                                                        in1=sm[:, 8:9], op0=ALU.subtract, op1=ALU.mult))
            link(dve, "setup", dve.tensor_scalar(smi[:, 3:4], sm[:, 9:10], SKIP, None, ALU.add))
            link(dve, "setup", dve.tensor_scalar(smi[:, 1:2], dext[:, 1:2], float(N - 1), None, ALU.min))
            link(dve, "setup", dve.tensor_scalar(smi[:, 4:5], dext[:, C:C + 1], float(N - 1), None, ALU.min))
            link(dve, "setup", dve.tensor_tensor(sm[:, 10:11], sm[:, 0:1], sm[:, 1:2], ALU.mult))
            link(dve, "setup", dve.tensor_scalar(sm[:, 11:12], sm[:, 10:11], 1.0, -FAR, ALU.subtract, ALU.mult))
            link(dve, "setup", dve.tensor_scalar(sm[:, 12:13], sm[:, 0:1], 1.0, -FAR, ALU.subtract, ALU.mult), s["head_idx"], 1)

            dve.wait_ge(s["weights_in"], 16 * (2 * (2 + 2 + 4 + 3) + 2))
            dve.wait_ge(s["ident_ready"], 1)
            link(dve, "setup", dve.tensor_scalar(w1d2[:, :], w1d[:, :], 2.0, None, ALU.mult))
            link(dve, "setup", dve.tensor_scalar(ident2[:, :], ident[:, :], 2.0, None, ALU.mult))
            for l in range(2):
                link(dve, "setup", dve.tensor_scalar(attr[:, l, 0, :], attp[:, l, :], 1.0 - NEG_SLOPE, None, ALU.mult))
                link(dve, "setup", dve.tensor_scalar(attr[:, l, 1, :], attp[:, l, :], NEG_SLOPE, None, ALU.mult))
            link(dve, "setup", dve.tensor_scalar(zb[:, 0:1], vecs[:, 0:1], 2.0, None, ALU.mult))
            link(dve, "setup", dve.tensor_tensor(cb[:, :], rows[:, 0, :], rows[:, 1, :], ALU.add))
            link(dve, "setup", dve.tensor_tensor(vsum[:, :], vecs[:, 0:1], vecs[:, 1:2], ALU.add))
            link(dve, "setup", dve.tensor_scalar(vrep[:, :], ones[:, :], vsum[:, 0:1], None, ALU.mult), s["weights_made"], 1)
            dve.wait_ge(s["w1_turned"], 1)
            link(dve, "setup", dve.tensor_copy(w1t[:, :], pT[0][:, 0:P]), s["w1t_ready"], 1)
            dve.wait_ge(s["w12_made"], 1)
            link(dve, "setup", dve.tensor_copy(w12[:, :], pT[1][:, 0:P]))
            link(dve, "setup", dve.tensor_scalar(zb[:, 1:2], vecs[:, 2:3], -2.0, None, ALU.mult))
            link(dve, "setup", dve.tensor_tensor(cb[:, :], cb[:, :], pS[:, 0:D], ALU.add))
            for i in range(3):
                left = cb[:, :] if i == 0 else rest[:, i - 1, :]
                link(dve, "setup", dve.tensor_copy(part[:, i, :], left))
                link(dve, "setup", dve.tensor_tensor(rest[:, i, :], left, part[:, i, :], ALU.subtract))
                link(dve, "setup", dve.tensor_scalar(third[:, i:i + 1], iota_p[:, :], float(i), None, ALU.is_equal))
                link(dve, "setup", dve.tensor_scalar(part[:, i, :], part[:, i, :], third[:, i:i + 1], None, ALU.mult))
            link(dve, "setup", dve.tensor_tensor(part[:, 0, :], part[:, 0, :], part[:, 1, :], ALU.add))
            link(dve, "setup", dve.tensor_tensor(part[:, 0, :], part[:, 0, :], part[:, 2, :], ALU.add))
            link(dve, "setup", dve.tensor_copy(ones_h[:, :], ones[:, :]))
            link(dve, "setup", dve.tensor_copy(cb3[:, :].rearrange("p (a d) -> p a d", d=D),
                                               part[:, 0, :].unsqueeze(1).to_broadcast([P, T, D])),
                 s["consts_ready"], 1)
            dve.wait_ge(s["consts_ready"], 1)

            def edge_attrs(k, r):
                step = s["attr_step"]
                base = k * AT_STEPS
                Va = V[:, D:W, :]
                dve.wait_ge(s[f"ea_in{r}"], dma_uses(k, r))
                dve.tensor_copy(Va.rearrange("p f t -> p t f"), EA[:, r, :, :]).then_inc(step, 1)
                yield
                dve.wait_ge(step, base + 1)
                dve.scalar_tensor_tensor(out=V[:, D:W, 0], in0=ST[:, 1 - r, D:W, T - 1],
                                         scalar=same[:, bass.ds(k * T, 1)], in1=V[:, D:W, 0],
                                         op0=ALU.mult, op1=ALU.add).then_inc(step, 1)
                yield
                dve.wait_ge(step, base + 2)
                dve.wait_ge(s["mask_spread"], k + 1)
                if known(k, 2):
                    dve.wait_ge(s[f"sums_saved{r}"], dma_uses(k - 2, r))
                dve.tensor_tensor_scan(ST[:, r, D:W, :].rearrange("p f t -> p (f t)"),
                                       RM[:, D:W, :].rearrange("p f t -> p (f t)"),
                                       Va.rearrange("p f t -> p (f t)"), 0.0, ALU.mult, ALU.add).then_inc(step, 1)
                yield
                dve.wait_ge(step, base + 3)
                if known(k, 2):
                    dve.wait_ge(s["ea_turned"], k - 1)
                dve.tensor_tensor(LA[:, r, :, :], ST[:, r, D:W, :].rearrange("p f t -> p t f"),
                                  bc(rcnt[:, bass.ds(k * T, T)], DE), ALU.mult).then_inc(step, 1)
                yield

            def row_stats(k, r, r4):
                dve.wait_ge(s[f"gathered{r}"], gathered(k, r))
                for t in range(2 * T):
                    last = dve.bn_stats(stats[:, t, :], X[:, r, t, :])
                last.then_inc(s["stats_read"], 1)
                dve.wait_ge(s[f"dense_in{r4}"], dma_uses(k, r4, 32, 4))
                for t in range(2 * T):
                    last = dve.bn_stats(stats[:, 2 * T + t, :], XD[:, r4, t, :])
                last.then_inc(s["dense_stats"], 1)
                dve.wait_ge(s["dense_stats"], k + 1)

            def norm_chain(k, r):
                base = k * LN_STEPS
                step = s["stats_step"]
                me, ve, mo, vo = (stats[:, :, c] for c in (1, 2, 4, 5))
                t = [lnb[:, i, :] for i in range(7)]
                rs = rstd[:, r, :]
                mean = meanb[:, r, :]
                dve.tensor_tensor(t[0], me, mo, ALU.add).then_inc(step, 1)
                dve.tensor_tensor(t[1], me, mo, ALU.subtract).then_inc(step, 1)
                dve.tensor_tensor(t[2], ve, vo, ALU.add).then_inc(step, 1)
                yield
                dve.wait_ge(step, base + 3)
                dve.scalar_tensor_tensor(out=t[3], in0=t[1], scalar=0.25, in1=t[1],
                                         op0=ALU.mult, op1=ALU.mult).then_inc(step, 1)
                dve.tensor_scalar(t[4], t[2], 1.0 / D, EPS, ALU.mult, ALU.add).then_inc(step, 1)
                dve.tensor_scalar(mean, t[0], 0.5, None, ALU.mult).then_inc(step, 1)
                yield
                dve.wait_ge(step, base + 6)
                dve.tensor_tensor(t[5], t[3], t[4], ALU.add).then_inc(step, 1)
                yield
                dve.wait_ge(step, base + 7)
                dve.tensor_scalar(t[6].bitcast(I32), t[5].bitcast(I32), 1, None,
                                  ALU.logical_shift_right).then_inc(step, 1)
                yield
                dve.wait_ge(step, base + 8)
                dve.tensor_scalar(rs.bitcast(I32), t[6].bitcast(I32), -1.0, RSQRT_MAGIC,
                                  ALU.mult, ALU.add).then_inc(step, 1)
                yield
                n = 9
                for _ in range(3):
                    dve.wait_ge(step, base + n)
                    dve.scalar_tensor_tensor(out=t[0], in0=rs, scalar=-0.5, in1=rs,
                                             op0=ALU.mult, op1=ALU.mult).then_inc(step, 1)
                    yield
                    dve.wait_ge(step, base + n + 1)
                    dve.tensor_tensor(t[1], t[0], t[5], ALU.mult).then_inc(step, 1)
                    yield
                    dve.wait_ge(step, base + n + 2)
                    dve.scalar_tensor_tensor(out=rs, in0=t[1], scalar=1.5, in1=rs,
                                             op0=ALU.add, op1=ALU.mult).then_inc(step, 1)
                    yield
                    n += 3
                dve.wait_ge(step, base + n)
                dve.scalar_tensor_tensor(out=nmr[:, r, :], in0=mean, scalar=-1.0,
                                         in1=rs, op0=ALU.mult, op1=ALU.mult).then_inc(step, 1)
                assert n + 1 == LN_STEPS
                yield

            def edge_rows(k, r):
                if known(k, 2):
                    dve.wait_ge(s["hd_turned"], k - 1)
                for side in range(2):
                    c = slice(side * T, (side + 1) * T)
                    h = H[:, r, c, :]
                    step = s["edges_step"]
                    base = k * 4 + side * 2
                    dve.tensor_tensor(h, X[:, r, c, :], bc(meanb[:, r, c], D), ALU.subtract).then_inc(step, 1)
                    yield
                    dve.wait_ge(step, base + 1)
                    dve.tensor_tensor(h, h, bc(rstd[:, r, c], D), ALU.mult).then_inc(step, 1)
                    yield

            def out_dense(k, r, r4):
                dve.wait_ge(s["z_dense_ready"], k + 1)
                if known(k, 2):
                    dve.wait_ge(s[f"out_dense_saved{r}"], dma_uses(k - 2, r, 32))
                for b in range(2):
                    c = slice(b * T, (b + 1) * T)
                    last = dve.tensor_tensor(OD[:, r, c, :].rearrange("p t d -> p (t d)"),
                                             XD[:, r4, c, :].rearrange("p t d -> p (t d)"),
                                             TD[:, r, b, :], ALU.add)
                    if b == 0:
                        yield
                last.then_inc(s["out_dense_done"], 1)
                yield

            def mean1(k, r):
                def before_state():
                    if known(k, 2):
                        dve.wait_ge(s[f"state_saved{r}"], dma_uses(k - 2, r))

                yield from aggregate(dve, k, r, k, H[:, r, 0:T, :], H[:, r, T:2 * T, :], True, before_state)
                if known(k, 2):
                    dve.wait_ge(s["h1_turned"], k - 1)
                dve.tensor_tensor(H1[:, r, :, :], tmpf[:, 0, :, :], tmpf[:, 1, :, :], ALU.add
                                  ).then_inc(s["h1_ready"], 1)
                yield

            def turn(k, r4):
                r = r4 % 2
                late = isinstance(k, int) and k >= U
                if not late:
                    row_stats(k, r, r4)
                chains = [] if late else [norm_chain(k, r), edge_attrs(k, r)]
                if known(k, 2):
                    chains += [mean1(k - 2, r), out_dense(k - 2, r, (r4 + 2) % 4)]
                weave(*chains)
                chains = []
                if not late:
                    dve.wait_ge(s["stats_step"], k * LN_STEPS + LN_STEPS)
                    chains.append(edge_rows(k, r))
                if known(k, 1) and not (late and k - 1 >= U):
                    chains.append(softmax_logits(dve, k - 1, 1 - r, k - 1))
                weave(*chains)

            turns(dve, 0, 4, U - 1, turn, 4)
            for k in range(U - 1, U + 2):
                turn(k, k % 4)

            def spread_states(layer, rT, width):
                dve.wait_ge(s["head_in"], 32 if layer == 0 else 48)
                hb = HB[:, 0:width * T].rearrange("p (f t) -> p f t", t=T)
                link(dve, "seam", dve.tensor_tensor(V[:, 0:width, :], hb,
                                                    mask8[:, :].unsqueeze(1).to_broadcast([P, width, T]), ALU.mult))
                link(dve, "seam", dve.tensor_reduce(HS[:, 0:width], V[:, 0:width, :], AX_X, ALU.add))
                link(dve, "seam", dve.tensor_copy(TS[:, 0:width], ST[:, rT, 0:width, T - 1]))
                link(dve, "seam", dve.tensor_tensor(tmpc[:, :], hend[:, :], m_all[:, 1:C + 1], ALU.mult))
                link(dve, "seam", dve.tensor_reduce(sm[:, 13:14], tmpc[:, :], AX_X, ALU.add))
                link(dve, "seam", dve.tensor_tensor(tmpd[:, :], hend[:, :], den_all[:, 1:C + 1], ALU.mult))
                link(dve, "seam", dve.tensor_reduce(HS[:, W:W + 1], tmpd[:, :], AX_X, ALU.add))
                link(dve, "seam", dve.tensor_copy(TS[:, W:W + 1], den_all[:, C:C + 1]))
                if layer == 0:
                    link(dve, "seam", dve.tensor_tensor(tmpc[:, :], hend[:, :], cnt[:, :], ALU.mult))
                    link(dve, "seam", dve.tensor_reduce(HS[:, W + 1:W + 2], tmpc[:, :], AX_X, ALU.add))
                    link(dve, "seam", dve.tensor_copy(TS[:, W + 1:W + 2], cnt[:, C - 1:C]))
                link(dve, "seam", dve.tensor_copy(sm[:, 14:15], m_all[:, C:C + 1]))
                dve.sem_inc(s["tails_ready"], 1)

            def seam(layer, rT):
                width = W if layer == 0 else D
                spread_states(layer, rT, width)
                dve.wait_ge(s["rows_turned"], layer + 1)
                link(dve, "seam", dve.tensor_copy(row[:, 2:5, 0:P], pS[0:1, 0:3 * P].rearrange("p (a b) -> p a b", a=3)))
                link(dve, "seam", dve.tensor_tensor_scan(row[:, 1, 1:P + 1], row[:, 3, 0:P], row[:, 2, 0:P], FAR,
                                                         ALU.add, ALU.max))
                link(dve, "seam", dve.tensor_tensor(row[:, 5, 0:P], row[:, 2, 0:P], row[:, 1, 1:P + 1], ALU.subtract))
                link(dve, "seam", dve.tensor_tensor(row[:, 6, 0:P], row[:, 1, 0:P], row[:, 3, 0:P], ALU.add))
                link(dve, "seam", dve.tensor_tensor(row[:, 6, 0:P], row[:, 6, 0:P], row[:, 1, 1:P + 1], ALU.subtract))
                dve.sem_inc(s["row_exps_asked"], 1)
                dve.wait_ge(s["decay_spread"], layer + 1)
                link(dve, "seam", dve.tensor_copy(QT[0:W + 2, :], pM[0:W + 2, 0:P]))
                dve.wait_ge(s["tails_turned"], layer + 1)
                link(dve, "seam", dve.tensor_tensor(QT[0:W + 2, :], QT[0:W + 2, :], pT[0][0:W + 2, 0:P], ALU.mult))
                link(dve, "seam", dve.tensor_tensor_scan(OT[0:W + 2, 1:P + 1], pM[0:W + 2, P:2 * P], QT[0:W + 2, :], 0.0,
                                                         ALU.mult, ALU.add))
                dve.sem_inc(s["carries_made"], 1)
                dve.wait_ge(s["carries_turned"], layer + 1)
                link(dve, "seam", dve.tensor_copy(CS[:, 0:W + 2], pT[1][:, 0:W + 2]))
                link(dve, "seam", dve.tensor_scalar(sm[:, 15:16], pS[:, 3 * P:3 * P + 1], sm[:, 12:13], None, ALU.add))
                link(dve, "seam", dve.tensor_tensor(sm[:, 16:17], sm[:, 15:16], sm[:, 13:14], ALU.max))
                link(dve, "seam", dve.tensor_tensor(sm[:, 17:18], sm[:, 13:14], sm[:, 16:17], ALU.subtract))
                link(dve, "seam", dve.tensor_tensor(sm[:, 18:19], sm[:, 15:16], sm[:, 16:17], ALU.subtract))
                dve.sem_inc(s["seam_exps_asked"], 1)
                dve.wait_ge(s["seam_exps"], 2 * layer + 1)
                for a, b in ((0, D), (W, W + 1)):
                    link(dve, "seam", dve.tensor_scalar(HS[:, a:b], HS[:, a:b], sm[:, 19:20], None, ALU.mult))
                    link(dve, "seam", dve.scalar_tensor_tensor(out=HS[:, a:b], in0=CS[:, a:b], scalar=sm[:, 20:21],
                                                               in1=HS[:, a:b], op0=ALU.mult, op1=ALU.add))
                if layer == 0:
                    for a, b in ((D, W), (W + 1, W + 2)):
                        link(dve, "seam", dve.scalar_tensor_tensor(out=HS[:, a:b], in0=CS[:, a:b], scalar=sm[:, 0:1],
                                                                   in1=HS[:, a:b], op0=ALU.mult, op1=ALU.add))
                    link(dve, "seam", dve.reciprocal(sm[:, 21:22], HS[:, W + 1:W + 2]))
                    link(dve, "seam", dve.tensor_scalar(loopm[:, :], HS[:, D:W], sm[:, 21:22], None, ALU.mult))
                    mean = lnb[:, 0, 0:1]
                    link(dve, "seam", dve.bn_stats(stats[:, 0, :], xh[:, :]))
                    link(dve, "seam", dve.tensor_tensor(lnb[:, 0, 0:1], stats[:, 0, 1:2], stats[:, 0, 4:5], ALU.add))
                    link(dve, "seam", dve.tensor_tensor(lnb[:, 1, 0:1], stats[:, 0, 1:2], stats[:, 0, 4:5], ALU.subtract))
                    link(dve, "seam", dve.tensor_tensor(lnb[:, 2, 0:1], stats[:, 0, 2:3], stats[:, 0, 5:6], ALU.add))
                    link(dve, "seam", dve.scalar_tensor_tensor(out=lnb[:, 3, 0:1], in0=lnb[:, 1, 0:1], scalar=0.25, in1=lnb[:, 1, 0:1],
                                             op0=ALU.mult, op1=ALU.mult))
                    link(dve, "seam", dve.tensor_scalar(lnb[:, 4, 0:1], lnb[:, 2, 0:1], 1.0 / D, EPS, ALU.mult, ALU.add))
                    link(dve, "seam", dve.tensor_scalar(lnb[:, 7, 0:1], mean, 0.5, None, ALU.mult))
                    v = lnb[:, 5, 0:1]
                    y = lnb[:, 6, 0:1]
                    link(dve, "seam", dve.tensor_tensor(v, lnb[:, 3, 0:1], lnb[:, 4, 0:1], ALU.add))
                    link(dve, "seam", dve.tensor_scalar(y.bitcast(I32), v.bitcast(I32), 1, None,
                                                        ALU.logical_shift_right))
                    link(dve, "seam", dve.tensor_scalar(y.bitcast(I32), y.bitcast(I32), -1.0, RSQRT_MAGIC,
                                                        ALU.mult, ALU.add))
                    for _ in range(3):
                        link(dve, "seam", dve.scalar_tensor_tensor(out=lnb[:, 0, 0:1], in0=y, scalar=-0.5, in1=y,
                                                                   op0=ALU.mult, op1=ALU.mult))
                        link(dve, "seam", dve.tensor_tensor(lnb[:, 1, 0:1], lnb[:, 0, 0:1], v, ALU.mult))
                        link(dve, "seam", dve.scalar_tensor_tensor(out=y, in0=lnb[:, 1, 0:1], scalar=1.5, in1=y,
                                                                   op0=ALU.add, op1=ALU.mult))
                    link(dve, "seam", dve.tensor_scalar(hh[:, :], xh[:, :], lnb[:, 7, 0:1], y, ALU.subtract, ALU.mult))
                    link(dve, "seam", dve.tensor_scalar(hh[:, :], hh[:, :], 0.0, None, ALU.max))
                node = hh if layer == 0 else zh
                if layer == 1:
                    dve.wait_ge(s["zh_in"], 16)
                dve.sem_inc(s["node_ready"], 1)
                dve.wait_ge(s["loop_logit"], layer + 1)
                ls = pL[:, 4 * T:4 * T + 1]
                link(dve, "seam", dve.tensor_tensor(sm[:, 15:16], ls, sm[:, 16:17], ALU.max))
                link(dve, "seam", dve.tensor_tensor(sm[:, 17:18], sm[:, 16:17], sm[:, 15:16], ALU.subtract))
                link(dve, "seam", dve.tensor_tensor(sm[:, 18:19], ls, sm[:, 15:16], ALU.subtract))
                dve.sem_inc(s["seam_exps_asked"], 1)
                dve.wait_ge(s["seam_exps"], 2 * layer + 2)
                link(dve, "seam", dve.scalar_tensor_tensor(out=sm[:, 21:22], in0=HS[:, W:W + 1], scalar=sm[:, 19:20],
                                                           in1=sm[:, 20:21], op0=ALU.mult, op1=ALU.add))
                link(dve, "seam", dve.reciprocal(sm[:, 22:23], sm[:, 21:22]))
                link(dve, "seam", dve.tensor_scalar(sm[:, 19:21], sm[:, 19:21], sm[:, 22:23], None, ALU.mult))
                link(dve, "seam", dve.tensor_scalar(fixv[:, 0, :], HS[:, 0:D], sm[:, 19:20], None, ALU.mult))
                link(dve, "seam", dve.scalar_tensor_tensor(out=fixv[:, 1, :], in0=node[:, :], scalar=sm[:, 20:21],
                                                           in1=fixv[:, 0, :], op0=ALU.mult, op1=ALU.add))

            seam(0, 0)
            dve.sem_inc(s["fixv_ready"], 1)
            dve.wait_ge(s["zfix_made"], 1)
            link(dve, "seam", dve.tensor_tensor(zfix[:, :], pM[:, 0:D], cb[:, :], ALU.add), s["zfix_ready"], 1)
            link(dve, "seam", dve.memset(m_all[:, 0:1], FAR))

            dve.wait_ge(s["tail_in"], 16)

            def turn2(k, r):
                u = (U - 1) - k
                a = bass.ds(u * T, T)
                base = k * (T + 1)
                wait(dve, s[f"z_back{r}"], dma_uses(k, r), s["dve_went_on"])
                if known(k, 2):
                    wait(dve, s[f"zd_saved{r}"], dma_uses(k - 2, r), s["dve_went_on"])
                dve.tensor_tensor(ZB[:, r, :, :], ZL[:, r, :, :], bc(lastm[:, a], D), ALU.mult
                                  ).then_inc(s["back_step"], 1)
                for n, t in enumerate(reversed(range(T))):
                    prev = ZB[:, r, t + 1, :] if t + 1 < T else (ZB[:, 1 - r, 0, :] if known(k, 1) else tailc[:, :])
                    wait(dve, s["back_step"], base + n + 1, s["dve_went_on"])
                    ins = dve.scalar_tensor_tensor(out=ZB[:, r, t, :], in0=prev,
                                                   scalar=notlast[:, bass.ds(u * T + t, 1)], in1=ZB[:, r, t, :],
                                                   op0=ALU.mult, op1=ALU.add).then_inc(s["back_step"], 1)
                wait(dve, s["back_step"], base + T + 1, s["dve_went_on"])
                dve.sem_inc(s["zd_ready"], 1)

            turns(dve, 0, 3, U, turn2)

            def turn3(k, r):
                n = k + U
                dve.wait_ge(s[f"dst2_in{r}"], dma_uses(k, r, 48))
                weave(softmax_logits(dve, k, r, n))

                def before_state():
                    if known(k, 2):
                        dve.wait_ge(s[f"state2_saved{r}"], dma_uses(k - 2, r))

                weave(aggregate(dve, k, r, n, ZS[:, r, :, :], ZD[:, r, :, :], False, before_state))
                dve.tensor_tensor(tmpf[:, 0, :, :], tmpf[:, 0, :, :], tmpf[:, 1, :, :], ALU.add
                                  ).then_inc(s["mean2_ready"], 1)
                dve.wait_ge(s["mean2_ready"], k + 1)
                if known(k, 2):
                    dve.wait_ge(s[f"out_scattered{r}"], scattered(k - 2, r))
                dve.tensor_tensor(OE[:, r, :, :], tmpf[:, 0, :, :], XR[:, r, :, :], ALU.add
                                  ).then_inc(s["agg2_done"], 1)

            turns(dve, 0, 3, U, turn3)
            seam(1, 0)
            dve.tensor_tensor(zfix[:, :], fixv[:, 1, :], xh[:, :], ALU.add).then_inc(s["outfix_ready"], 1)

        @block.scalar
        def _(act):
            def exps(k, q, n):
                act.wait_ge(s["soft_step"], n * SM_STEPS + SM_STEPS)
                act.activation(EX[:, q, :], DX[:, q, :], ACT.Exp).then_inc(s["exps_ready"], 1)
                act.wait_ge(s["exps_ready"], n + 1)
                if known(n, 1):
                    act.wait_ge(s["agg_step"], (n - 1) * AG_STEPS + 5)
                act.activation(RM[:, 0:D, 1:T], EX[:, q, 1:T].unsqueeze(1).to_broadcast([P, D, T - 1]),
                               ACT.Copy).then_inc(s["decay_ready"], 1)

            def leaky_rows(n, layer, done_m, done_s):
                for i, (ps_i, made) in enumerate(((pM, "rows_m"), (pS, "rows_s"))):
                    act.wait_ge(s[made], n + 1)
                    if known(n, 1):
                        act.wait_ge(s["logits_ready"], n)
                    act.activation(mz[:, 2 * i, :], ps_i[:, :], ACT.Relu, bias=zb[:, layer:layer + 1])
                    act.activation(mz[:, 2 * i + 1, :], ps_i[:, :], ACT.Identity, bias=zb[:, layer:layer + 1]
                                   ).then_inc(s[(done_m, done_s)[i]], 1)

            def mask(k):
                if known(k, 1):
                    act.wait_ge(s["attr_step"], (k - 1) * AT_STEPS + 3)
                act.activation(RM[:, D:W, 1:T],
                               same[:, bass.ds(k * T + 1, T - 1)].unsqueeze(1).to_broadcast([P, DE, T - 1]),
                               ACT.Copy).then_inc(s["mask_spread"], 1)

            def dense_rows(k, r, r4, b):
                if b == 0:
                    act.wait_ge(s["stats_step"], k * LN_STEPS + LN_STEPS)
                    if known(k, 2):
                        act.wait_ge(s["dense1_turned"], k - 1)
                for t in range(b * T, (b + 1) * T):
                    c = slice(2 * T + t, 2 * T + t + 1)
                    last = act.activation(HD[:, r, t, :], XD[:, r4, t, :], ACT.Relu,
                                          bias=nmr[:, r, c], scale=rstd[:, r, c])
                last.then_inc(s["dense0_normed" if b == 0 else "dense_normed"], 1)

            def first_part(k, r, r4):
                dense_rows(k, r, r4, 0)
                for b, nm in enumerate(("hs", "hd")):
                    act.wait_ge(s[f"{nm}_turned"], k + 1)
                    if known(k, 1):
                        act.wait_ge(s["rows_s"], k)
                    act.activation(hts[:, b, :], pT[b][:, :], ACT.Relu).then_inc(s[f"{nm}_out"], 1)

            def second_part(k, r, r4):
                act.wait_ge(s["ea_turned"], k + 1)
                if known(k, 2):
                    act.wait_ge(s[f"el_saved{r}"], dma_uses(k - 2, r))
                    act.wait_ge(s["rows_s"], k - 1)
                act.activation(EL[:, r, :], pT[0][:, :], ACT.Copy).then_inc(s["el_ready"], 1)
                if not isinstance(k, int) or k + 1 < U:
                    mask(k + 1)
                dense_rows(k, r, r4, 1)

            def z_dense_out(k, r):
                act.wait_ge(s["z_dense_made"], k + 1)
                if known(k, 2):
                    act.wait_ge(s[f"z_dense_saved{r}"], dma_uses(k - 2, r, 32))
                    act.wait_ge(s["out_dense_done"], k - 1)
                act.activation(TD[:, r, :, :].rearrange("p b f -> p (b f)"), pY[:, :, :].rearrange("p b f -> p (b f)"),
                               ACT.Copy).then_inc(s["z_dense_ready"], 1)

            def third_part(k, r):
                leaky_rows(k, 0, "mz_m", "mz_s")
                for b in range(2):
                    act.wait_ge(s[f"dense{b}_turned"], k + 1)
                    if known(k, 1):
                        act.wait_ge(s["z_dense_made"], k)
                    act.activation(htd[:, b, :], pT[1 - b][:, :], ACT.Copy).then_inc(s[f"dense{b}_out"], 1)

            def edges_out(k, r):
                act.wait_ge(s["h1_turned"], k + 1)
                if known(k, 1):
                    act.wait_ge(s["z_edge_made"], k)
                act.activation(h1t[:, :], pT[1][:, :], ACT.Copy).then_inc(s["h1t_ready"], 1)
                act.wait_ge(s["z_edge_made"], k + 1)
                if known(k, 2):
                    act.wait_ge(s[f"z_edge_saved{r}"], dma_uses(k - 2, r))
                act.activation(ZE[:, r, :], pZ[:, :], ACT.Copy).then_inc(s["z_edge_ready"], 1)

            act.wait_ge(s["consts_ready"], 1)
            mask(0)

            def turn(k, r4):
                r = r4 % 2
                late = isinstance(k, int) and k >= U
                before = known(k, 1) and not (late and k - 1 >= U)
                if not late:
                    first_part(k, r, r4)
                if before:
                    exps(k - 1, 1 - r, k - 1)
                if not late:
                    second_part(k, r, r4)
                if before:
                    z_dense_out(k - 1, 1 - r)
                if not late:
                    third_part(k, r)
                if known(k, 2):
                    edges_out(k - 2, r)

            turns(act, 0, 4, U - 1, turn, 4)
            for k in range(U - 1, U + 2):
                turn(k, k % 4)

            def seam(layer):
                act.wait_ge(s["row_exps_asked"], layer + 1)
                act.activation(row[:, 7:9, 0:P], row[:, 5:7, 0:P], ACT.Exp).then_inc(s["row_exps"], 1)
                act.wait_ge(s["seam_exps_asked"], 2 * layer + 1)
                act.activation(sm[:, 19:21], sm[:, 17:19], ACT.Exp).then_inc(s["seam_exps"], 1)
                act.wait_ge(s["node_turned"], layer + 1)
                if layer == 0:
                    act.activation(lpt[:, :], pT[0][0:DE, P:2 * P], ACT.Copy)
                act.activation(hht[0:D, :], pT[0][0:D, 0:P], ACT.Copy).then_inc(s["node_out"], 1)
                act.wait_ge(s["loop_rows"], layer + 1)
                act.activation(srz[:, 0, :], pM[0:D, 0:P], ACT.Relu, bias=zb[0:D, layer:layer + 1])
                act.activation(srz[:, 1, :], pM[0:D, 0:P], ACT.Identity, bias=zb[0:D, layer:layer + 1]
                               ).then_inc(s["loop_leaky"], 1)
                act.wait_ge(s["seam_exps_asked"], 2 * layer + 2)
                act.activation(sm[:, 19:21], sm[:, 17:19], ACT.Exp).then_inc(s["seam_exps"], 1)

            seam(0)
            act.wait_ge(s["fix_turned"], 1)
            act.activation(fixt[:, :], pT[0][0:D, 0:P], ACT.Copy).then_inc(s["fixt_ready"], 1)

            def turn3(k, r):
                n = k + U
                leaky_rows(n, 1, "mz_m", "mz_s")
                exps(k, r, n)

            turns(act, 0, 1, U, turn3)
            seam(1)

        @block.tensor
        def _(pe):
            def turned(to, tile, signal):
                for j in range(F // P):
                    last = pe.transpose(to[:, j * P:(j + 1) * P], tile[:, j * P:(j + 1) * P], ident[:, :])
                last.then_inc(signal, 1)

            def flat(ap):
                return ap.rearrange("p t d -> p (t d)")

            def logits(n, q, layer):
                for i, ready in enumerate(("mz_m", "mz_s")):
                    pe.wait_ge(s[ready], n + 1)
                    if i == 0 and known(n, 1):
                        pe.wait_ge(s["soft_step"], (n - 1) * SM_STEPS + SM_STEPS)
                    for j in range(T // 2):
                        c = q * 2 * T + i * T + 2 * j
                        for h in range(2):
                            last = pe.matmul(pL[:, c:c + 2], mz[:, 2 * i + h, j * P:(j + 1) * P], attr[:, layer, h, :],
                                             start=(h == 0), stop=(h == 1))
                last.then_inc(s["logits_ready"], 1)

            pe.wait_ge(s["weights_made"], 1)
            pe.transpose(pT[0][:, 0:P], w1d[:, :], ident[:, :]).then_inc(s["w1_turned"], 1)
            pe.wait_ge(s["w1t_ready"], 1)
            pe.matmul(pS[:, 0:D], vrep[0:D, :], w2d[0:D, 0:D], start=True, stop=True)
            pe.matmul(pT[1][:, 0:P], w1t[:, :], w2d[:, :], start=True, stop=True).then_inc(s["w12_made"], 1)
            pe.wait_ge(s["consts_ready"], 1)

            def z_dense(k, b):
                if b == 0 and known(k, 1):
                    pe.wait_ge(s["z_dense_ready"], k)
                pe.wait_ge(s[f"dense{b}_out"], k + 1)
                for j in range(T // 2):
                    pe.matmul(pY[:, b, j * P:(j + 1) * P], htd[:, b, j * P:(j + 1) * P], w12[:, :],
                              start=(j == 0), stop=True, skip_group_check=True)
                last = pe.matmul(pY[:, b, :], ones_h[:, :], cb3[:, :], start=False, stop=True, skip_group_check=True)
                if b == 1:
                    last.then_inc(s["z_dense_made"], 1)

            def turn_src(k, r):
                pe.wait_ge(s["edges_step"], k * 4 + 2)
                if known(k, 1):
                    pe.wait_ge(s["dense1_out"], k)
                turned(pT[0], flat(H[:, r, 0:T, :]), s["hs_turned"])

            def turn_dst(k, r):
                pe.wait_ge(s["edges_step"], k * 4 + 4)
                if known(k, 3):
                    pe.wait_ge(s["h1t_ready"], k - 2)
                elif known(k, 1):
                    pe.wait_ge(s["dense0_out"], k)
                turned(pT[1], flat(H[:, r, T:2 * T, :]), s["hd_turned"])
                pe.wait_ge(s["attr_step"], k * AT_STEPS + AT_STEPS)
                pe.wait_ge(s["hs_out"], k + 1)
                for i, tile in enumerate((EA, LA)):
                    tile = flat(tile[:, r, :, :])
                    for j in range(2):
                        last = pe.transpose(pT[0][:, (2 * i + j) * P:(2 * i + j + 1) * P],
                                            tile[:, j * P:(j + 1) * P], ident[:, :])
                last.then_inc(s["ea_turned"], 1)

            def logit_rows(k, r):
                pe.wait_ge(s["hd_out"], k + 1)
                if known(k, 1):
                    pe.wait_ge(s["mz_m"], k)
                pe.matmul(pM[:, :], w1d[:, :], hts[:, 0, :], start=True, stop=False)
                pe.matmul(pM[:, :], w1d[:, :], hts[:, 1, :], start=False, stop=True)
                pe.wait_ge(s["el_ready"], k + 1)
                for j in range(T // 2):
                    last = pe.matmul(pM[:, j * P:(j + 1) * P], we[:, 0, j % 2, :],
                                     EL[:, r, j // 2 * P:(j // 2 + 1) * P], start=False, stop=True,
                                     skip_group_check=True)
                last.then_inc(s["rows_m"], 1)
                if known(k, 1):
                    pe.wait_ge(s["mz_s"], k)
                pe.matmul(pS[:, :], w1d2[:, :], hts[:, 1, :], start=True, stop=True)
                for j in range(T // 2):
                    last = pe.matmul(pS[:, j * P:(j + 1) * P], we[:, 0, j % 2, :],
                                     EL[:, r, (2 + j // 2) * P:(3 + j // 2) * P], start=False,
                                     stop=True, skip_group_check=True)
                last.then_inc(s["rows_s"], 1)

            def turn_edges(k, r, dense_ahead):
                pe.wait_ge(s["h1_ready"], k + 1)
                if dense_ahead:
                    pe.wait_ge(s["dense0_out"], k + 3)
                elif k == U - 1:
                    pe.wait_ge(s["h1t_ready"], k)
                turned(pT[1], flat(H1[:, r, :, :]), s["h1_turned"])

            def z_edges(k):
                pe.wait_ge(s["h1t_ready"], k + 1)
                if known(k, 1):
                    pe.wait_ge(s["z_edge_ready"], k)
                for j in range(T // 2):
                    pe.matmul(pZ[:, j * P:(j + 1) * P], h1t[:, j * P:(j + 1) * P], w12[:, :],
                              start=(j == 0), stop=True, skip_group_check=True)
                last = pe.matmul(pZ[:, :], ones_h[:, :], cb3[:, :], start=False, stop=True, skip_group_check=True)
                last.then_inc(s["z_edge_made"], 1)

            def turn(k, r):
                late = isinstance(k, int) and k >= U
                before = known(k, 1) and not (late and k - 1 >= U)
                if not late:
                    turn_src(k, r)
                if before:
                    z_dense(k - 1, 0)
                if not late:
                    turn_dst(k, r)
                if before:
                    z_dense(k - 1, 1)
                if not late:
                    logit_rows(k, r)
                    pe.wait_ge(s["dense0_normed"], k + 1)
                    turned(pT[1], flat(HD[:, r, 0:T, :]), s["dense0_turned"])
                    logits(k, r, 0)
                    pe.wait_ge(s["dense_normed"], k + 1)
                    turned(pT[0], flat(HD[:, r, T:2 * T, :]), s["dense1_turned"])
                if known(k, 2):
                    turn_edges(k - 2, r, not late)
                    z_edges(k - 2)

            turns(pe, 0, 4, U - 1, turn)
            for k in range(U - 1, U + 2):
                turn(k, k % 2)

            def seam(layer):
                pe.wait_ge(s["tails_ready"], layer + 1)
                for i, c in enumerate((14, 11, 10)):
                    last = pe.transpose(pS[0:1, i * P:(i + 1) * P], sm[:, c:c + 1], ident[:, :])
                last.then_inc(s["rows_turned"], 1)
                pe.transpose(pT[0][0:W + 2, 0:P], TS[:, :], ident[:, :]).then_inc(s["tails_turned"], 1)
                pe.wait_ge(s["row_exps"], layer + 1)
                pe.matmul(pM[:, 0:P], sel[:, 0, :], row[:, 7, 0:P], start=True, stop=False)
                pe.matmul(pM[:, 0:P], sel[:, 1, :], ones[0:1, :], start=False, stop=True)
                pe.matmul(pM[:, P:2 * P], sel[:, 0, :], row[:, 8, 0:P], start=True, stop=False)
                pe.matmul(pM[:, P:2 * P], sel[:, 1, :], row[:, 4, 0:P], start=False, stop=True
                          ).then_inc(s["decay_spread"], 1)
                pe.wait_ge(s["carries_made"], layer + 1)
                pe.transpose(pT[1][:, 0:W + 2], OT[0:W + 2, 0:P], ident[0:W + 2, 0:W + 2])
                pe.transpose(pS[:, 3 * P:3 * P + 1], row[:, 1, 0:P], ident[0:1, 0:1]).then_inc(s["carries_turned"], 1)
                pe.wait_ge(s["node_ready"], layer + 1)
                node = hh if layer == 0 else zh
                if layer == 0:
                    pe.transpose(pT[0][0:DE, P:2 * P], loopm[:, :], ident[:, :])
                pe.transpose(pT[0][0:D, 0:P], node[:, :], ident[:, :]).then_inc(s["node_turned"], 1)
                pe.wait_ge(s["node_out"], layer + 1)
                wn = w1d2 if layer == 0 else ident2
                pe.matmul(pM[0:D, 0:P], wn[0:D, 0:D], hht[0:D, :], start=True, stop=False)
                pe.matmul(pM[0:D, 0:P], we[0:DE, layer, 0, 0:D], lpt[:, :], start=False, stop=True
                          ).then_inc(s["loop_rows"], 1)
                pe.wait_ge(s["loop_leaky"], layer + 1)
                for h in range(2):
                    last = pe.matmul(pL[:, 4 * T:4 * T + 1], srz[:, h, :], attr[0:D, layer, h, 0:1],
                                     start=(h == 0), stop=(h == 1))
                last.then_inc(s["loop_logit"], 1)

            seam(0)
            pe.wait_ge(s["fixv_ready"], 1)
            pe.transpose(pT[0][0:D, 0:P], fixv[:, 1, :], ident[:, :]).then_inc(s["fix_turned"], 1)
            pe.wait_ge(s["fixt_ready"], 1)
            pe.matmul(pM[:, 0:D], fixt[:, :], w12[0:D, 0:D], start=True, stop=True).then_inc(s["zfix_made"], 1)
            pe.wait_ge(s["zfix_ready"], 1)

            def turn3(k, r):
                n = k + U
                pe.wait_ge(s[f"src2_in{r}"], scattered(k, r))
                pe.wait_ge(s[f"dst2_in{r}"], dma_uses(k, r, 48))
                pe.wait_ge(s["mz_m"], n)
                zs, zd = flat(ZS[:, r, :, :]), flat(ZD[:, r, :, :])
                for j in range(T // 2):
                    c = slice(j * P, (j + 1) * P)
                    pe.matmul(pM[:, c], zs[:, c], ident[:, :], start=True, stop=False)
                    pe.matmul(pM[:, c], zd[:, c], ident[:, :], start=False, stop=False)
                    last = pe.matmul(pM[:, c], we[:, 1, j % 2, :], EL[:, r, j // 2 * P:(j // 2 + 1) * P],
                                     start=False, stop=True)
                last.then_inc(s["rows_m"], 1)
                pe.wait_ge(s["mz_s"], n)
                for j in range(T // 2):
                    c = slice(j * P, (j + 1) * P)
                    pe.matmul(pS[:, c], zd[:, c], ident2[:, :], start=True, stop=False)
                    last = pe.matmul(pS[:, c], we[:, 1, j % 2, :], EL[:, r, (2 + j // 2) * P:(3 + j // 2) * P],
                                     start=False, stop=True)
                last.then_inc(s["rows_s"], 1)
                pe.wait_ge(s["rows_s"], n + 1)
                pe.nop().then_inc(s["rows2_done"], 1)
                logits(n, r, 1)

            turns(pe, 0, 3, U, turn3)
            seam(1)


_INS = ["x", "src", "dst", "edge_attr_32"] + [f"L0_gnn_{n}" for n in
        ("W1", "b1", "We1", "att1", "bias1", "W2", "b2", "We2", "att2", "bias2")]


def kernel(**inputs):
    import numpy as np
    import concourse.bacc as bacc
    from concourse.bass_utils import run_bass_kernel_spmd

    nc = bacc.Bacc("TRN2", target_bir_lowering=False, num_devices=1)
    arrays, args = {}, []
    for name in _INS:
        a = np.ascontiguousarray(inputs[name])
        arrays[f"in_{name}"] = a
        args.append(nc.dram_tensor(f"in_{name}", a.shape, mybir.dt.from_np(a.dtype), kind="ExternalInput").ap())
    out = nc.dram_tensor("out_0", tuple(inputs["x"].shape), F32, kind="ExternalOutput").ap()
    gnn_kernel(nc, *args, out)
    r = run_bass_kernel_spmd(nc, [arrays], core_ids=[0])
    return r.results[0]["out_0"]
```

```python
from contextlib import ExitStack
from itertools import chain

import concourse.bass as bass
from concourse import mybir

F32 = mybir.dt.float32
I32 = mybir.dt.int32
BF16 = mybir.dt.bfloat16
ALU = mybir.AluOpType
ACT = mybir.ActivationFunctionType
AX_X = mybir.AxisListType.X

P = 128
T = 8
D = 64
DE = 32
W = D + DE
NEG_SLOPE = 0.2
EPS = 1e-5
FAR = -1e30
SKIP = 200000.0
RSQRT_MAGIC = float(0x5F3759DF)
LN_STEPS = 19
SM_STEPS = 7
AG_STEPS = 11
AT_STEPS = 4


def gnn_kernel(nc, x, src, dst, ea, W1, b1, We1, att1, bias1, W2, b2, We2, att2, bias2, out):
    N = x.shape[0]
    E = src.shape[0]
    C = -(-E // (P * T)) * T
    U = C // T
    EP = P * C
    ROWS = E - (P - 1) * C
    DB = P * T
    NDB = -(-N // DB)
    TAILP = (N - (NDB - 1) * DB) // T
    assert 0 < ROWS <= C and NDB == 2 * U and (N - (NDB - 1) * DB) % T == 0 and U % 2 == 1
    AHEAD = 4
    assert AHEAD == 4
    F = T * D

    ea_pad = nc.dram_tensor("ea_pad", (EP, DE), F32, kind="Internal").ap()
    z_tab = nc.dram_tensor("z_tab", (N, D), F32, kind="Internal").ap()
    st_all = nc.dram_tensor("st_all", (U * P, W * T), F32, kind="Internal").ap()
    xd_all = nc.dram_tensor("xd_all", (U * P, F), F32, kind="Internal").ap()
    el_all = nc.dram_tensor("el_all", (U * P, F), F32, kind="Internal").ap()
    z_all = nc.dram_tensor("z_all", (U * P * T, D), F32, kind="Internal").ap()
    zd_all = nc.dram_tensor("zd_all", (U * P, F), F32, kind="Internal").ap()
    dst_pad = nc.dram_tensor("dst_pad", (1, EP), I32, kind="Internal").ap()
    ends_sorted = nc.dram_tensor("ends_sorted", (EP, 2), I32, kind="Internal").ap()
    ea_sorted = nc.dram_tensor("ea_sorted", (EP, DE), F32, kind="Internal").ap()
    z_blk = z_all.rearrange("(u p t) d -> (u p) (t d)", p=P, t=T)
    ea_cols = ea_pad.rearrange("(p c) f -> p (c f)", p=P)

    with ExitStack() as ctx:
        def sb(name, shape, dt=F32):
            return ctx.enter_context(nc.sbuf_tensor(name, shape, dt))

        def ps(name, shape):
            return ctx.enter_context(nc.psum_tensor(name, shape, F32))

        def sem(name):
            return ctx.enter_context(nc.semaphore(name))

        src_i = sb("src_i", [P, C], I32)
        dst_i = sb("dst_i", [P, C], I32)
        gat_i = sb("gat_i", [P, U, 2, T], I32)
        sca_i = sb("sca_i", [P, C], I32)
        dext = sb("dext", [P, C + 2])
        edge_i = sb("edge_i", [P, 2], I32)
        same = sb("same", [P, C + 1])
        lastm = sb("lastm", [P, C])
        notlast = sb("notlast", [P, C])
        far = sb("far", [P, C])
        rcnt = sb("rcnt", [P, C])
        cnt = sb("cnt", [P, C])
        hend = sb("hend", [P, C])
        eq0 = sb("eq0", [P, C])
        tmpc = sb("tmpc", [P, C])
        tmpd = sb("tmpd", [P, C])
        iota_c = sb("iota_c", [P, C])
        iota_p = sb("iota_p", [P, 1])
        m_all = sb("m_all", [P, C + 1])
        den_all = sb("den_all", [P, C + 1])
        gidx = sb("gidx", [P, 2, 2 * T], I32)
        sidx = sb("sidx", [P, 4, T], I32)

        unsorted = sb("unsorted", [P, 1])
        flag = sb("flag", [1, 1], I32)
        other_i = sb("other_i", [P, C], I32)
        other = sb("other", [P, C])
        place = sb("place", [P, C])
        rank = sb("rank", [P, C])
        lowers = sb("lowers", [P, T])
        ends = sb("ends", [P, T, 2], I32)

        ident = sb("ident", [P, P])
        ident2 = sb("ident2", [P, P])
        w1d = sb("w1d", [P, P])
        w1d2 = sb("w1d2", [P, P])
        w1t = sb("w1t", [P, P])
        w2d = sb("w2d", [P, P])
        w12 = sb("w12", [P, P])
        we = sb("we", [P, 2, 2, P])
        attp = sb("attp", [P, 2, 2])
        attr = sb("attr", [P, 2, 2, 2])
        vecs = sb("vecs", [P, 4])
        vsum = sb("vsum", [P, 1])
        vrep = sb("vrep", [P, P])
        zb = sb("zb", [P, 2])
        rows = sb("rows", [P, 2, D])
        cb = sb("cb", [P, D])
        ones = sb("ones", [P, P])
        ones_h = sb("ones_h", [P, P], BF16)
        cb3 = sb("cb3", [P, F], BF16)
        part = sb("part", [P, 3, D], BF16)
        rest = sb("rest", [P, 3, D])
        third = sb("third", [P, 3])

        X = sb("X", [P, 2, 2 * T, D])
        XD = sb("XD", [P, 4, 2 * T, D])
        H = sb("H", [P, 2, 2 * T, D])
        HD = sb("HD", [P, 2, 2 * T, D])
        EA = sb("EA", [P, 2, T, DE])
        LA = sb("LA", [P, 2, T, DE])
        ST = sb("ST", [P, 2, W, T])
        H1 = sb("H1", [P, 2, T, D])
        ZE = sb("ZE", [P, 2, F])
        TD = sb("TD", [P, 2, 2, F])
        OD = sb("OD", [P, 2, 2 * T, D])
        EL = sb("EL", [P, 2, F])
        DX = sb("DX", [P, 2, 4 * T])
        EX = sb("EX", [P, 2, 4 * T])
        stats = sb("stats", [P, 4 * T, 6])
        lnb = sb("lnb", [P, 8, 4 * T])
        meanb = sb("meanb", [P, 2, 4 * T])
        mx8 = sb("mx8", [P, T])
        rstd = sb("rstd", [P, 2, 4 * T])
        nmr = sb("nmr", [P, 2, 4 * T])
        htd = sb("htd", [P, 2, F])
        hts = sb("hts", [P, 2, F])
        mz = sb("mz", [P, 4, F])
        V = sb("V", [P, W, T])
        RM = sb("RM", [P, W, T])
        h1t = sb("h1t", [P, F])
        tmpf = sb("tmpf", [P, 2, T, D])
        fin = sb("fin", [P, 4, T])

        pT = [ps(f"pT{i}", [P, F]) for i in range(2)]
        pM = ps("pM", [P, F])
        pS = ps("pS", [P, F])
        pY = ps("pY", [P, 2, F])
        pZ = ps("pZ", [P, F])
        pL = ps("pL", [P, F])

        earlier, lower = (tile.rearrange("p a b d -> p (a b d)")[:, 0:T * C].rearrange("p (t c) -> p t c", t=T)
                          for tile in (H[:, :, :, :].bitcast(BF16), XD[:, :, :, :]))

        HB = sb("HB", [P, W * T])
        HS = sb("HS", [P, W + 2])
        TS = sb("TS", [P, W + 2])
        sm = sb("sm", [P, 24])
        smi = sb("smi", [P, 6], I32)
        mask8 = sb("mask8", [P, T])
        xh = sb("xh", [P, D])
        hh = sb("hh", [P, D])
        zh = sb("zh", [P, D])
        row = sb("row", [1, 12, P + 1])
        sel = sb("sel", [1, 2, P])
        OT = sb("OT", [P, P + 1])
        QT = sb("QT", [P, P])
        CS = sb("CS", [P, P])
        loopm = sb("loopm", [P, DE])
        hht = sb("hht", [P, P])
        lpt = sb("lpt", [DE, P])
        srz = sb("srz", [D, 2, P])
        fixv = sb("fixv", [P, 2, D])
        fixt = sb("fixt", [D, P])
        zfix = sb("zfix", [P, D])
        tailc = sb("tailc", [P, D])

        ZD = sb("ZD", [P, 2, T, D])
        XR = sb("XR", [P, 2, T, D])
        ZB = sb("ZB", [P, 2, T, D])

        ZS = [X[:, i // 2, i % 2 * T:(i % 2 + 1) * T, :] for i in range(4)]
        ZL = [H[:, i // 2, i % 2 * T:(i % 2 + 1) * T, :] for i in range(4)]
        ZT = [HD[:, i // 2, i % 2 * T:(i % 2 + 1) * T, :] for i in range(4)]
        OE = [HD[:, i // 2, i % 2 * T:(i % 2 + 1) * T, :] for i in range(4)]
        gidx4 = [gidx[:, i // 2, i % 2 * T:(i % 2 + 1) * T] for i in range(4)]

        names = {}

        class Sems:

            def __getitem__(self, name):
                if name not in names:
                    names[name] = sem(name)
                return names[name]

        s = Sems()

        def turns(eng, first, peeled, end, body, by=2):
            for t in range(first, first + peeled):
                body(t, t % by)
            t0 = first + peeled
            rounds = (end - t0) // by
            with eng.Fori(0, rounds) as i:
                for t in range(t0, t0 + by):
                    body(i * by + t, t % by)
            for t in range(t0 + by * rounds, end):
                body(t, t % by)

        def known(k, n):
            return not isinstance(k, int) or k >= n

        def gathered(k, r):
            return (k - r) // 2 * (32 * T) + 32 * T if isinstance(k, int) else (k - r) * (16 * T) + 32 * T

        def dma_uses(k, r, n=16, ring=2):
            return (k - r) // ring * n + n if isinstance(k, int) else (k - r) * (n // ring) + n

        def by_four(k, r):
            return dma_uses(k, r, 16 * T, 4)

        def wait(eng, signal, value, went_on):
            eng.wait_ge(signal, value)
            if not isinstance(value, int):
                eng.sem_inc(went_on, 1)

        block = ctx.enter_context(nc.Block())

        @block.sync
        def _(sp):
            wait(sp, s["pads_set"], 1, s["sp_went_on"])
            full = (P - 1) * C
            sp.dma_start(src_i[0:P - 1, :], src[0:full].rearrange("(p c) -> p c", c=C)).then_inc(s["idx_in"], 16)
            sp.dma_start(src_i[P - 1:P, 0:ROWS], src[full:E].rearrange("(p c) -> p c", p=1)).then_inc(s["idx_in"], 16)
            sp.dma_start(dst_i[0:P - 1, :], dst[0:full].rearrange("(p c) -> p c", c=C)).then_inc(s["idx_in"], 16)
            sp.dma_start(dst_i[P - 1:P, 0:ROWS], dst[full:E].rearrange("(p c) -> p c", p=1)).then_inc(s["idx_in"], 16)
            sp.dma_start(edge_i[1:P, 0:1], dst[0:full].rearrange("(p c) -> p c", c=C)[:, C - 1:C],
                         allow_slow_non_contiguous=True).then_inc(s["idx_in"], 16)
            sp.dma_start(edge_i[0:P - 2, 1:2], dst[C:full].rearrange("(p c) -> p c", c=C)[:, 0:1],
                         allow_slow_non_contiguous=True).then_inc(s["idx_in"], 16)
            sp.dma_start(edge_i[P - 2:P - 1, 1:2], dst[full:full + 1].rearrange("(p c) -> p c", p=1)).then_inc(s["idx_in"], 16)

            wait(sp, s["tiles_zeroed"], 1, s["sp_went_on"])
            sp.dma_start(ea_pad[0:E, :].rearrange("(a b) f -> a (b f)", a=16),
                         ea.rearrange("(a b) f -> a (b f)", a=16)).then_inc(s["ea_padded"], 16)
            padr = EP - E
            sp.dma_start(ea_pad[E:EP, :].rearrange("(a b) f -> a (b f)", a=16),
                         ZB[0:16, 0, :, :].rearrange("p t d -> p (t d)")[:, 0:padr // 16 * DE]).then_inc(s["ea_padded"], 16)

            for g in range(2):
                q = slice(g * D, (g + 1) * D)
                sp.dma_start(w1d[q, q], W1).then_inc(s["weights_in"], 16)
                sp.dma_start(w2d[q, q], W2).then_inc(s["weights_in"], 16)
                for l, (we_l, att_l) in enumerate(((We1, att1), (We2, att2))):
                    sp.dma_start(attp[q, l, g:g + 1], att_l.rearrange("(p c) -> p c", c=1)).then_inc(s["weights_in"], 16)
                    for v in range(2):
                        q2 = slice(v * D + g * DE, v * D + (g + 1) * DE)
                        sp.dma_start(we[q2, l, v, q], we_l).then_inc(s["weights_in"], 16)
                for c, v in enumerate((b1, bias1, bias2)):
                    sp.dma_start(vecs[q, c:c + 1], v.rearrange("(p c) -> p c", c=1)).then_inc(s["weights_in"], 16)
            for c, v in enumerate((b2, bias2)):
                sp.dma_start(rows[:, c, :], v.rearrange("(p c) -> p c", p=1).to_broadcast([P, D])).then_inc(s["weights_in"], 16)

            wait(sp, s["flag_ready"], 1, s["sp_went_on"])
            with sp.If(sp.value_load(flag[0:1, 0:1]) > 0):
                sp.dma_start(dst_pad.rearrange("o (p c) -> (o p) c", p=P), dst_i[:, :]).then_inc(s["dst_padded"], 16)
                wait(sp, s["dst_padded"], 16, s["sp_went_on"])
                with sp.Fori(0, P) as i:
                    wait(sp, s["other_free"], i + 1, s["sp_went_on"])
                    sp.dma_start(other_i[:, :], dst_pad[:, bass.ds(i * C, C)].to_broadcast([P, C])
                                 ).then_inc(s["other_in"], 16)
                wait(sp, s["ea_padded"], 32, s["sp_went_on"])
                with sp.Fori(0, U) as u:
                    wait(sp, s["sort_slot_free"], u + 1, s["sp_went_on"])
                    sp.dma_start(EA[:, 0, :, :].rearrange("p t f -> p (t f)"),
                                 ea_cols[:, bass.ds(u * (T * DE), T * DE)]).then_inc(s["sort_ea_in"], 16)
                wait(sp, s["sort_slot_free"], U + 1, s["sp_went_on"])
                for c, tile in enumerate((src_i, dst_i)):
                    sp.dma_start(tile[:, :], ends_sorted[:, c:c + 1].rearrange("(p c) o -> p (c o)", p=P),
                                 allow_slow_non_contiguous=True).then_inc(s["sorted_in"], 16)
                first = ends_sorted[:, 1:2].rearrange("(p c) o -> p (c o)", p=P)
                sp.dma_start(edge_i[1:P, 0:1], first[0:P - 1, C - 1:C],
                             allow_slow_non_contiguous=True).then_inc(s["sorted_in"], 16)
                sp.dma_start(edge_i[0:P - 1, 1:2], first[1:P, 0:1],
                             allow_slow_non_contiguous=True).then_inc(s["sorted_in"], 16)
                sp.dma_start(ea_pad.rearrange("(a b) f -> a (b f)", a=16),
                             ea_sorted.rearrange("(a b) f -> a (b f)", a=16)).then_inc(s["sorted_in"], 16)
                wait(sp, s["sorted_in"], 16 * 5, s["sp_went_on"])

            def load_dense(k, r):
                if known(k, 4):
                    wait(sp, s["dense_stats"], k - 3, s["sp_went_on"])
                    wait(sp, s["dense_normed"], k - 3, s["sp_went_on"])
                    wait(sp, s["out_dense_done"], k - 3, s["sp_went_on"])
                n0 = k * (2 * DB)
                if isinstance(k, int) and k == U - 1:
                    sp.dma_start(XD[:, r, 0:T, :], x[n0:n0 + DB, :].rearrange("(p t) d -> p t d", p=P)
                                 ).then_inc(s[f"dense_in{r}"], 16)
                    sp.dma_start(XD[0:TAILP, r, T:2 * T, :], x[n0 + DB:N, :].rearrange("(p t) d -> p t d", p=TAILP)
                                 ).then_inc(s[f"dense_in{r}"], 16)
                else:
                    for b in range(2):
                        sp.dma_start(XD[:, r, b * T:(b + 1) * T, :],
                                     x[bass.ds(n0 + b * DB, DB), :].rearrange("(p t) d -> p t d", p=P)
                                     ).then_inc(s[f"dense_in{r}"], 16)

            def load_edge_features(k, r):
                if not known(k, 2):
                    wait(sp, s["ea_padded"], 32, s["sp_went_on"])
                else:
                    wait(sp, s["ea_turned"], k - 1, s["sp_went_on"])
                    wait(sp, s["attr_step"], (k - 1) * AT_STEPS, s["sp_went_on"])
                sp.dma_start(EA[:, r, :, :].rearrange("p t f -> p (t f)"),
                             ea_cols[:, bass.ds(k * (T * DE), T * DE)]).then_inc(s[f"ea_in{r}"], 16)

            def store_z_dense(k, r):
                wait(sp, s["z_dense_ready"], k + 1, s["sp_went_on"])
                n0 = k * (2 * DB)
                for b in range(2):
                    if isinstance(k, int) and k == U - 1 and b == 1:
                        sp.dma_start(z_tab[n0 + DB:N, :].rearrange("(p t) d -> p (t d)", p=TAILP),
                                     TD[0:TAILP, r, b, :]).then_inc(s[f"z_dense_saved{r}"], 16)
                    else:
                        sp.dma_start(z_tab[bass.ds(n0 + b * DB, DB), :].rearrange("(p t) d -> p (t d)", p=P),
                                     TD[:, r, b, :]).then_inc(s[f"z_dense_saved{r}"], 16)

            def store_out_dense(k, r):
                wait(sp, s["out_dense_done"], k + 1, s["sp_went_on"])
                n0 = k * (2 * DB)
                for b in range(2):
                    if isinstance(k, int) and k == U - 1 and b == 1:
                        sp.dma_start(out[n0 + DB:N, :].rearrange("(p t) d -> p t d", p=TAILP),
                                     OD[0:TAILP, r, T:2 * T, :]).then_inc(s[f"out_dense_saved{r}"], 16)
                    else:
                        sp.dma_start(out[bass.ds(n0 + b * DB, DB), :].rearrange("(p t) d -> p t d", p=P),
                                     OD[:, r, b * T:(b + 1) * T, :]).then_inc(s[f"out_dense_saved{r}"], 16)

            def turn(k, r4):
                r = r4 % 2
                late = isinstance(k, int) and k >= U
                if not late:
                    wait(sp, s[f"gathered{r}"], gathered(k, r), s["sp_went_on"])
                    sp.dma_start(xd_all[bass.ds(k * P, P), :],
                                 X[:, r, T:2 * T, :].rearrange("p t d -> p (t d)")).then_inc(s[f"xd_saved{r}"], 16)
                if known(k, 2) and not (late and k - 2 >= U):
                    wait(sp, s["agg_step"], (k - 2) * AG_STEPS + 6, s["sp_went_on"])
                    sp.dma_start(st_all[bass.ds((k - 2) * P, P), 0:F],
                                 ST[:, r, 0:D, :].rearrange("p f t -> p (f t)")).then_inc(s[f"state_saved{r}"], 16)
                    store_out_dense(k - 2, r)
                if not isinstance(k, int) or k + 1 < U:
                    load_edge_features(k + 1, 1 - r)
                if not isinstance(k, int) or k + 2 < U:
                    load_dense(k + 2, (r4 + 2) % 4)
                if not late:
                    wait(sp, s["attr_step"], k * AT_STEPS + 3, s["sp_went_on"])
                    sp.dma_start(st_all[bass.ds(k * P, P), F:W * T],
                                 ST[:, r, D:W, :].rearrange("p f t -> p (f t)")).then_inc(s[f"sums_saved{r}"], 16)
                if known(k, 3):
                    wait(sp, s["z_edge_ready"], k - 2, s["sp_went_on"])
                    sp.dma_start(z_blk[bass.ds((k - 3) * P, P), :], ZE[:, 1 - r, :]).then_inc(s[f"z_edge_saved{1 - r}"], 16)
                if not late:
                    wait(sp, s["el_ready"], k + 1, s["sp_went_on"])
                    sp.dma_start(el_all[bass.ds(k * P, P), :], EL[:, r, :]).then_inc(s[f"el_saved{r}"], 16)
                if known(k, 1) and not (late and k - 1 >= U):
                    store_z_dense(k - 1, 1 - r)

            load_dense(0, 0)
            load_edge_features(0, 0)
            load_dense(1, 1)
            turns(sp, 0, 4, U - 3, turn, 4)
            for k in range(U - 3, U):
                turn(k, k % 4)
            wait(sp, s["dense1_turned"], U, s["sp_went_on"])
            for n in range(AHEAD):
                wait(sp, s[f"z_edge_saved{n % 2}"], dma_uses(n, n % 2), s["sp_went_on"])
                sp.dma_start(ZT[n], z_blk[n * P:(n + 1) * P, :].rearrange("p (t d) -> p t d", t=T)
                             ).then_inc(s["z_ahead_in"], 16)
            for k in range(U, U + 3):
                turn(k, k % 4)

            wait(sp, s["z_patched"], 16, s["sp_went_on"])

            def turn2(k, r4):
                u = (U - 1) - k
                back = z_blk[bass.ds(u * P, P), :].rearrange("p (t d) -> p t d", t=T)
                if known(k, 4):
                    wait(sp, s[f"z_scattered{r4}"], by_four(k, r4), s["sp_went_on"])
                    wait(sp, s["zd_ready"], k - 3, s["sp_went_on"])
                sp.dma_start(ZL[r4], back).then_inc(s[f"z_back{r4}"], 16)
                if known(k, 1):
                    store_zd(k - 1, (r4 - 1) % 2)

            def store_zd(k, r):
                u = (U - 1) - k
                wait(sp, s["zd_ready"], k + 1, s["sp_went_on"])
                sp.dma_start(zd_all[bass.ds(u * P, P), :],
                             ZB[:, r, :, :].rearrange("p t d -> p (t d)")).then_inc(s[f"zd_saved{r}"], 16)

            turns(sp, 0, 5, U - AHEAD, turn2, 4)
            for i in range(AHEAD):
                u = AHEAD - 1 - i
                sp.dma_start(ZT[i], z_blk[u * P:(u + 1) * P, :].rearrange("p (t d) -> p t d", t=T)
                             ).then_inc(s["z_tail_back"], 16)
            for k in range(U - AHEAD - 1, U):
                store_zd(k, k % 2)

            for r in range(2):
                wait(sp, s[f"zd_saved{r}"], 16 * ((U + 1 - r) // 2), s["sp_went_on"])
                wait(sp, s[f"xd_saved{r}"], 16 * ((U + 1 - r) // 2), s["sp_went_on"])
                wait(sp, s[f"el_saved{r}"], 16 * ((U + 1 - r) // 2), s["sp_went_on"])

            def turn3(k, r):
                if known(k, 2):
                    wait(sp, s["agg2_done"], k - 1, s["sp_went_on"])
                    wait(sp, s["rows2_done"], k - 1, s["sp_went_on"])
                sp.dma_start(ZD[:, r, :, :].rearrange("p t d -> p (t d)"),
                             zd_all[bass.ds(k * P, P), :]).then_inc(s[f"dst2_in{r}"], 16)
                sp.dma_start(XR[:, r, :, :].rearrange("p t d -> p (t d)"),
                             xd_all[bass.ds(k * P, P), :]).then_inc(s[f"dst2_in{r}"], 16)
                sp.dma_start(EL[:, r, :], el_all[bass.ds(k * P, P), :]).then_inc(s[f"dst2_in{r}"], 16)
                if known(k, 1):
                    store_st(k - 1, 1 - r)

            def store_st(k, r):
                wait(sp, s["agg2_done"], k + 1, s["sp_went_on"])
                sp.dma_start(st_all[bass.ds(k * P, P), 0:F],
                             ST[:, r, 0:D, :].rearrange("p f t -> p (f t)")).then_inc(s[f"state2_saved{r}"], 16)

            turns(sp, 0, 3, U, turn3)
            store_st(U - 1, 0)

            for r in range(2):
                wait(sp, s[f"out_dense_saved{r}"], 32 * ((U + 1 - r) // 2), s["sp_went_on"])
                wait(sp, s[f"state2_saved{r}"], 16 * ((U + 1 - r) // 2), s["sp_went_on"])
            wait(sp, s["out_fixed"], 16, s["sp_went_on"])

        @block.gpsimd
        def _(pool):
            pool.memset(ident[:, :], 0.0).then_inc(s["ident_zero"], 1)
            wait(pool, s["ident_zero"], 1, s["pool_went_on"])
            pool.affine_select(out=ident[:, :], in_=ident[:, :], compare_op=ALU.not_equal, fill=1.0, base=0,
                               pattern=[[-1, P]], channel_multiplier=1).then_inc(s["ident_ready"], 1)
            pool.iota(iota_c[:, :], pattern=[[1, C]], base=0, channel_multiplier=0,
                      allow_small_or_imprecise_dtypes=True).then_inc(s["iotas"], 1)
            pool.iota(iota_p[:, :], pattern=[[0, 1]], base=0, channel_multiplier=1,
                      allow_small_or_imprecise_dtypes=True).then_inc(s["iotas"], 1)

            for tile, value in ((ST[:, :, :, :], 0.0), (RM[:, :, :], 0.0), (m_all[:, 0:1], FAR),
                                (den_all[:, 0:1], 0.0), (same[:, C:C + 1], 0.0), (OT[:, :], 0.0),
                                (sel[:, 0, 0:D], 1.0), (sel[:, 0, D:W], 0.0), (sel[:, 0, W:W + 1], 1.0),
                                (sel[:, 0, W + 1:P], 0.0), (sel[:, 1, 0:D], 0.0), (sel[:, 1, D:W], 1.0),
                                (sel[:, 1, W:W + 1], 0.0), (sel[:, 1, W + 1:P], 1.0),
                                (row[:, 1, 1:P + 1], 0.0), (row[:, 1, 0:1], FAR), (row[:, 2:12, :], 0.0)):
                pool.memset(tile, value).then_inc(s["pool_filled"], 1)

            def gather(to, table, index, signal):
                pool.indirect_dma_start(out=to, out_offset=None, in_=table,
                                        in_offset=bass.IndirectOffsetOnAxis(ap=index, axis=0)).then_inc(signal, 16)

            def scatter(table, index, frm, signal, limit):
                pool.indirect_dma_start(out=table, out_offset=bass.IndirectOffsetOnAxis(ap=index, axis=0), in_=frm,
                                        in_offset=None, bounds_check=limit, oob_is_err=False).then_inc(signal, 16)

            wait(pool, s["flag_ready"], 1, s["pool_went_on"])
            with pool.If(pool.value_load(flag[0:1, 0:1]) > 0):
                wait(pool, s["ranked"], 1, s["pool_went_on"])
                pool.sem_inc(s["sort_slot_free"], 1)
                with pool.Fori(0, U) as u:
                    pool.tensor_copy(sidx[:, 0, :], sca_i[:, bass.ds(u * T, T)]).then_inc(s["sort_staged"], 1)
                    pool.tensor_copy(ends[:, :, 0], src_i[:, bass.ds(u * T, T)]).then_inc(s["sort_staged"], 1)
                    pool.tensor_copy(ends[:, :, 1], dst_i[:, bass.ds(u * T, T)]).then_inc(s["sort_staged"], 1)
                    wait(pool, s["sort_staged"], u * 3 + 3, s["pool_went_on"])
                    wait(pool, s["sort_ea_in"], u * 16 + 16, s["pool_went_on"])
                    for t in range(T):
                        scatter(ends_sorted, sidx[:, 0, t:t + 1], ends[:, t, :], s["sort_scattered"], EP - 1)
                        scatter(ea_sorted, sidx[:, 0, t:t + 1], EA[:, 0, t, :], s["sort_scattered"], EP - 1)
                    wait(pool, s["sort_scattered"], u * (32 * T) + 32 * T, s["pool_went_on"])
                    pool.sem_inc(s["sort_slot_free"], 1)

            def turn(k, r):
                wait(pool, s["gidx_ready"], k + 1, s["pool_went_on"])
                if known(k, 2):
                    wait(pool, s["stats_read"], k - 1, s["pool_went_on"])
                    wait(pool, s["edges_step"], (k - 2) * 4 + 2, s["pool_went_on"])
                for t in range(T):
                    gather(X[:, r, t, :], x, gidx[:, r, t:t + 1], s[f"gathered{r}"])
                if known(k, 2):
                    wait(pool, s["edges_step"], (k - 1) * 4, s["pool_went_on"])
                    wait(pool, s[f"xd_saved{r}"], dma_uses(k - 2, r), s["pool_went_on"])
                for t in range(T, 2 * T):
                    gather(X[:, r, t, :], x, gidx[:, r, t:t + 1], s[f"gathered{r}"])

            turns(pool, 0, 5, U, lambda k, r4: turn(k, r4 % 2), 4)

            def put_z(rows_of, r, index):
                for t in range(T):
                    scatter(z_tab, index[:, t:t + 1], rows_of[:, t, :], s[f"z_scattered{r}"], N - 1)

            wait(pool, s["head_idx"], 1, s["pool_went_on"])
            gather(xh[:, :], x, smi[:, 1:2], s["node_in"])
            for r in range(2):
                wait(pool, s[f"state_saved{r}"], 16 * ((U + 1 - r) // 2), s["pool_went_on"])
                wait(pool, s[f"sums_saved{r}"], 16 * ((U + 1 - r) // 2), s["pool_went_on"])
            gather(HB[:, :], st_all, smi[:, 0:1], s["head_in"])
            for r in range(2):
                wait(pool, s[f"z_dense_saved{r}"], 32 * ((U + 1 - r) // 2), s["pool_went_on"])
            wait(pool, s["z_ahead_in"], 16 * AHEAD, s["pool_went_on"])
            for n in range(AHEAD - 1):
                put_z(ZT[n], n, sca_i[:, n * T:(n + 1) * T])
            for r in range(2):
                wait(pool, s[f"z_edge_saved{r}"], 16 * ((U + 1 - r) // 2), s["pool_went_on"])
            wait(pool, s["zfix_ready"], 1, s["pool_went_on"])
            scatter(z_all, smi[:, 3:4], zfix[:, :], s["z_patched"], U * P * T - 1)
            scatter(z_tab, smi[:, 2:3], zfix[:, :], s["z_fixed"], N - 1)
            put_z(ZT[AHEAD - 1], AHEAD - 1, sca_i[:, (AHEAD - 1) * T:AHEAD * T])
            wait(pool, s["z_fixed"], 16, s["pool_went_on"])
            for r in range(4):
                wait(pool, s[f"z_scattered{r}"], 16 * T, s["pool_went_on"])
            gather(tailc[:, :], z_tab, smi[:, 4:5], s["tail_in"])
            gather(zh[:, :], z_tab, smi[:, 1:2], s["zh_in"])

            def turn2(k, r4):
                wait(pool, s["sidx_ready"], k + 1, s["pool_went_on"])
                wait(pool, s[f"z_back{r4}"], dma_uses(k, r4, 16, 4), s["pool_went_on"])
                put_z(ZL[r4], r4, sidx[:, r4, :])

            turns(pool, 0, 5, U - AHEAD, turn2, 4)

            for r in range(4):
                wait(pool, s[f"z_scattered{r}"], 16 * T * ((U + 3 - r) // 4), s["pool_went_on"])
            for r in range(2):
                wait(pool, s[f"out_dense_saved{r}"], 32 * ((U + 1 - r) // 2), s["pool_went_on"])
            wait(pool, s["tail_in"], 16, s["pool_went_on"])

            def fetch(k, r):
                if known(k, 4):
                    wait(pool, s["agg2_done"], k - 3, s["pool_went_on"])
                    wait(pool, s["rows2_done"], k - 3, s["pool_went_on"])
                wait(pool, s["gidx_ready"], k + (U + 1), s["pool_went_on"])
                for t in range(T):
                    gather(ZS[r][:, t, :], z_tab, gidx4[r][:, t:t + 1], s[f"src2_in{r}"])

            def put(k, r):
                wait(pool, s["sidx_ready"], k + (U - AHEAD + 1), s["pool_went_on"])
                wait(pool, s["agg2_done"], k + 1, s["pool_went_on"])
                for t in range(T):
                    scatter(out, sidx[:, r, t:t + 1], OE[r][:, t, :], s[f"out_scattered{r}"], N - 1)

            def turn3(k, r):
                fetch(k, r)
                if known(k, 4):
                    put(k - 4, r)

            turns(pool, 0, 5, U, turn3, 4)
            for k in range(U - 4, U - 2):
                put(k, k % 4)
            for r in range(2):
                wait(pool, s[f"state2_saved{r}"], 16 * ((U + 1 - r) // 2), s["pool_went_on"])
            gather(HB[:, :], st_all, smi[:, 0:1], s["head_in"])
            for k in range(U - 2, U):
                put(k, k % 4)
            wait(pool, s["outfix_ready"], 1, s["pool_went_on"])
            scatter(out, smi[:, 2:3], zfix[:, :], s["out_fixed"], N - 1)
            for r in range(4):
                wait(pool, s[f"out_scattered{r}"], 16 * T * ((U + 3 - r) // 4), s["pool_went_on"])

        def link(eng, name, ins, also=None, n=1):
            links[name] = links.get(name, 0) + 1
            ins.then_inc(s[name], 1)
            eng.wait_ge(s[name], links[name])
            if also is not None:
                eng.sem_inc(also, n)

        links = {}

        def bc(ap, n):
            return ap.unsqueeze(2).to_broadcast([P, ap.shape[1], n])

        def weave(*chains):
            chains = list(chains)
            while chains:
                for c in list(chains):
                    if next(c, "end") == "end":
                        chains.remove(c)

        def softmax_logits(dve, k, q, n):
            a = bass.ds(k * T, T)
            m = m_all[:, bass.ds(k * T + 1, T)]
            L = pL[:, q * 2 * T:q * 2 * T + T]
            Ls = pL[:, q * 2 * T + T:(q + 1) * 2 * T]
            dx = [DX[:, q, i * T:(i + 1) * T] for i in range(4)]
            step = s["soft_step"]
            base = n * SM_STEPS
            dve.wait_ge(s["logits_ready"], n + 1)
            dve.tensor_tensor_scan(m, far[:, a], L, m_all[:, bass.ds(k * T, 1)], ALU.add, ALU.max).then_inc(step, 1)
            yield
            dve.wait_ge(step, base + 1)
            dve.tensor_tensor(dx[0], m_all[:, a], far[:, a], ALU.add).then_inc(step, 1)
            dve.tensor_tensor(dx[1], L, m, ALU.subtract).then_inc(step, 1)
            dve.tensor_tensor(mx8[:, :], m, Ls, ALU.max).then_inc(step, 1)
            yield
            dve.wait_ge(step, base + 4)
            dve.tensor_tensor(dx[0], dx[0], m, ALU.subtract).then_inc(step, 1)
            dve.tensor_tensor(dx[2], m, mx8[:, :], ALU.subtract).then_inc(step, 1)
            dve.tensor_tensor(dx[3], Ls, mx8[:, :], ALU.subtract).then_inc(step, 1)
            yield

        def aggregate(dve, k, q, n, hs, hd, relu, before_state):
            b = bass.ds(k * T + 1, T)
            ex = [EX[:, q, i * T:(i + 1) * T] for i in range(4)]
            step = s["agg_step"]
            base = n * AG_STEPS
            acc = ST[:, q, 0:D, :]
            prev = ST[:, 1 - q, 0:D, T - 1]
            dve.wait_ge(s["exps_ready"], n + 1)
            if relu:
                dve.scalar_tensor_tensor(out=V[:, 0:D, :].rearrange("p f t -> p t f"), in0=hs, scalar=0.0,
                                         in1=bc(ex[1], D), op0=ALU.max, op1=ALU.mult).then_inc(step, 1)
            else:
                dve.tensor_tensor(V[:, 0:D, :].rearrange("p f t -> p t f"), hs, bc(ex[1], D), ALU.mult
                                  ).then_inc(step, 1)
            dve.tensor_tensor_scan(den_all[:, b], ex[0], ex[1], den_all[:, bass.ds(k * T, 1)],
                                   ALU.mult, ALU.add).then_inc(step, 1)
            yield
            dve.wait_ge(step, base + 2)
            dve.scalar_tensor_tensor(out=V[:, 0:D, 0], in0=prev, scalar=EX[:, q, 0:1], in1=V[:, 0:D, 0],
                                     op0=ALU.mult, op1=ALU.add).then_inc(step, 1)
            dve.tensor_tensor(fin[:, 0, :], den_all[:, b], ex[2], ALU.mult).then_inc(step, 1)
            yield
            dve.wait_ge(step, base + 4)
            dve.wait_ge(s["decay_ready"], n + 1)
            before_state()
            dve.tensor_tensor_scan(acc.rearrange("p f t -> p (f t)"), RM[:, 0:D, :].rearrange("p f t -> p (f t)"),
                                   V[:, 0:D, :].rearrange("p f t -> p (f t)"), 0.0, ALU.mult, ALU.add
                                   ).then_inc(step, 1)
            dve.tensor_tensor(fin[:, 0, :], fin[:, 0, :], ex[3], ALU.add).then_inc(step, 1)
            yield
            dve.wait_ge(step, base + 6)
            dve.reciprocal(fin[:, 1, :], fin[:, 0, :]).then_inc(step, 1)
            yield
            dve.wait_ge(step, base + 7)
            dve.tensor_tensor(fin[:, 2, :], ex[2], fin[:, 1, :], ALU.mult).then_inc(step, 1)
            dve.tensor_tensor(fin[:, 3, :], ex[3], fin[:, 1, :], ALU.mult).then_inc(step, 1)
            yield
            dve.wait_ge(step, base + 9)
            dve.tensor_tensor(tmpf[:, 0, :, :], acc.rearrange("p f t -> p t f"), bc(fin[:, 2, :], D),
                              ALU.mult).then_inc(step, 1)
            if relu:
                dve.scalar_tensor_tensor(out=tmpf[:, 1, :, :], in0=hd, scalar=0.0, in1=bc(fin[:, 3, :], D),
                                         op0=ALU.max, op1=ALU.mult).then_inc(step, 1)
            else:
                dve.tensor_tensor(tmpf[:, 1, :, :], hd, bc(fin[:, 3, :], D), ALU.mult).then_inc(step, 1)
            yield
            dve.wait_ge(step, base + 11)

        @block.vector
        def _(dve):
            link(dve, "setup", dve.memset(src_i[:, :], 0))
            link(dve, "setup", dve.memset(dst_i[:, :], N))
            link(dve, "setup", dve.memset(edge_i[:, :], -1), s["pads_set"], 1)
            link(dve, "setup", dve.memset(ones[:, :], 1.0))
            link(dve, "setup", dve.memset(ZB[:, :, :, :], 0.0))
            link(dve, "setup", dve.memset(w1d[:, :], 0.0))
            link(dve, "setup", dve.memset(w2d[:, :], 0.0))
            link(dve, "setup", dve.memset(attp[:, :, :], 0.0))
            link(dve, "setup", dve.memset(we[:, :, :, :], 0.0), s["tiles_zeroed"], 1)

            def widen_dst():
                link(dve, "setup", dve.tensor_copy(dext[:, 1:C + 1], dst_i[:, :]))
                link(dve, "setup", dve.tensor_copy(dext[:, 0:1], edge_i[:, 0:1]))
                link(dve, "setup", dve.tensor_copy(dext[:, C + 1:C + 2], edge_i[:, 1:2]))

            dve.wait_ge(s["idx_in"], 16 * 7)
            widen_dst()
            link(dve, "setup", dve.tensor_tensor(tmpc[:, :], dext[:, 0:C], dext[:, 1:C + 1], ALU.is_gt))
            link(dve, "setup", dve.tensor_reduce(unsorted[:, :], tmpc[:, :], AX_X, ALU.add), s["falls_counted"], 1)
            dve.wait_ge(s["falls_summed"], 1)
            link(dve, "setup", dve.tensor_copy(flag[:, :], pL[0:1, 0:1]), s["flag_ready"], 1)
            with dve.If(dve.value_load(flag[0:1, 0:1]) > 0):
                def tell(ins):
                    link(dve, "rank_setup", ins)

                dve.wait_ge(s["iotas"], 2)
                tell(dve.memset(rank[:, :], 0.0))
                tell(dve.tensor_scalar(place[:, 0:1], iota_p[:, :], float(C), None, ALU.mult))
                tell(dve.tensor_scalar(place[:, :], iota_c[:, :], place[:, 0:1], None, ALU.add))
                dve.sem_inc(s["other_free"], 1)
                with dve.Fori(0, P) as i:
                    wait(dve, s["other_in"], i * 16 + 16, s["dve_went_on"])
                    dve.tensor_copy(other[:, :], other_i[:, :]).then_inc(s["other_ready"], 1)
                    wait(dve, s["other_ready"], i + 1, s["dve_went_on"])
                    with dve.Fori(0, U) as u:
                        a = bass.ds(u * T, T)
                        mine = dext[:, bass.ds(u * T + 1, T)]
                        done = (i * U + u) * 5
                        dve.tensor_tensor(earlier[:, :, :], iota_c[:, :].unsqueeze(1).to_broadcast([P, T, C]),
                                          bc(place[:, a], C), ALU.is_lt).then_inc(s["rank_step"], 1)
                        dve.tensor_tensor(lower[:, :, :], other[:, :].unsqueeze(1).to_broadcast([P, T, C]),
                                          bc(mine, C), ALU.subtract).then_inc(s["rank_step"], 1)
                        wait(dve, s["rank_step"], done + 2, s["dve_went_on"])
                        dve.tensor_tensor(lower[:, :, :], lower[:, :, :], earlier[:, :, :], ALU.is_lt
                                          ).then_inc(s["rank_step"], 1)
                        wait(dve, s["rank_step"], done + 3, s["dve_went_on"])
                        dve.tensor_reduce(lowers[:, :], lower[:, :, :], AX_X, ALU.add).then_inc(s["rank_step"], 1)
                        wait(dve, s["rank_step"], done + 4, s["dve_went_on"])
                        dve.tensor_tensor(rank[:, a], rank[:, a], lowers[:, :], ALU.add).then_inc(s["rank_step"], 1)
                        wait(dve, s["rank_step"], done + 5, s["dve_went_on"])
                    dve.tensor_scalar(place[:, :], place[:, :], -float(C), None, ALU.add).then_inc(s["placed"], 1)
                    wait(dve, s["placed"], i + 1, s["dve_went_on"])
                    dve.sem_inc(s["other_free"], 1)
                tell(dve.tensor_copy(sca_i[:, :], rank[:, :]))
                dve.sem_inc(s["ranked"], 1)
                dve.wait_ge(s["sorted_in"], 16 * 5)
                dve.tensor_copy(dext[:, 1:C + 1], dst_i[:, :]).then_inc(s["resorted"], 1)
                dve.tensor_copy(dext[:, 0:1], edge_i[:, 0:1]).then_inc(s["resorted"], 1)
                dve.tensor_copy(dext[:, C + 1:C + 2], edge_i[:, 1:2]).then_inc(s["resorted"], 1)
                dve.wait_ge(s["resorted"], 3)
                dve.nop()
            link(dve, "setup", dve.tensor_copy(gat_i[:, :, 0, :], src_i[:, :].rearrange("p (u t) -> p u t", t=T)))
            link(dve, "setup", dve.tensor_scalar(gat_i[:, :, 1, :], dext[:, 1:C + 1].rearrange("p (u t) -> p u t", t=T),
                              float(N - 1), None, ALU.min), s["gat_i_ready"], 1)
            dve.wait_ge(s["pool_filled"], 17)
            link(dve, "setup", dve.tensor_tensor(same[:, 0:C], dext[:, 1:C + 1], dext[:, 0:C], ALU.is_equal))
            link(dve, "setup", dve.tensor_tensor(notlast[:, :], dext[:, 1:C + 1], dext[:, 2:C + 2], ALU.is_equal))
            link(dve, "setup", dve.tensor_scalar(eq0[:, :], dext[:, 1:C + 1], dext[:, 1:2], None, ALU.is_equal))
            link(dve, "setup", dve.tensor_copy(sm[:, 0:1], same[:, 0:1]))
            link(dve, "setup", dve.tensor_copy(sm[:, 1:2], eq0[:, C - 1:C]))
            link(dve, "setup", dve.memset(same[:, 0:1], 0.0))
            link(dve, "setup", dve.tensor_scalar(far[:, :], same[:, 0:C], 1.0, -FAR, ALU.subtract, ALU.mult))
            link(dve, "setup", dve.tensor_tensor_scan(cnt[:, :], same[:, 0:C], ones[:, 0:1].to_broadcast([P, C]), 0.0,
                                                      ALU.mult, ALU.add))
            link(dve, "setup", dve.reciprocal(rcnt[:, :], cnt[:, :]))
            dve.wait_ge(s["weights_in"], 16 * (2 * (2 + 2 + 4 + 3) + 2))
            dve.wait_ge(s["ident_ready"], 1)
            link(dve, "setup", dve.tensor_scalar(w1d2[:, :], w1d[:, :], 2.0, None, ALU.mult))
            link(dve, "setup", dve.tensor_scalar(ident2[:, :], ident[:, :], 2.0, None, ALU.mult))
            for l in range(2):
                link(dve, "setup", dve.tensor_scalar(attr[:, l, 0, :], attp[:, l, :], 1.0 - NEG_SLOPE, None, ALU.mult))
                link(dve, "setup", dve.tensor_scalar(attr[:, l, 1, :], attp[:, l, :], NEG_SLOPE, None, ALU.mult))
            link(dve, "setup", dve.tensor_scalar(zb[:, 0:1], vecs[:, 0:1], 2.0, None, ALU.mult))
            link(dve, "setup", dve.tensor_tensor(cb[:, :], rows[:, 0, :], rows[:, 1, :], ALU.add))
            link(dve, "setup", dve.tensor_tensor(vsum[:, :], vecs[:, 0:1], vecs[:, 1:2], ALU.add))
            link(dve, "setup", dve.tensor_scalar(vrep[:, :], ones[:, :], vsum[:, 0:1], None, ALU.mult), s["weights_made"], 1)
            dve.wait_ge(s["w1_turned"], 1)
            link(dve, "setup", dve.tensor_copy(w1t[:, :], pT[0][:, 0:P]), s["w1t_ready"], 1)
            dve.wait_ge(s["w12_made"], 1)
            link(dve, "setup", dve.tensor_copy(w12[:, :], pT[1][:, 0:P]))
            link(dve, "setup", dve.tensor_scalar(zb[:, 1:2], vecs[:, 2:3], -2.0, None, ALU.mult))
            link(dve, "setup", dve.tensor_tensor(cb[:, :], cb[:, :], pS[:, 0:D], ALU.add))
            for i in range(3):
                left = cb[:, :] if i == 0 else rest[:, i - 1, :]
                link(dve, "setup", dve.tensor_copy(part[:, i, :], left))
                link(dve, "setup", dve.tensor_tensor(rest[:, i, :], left, part[:, i, :], ALU.subtract))
                link(dve, "setup", dve.tensor_scalar(third[:, i:i + 1], iota_p[:, :], float(i), None, ALU.is_equal))
                link(dve, "setup", dve.tensor_scalar(part[:, i, :], part[:, i, :], third[:, i:i + 1], None, ALU.mult))
            link(dve, "setup", dve.tensor_tensor(part[:, 0, :], part[:, 0, :], part[:, 1, :], ALU.add))
            link(dve, "setup", dve.tensor_tensor(part[:, 0, :], part[:, 0, :], part[:, 2, :], ALU.add))
            link(dve, "setup", dve.tensor_copy(ones_h[:, :], ones[:, :]))
            link(dve, "setup", dve.tensor_copy(cb3[:, :].rearrange("p (a d) -> p a d", d=D),
                                               part[:, 0, :].unsqueeze(1).to_broadcast([P, T, D])),
                 s["consts_ready"], 1)
            dve.wait_ge(s["consts_ready"], 1)

            def edge_attrs(k, r):
                step = s["attr_step"]
                base = k * AT_STEPS
                Va = V[:, D:W, :]
                dve.wait_ge(s[f"ea_in{r}"], dma_uses(k, r))
                dve.tensor_copy(Va.rearrange("p f t -> p t f"), EA[:, r, :, :]).then_inc(step, 1)
                yield
                dve.wait_ge(step, base + 1)
                dve.scalar_tensor_tensor(out=V[:, D:W, 0], in0=ST[:, 1 - r, D:W, T - 1],
                                         scalar=same[:, bass.ds(k * T, 1)], in1=V[:, D:W, 0],
                                         op0=ALU.mult, op1=ALU.add).then_inc(step, 1)
                yield
                dve.wait_ge(step, base + 2)
                dve.wait_ge(s["mask_spread"], k + 1)
                if known(k, 2):
                    dve.wait_ge(s[f"sums_saved{r}"], dma_uses(k - 2, r))
                dve.tensor_tensor_scan(ST[:, r, D:W, :].rearrange("p f t -> p (f t)"),
                                       RM[:, D:W, :].rearrange("p f t -> p (f t)"),
                                       Va.rearrange("p f t -> p (f t)"), 0.0, ALU.mult, ALU.add).then_inc(step, 1)
                yield
                dve.wait_ge(step, base + 3)
                if known(k, 2):
                    dve.wait_ge(s["ea_turned"], k - 1)
                dve.tensor_tensor(LA[:, r, :, :], ST[:, r, D:W, :].rearrange("p f t -> p t f"),
                                  bc(rcnt[:, bass.ds(k * T, T)], DE), ALU.mult).then_inc(step, 1)
                yield

            def row_stats(k, r, r4):
                dve.wait_ge(s[f"gathered{r}"], gathered(k, r))
                for t in range(2 * T):
                    last = dve.bn_stats(stats[:, t, :], X[:, r, t, :])
                last.then_inc(s["stats_read"], 1)
                dve.wait_ge(s[f"dense_in{r4}"], dma_uses(k, r4, 32, 4))
                for t in range(2 * T):
                    last = dve.bn_stats(stats[:, 2 * T + t, :], XD[:, r4, t, :])
                last.then_inc(s["dense_stats"], 1)
                dve.wait_ge(s["dense_stats"], k + 1)

            def norm_chain(k, r):
                base = k * LN_STEPS
                step = s["stats_step"]
                me, ve, mo, vo = (stats[:, :, c] for c in (1, 2, 4, 5))
                t = [lnb[:, i, :] for i in range(7)]
                rs = rstd[:, r, :]
                mean = meanb[:, r, :]
                dve.tensor_tensor(t[0], me, mo, ALU.add).then_inc(step, 1)
                dve.tensor_tensor(t[1], me, mo, ALU.subtract).then_inc(step, 1)
                dve.tensor_tensor(t[2], ve, vo, ALU.add).then_inc(step, 1)
                yield
                dve.wait_ge(step, base + 3)
                dve.scalar_tensor_tensor(out=t[3], in0=t[1], scalar=0.25, in1=t[1],
                                         op0=ALU.mult, op1=ALU.mult).then_inc(step, 1)
                dve.tensor_scalar(t[4], t[2], 1.0 / D, EPS, ALU.mult, ALU.add).then_inc(step, 1)
                dve.tensor_scalar(mean, t[0], 0.5, None, ALU.mult).then_inc(step, 1)
                yield
                dve.wait_ge(step, base + 6)
                dve.tensor_tensor(t[5], t[3], t[4], ALU.add).then_inc(step, 1)
                yield
                dve.wait_ge(step, base + 7)
                dve.tensor_scalar(t[6].bitcast(I32), t[5].bitcast(I32), 1, None,
                                  ALU.logical_shift_right).then_inc(step, 1)
                yield
                dve.wait_ge(step, base + 8)
                dve.tensor_scalar(rs.bitcast(I32), t[6].bitcast(I32), -1.0, RSQRT_MAGIC,
                                  ALU.mult, ALU.add).then_inc(step, 1)
                yield
                n = 9
                for _ in range(3):
                    dve.wait_ge(step, base + n)
                    dve.scalar_tensor_tensor(out=t[0], in0=rs, scalar=-0.5, in1=rs,
                                             op0=ALU.mult, op1=ALU.mult).then_inc(step, 1)
                    yield
                    dve.wait_ge(step, base + n + 1)
                    dve.tensor_tensor(t[1], t[0], t[5], ALU.mult).then_inc(step, 1)
                    yield
                    dve.wait_ge(step, base + n + 2)
                    dve.scalar_tensor_tensor(out=rs, in0=t[1], scalar=1.5, in1=rs,
                                             op0=ALU.add, op1=ALU.mult).then_inc(step, 1)
                    yield
                    n += 3
                dve.wait_ge(step, base + n)
                dve.scalar_tensor_tensor(out=nmr[:, r, :], in0=mean, scalar=-1.0,
                                         in1=rs, op0=ALU.mult, op1=ALU.mult).then_inc(step, 1)
                assert n + 1 == LN_STEPS
                yield

            def edge_rows(k, r):
                if known(k, 2):
                    dve.wait_ge(s["hd_turned"], k - 1)
                for side in range(2):
                    c = slice(side * T, (side + 1) * T)
                    h = H[:, r, c, :]
                    step = s["edges_step"]
                    base = k * 4 + side * 2
                    dve.tensor_tensor(h, X[:, r, c, :], bc(meanb[:, r, c], D), ALU.subtract).then_inc(step, 1)
                    yield
                    dve.wait_ge(step, base + 1)
                    dve.tensor_tensor(h, h, bc(rstd[:, r, c], D), ALU.mult).then_inc(step, 1)
                    yield

            def out_dense(k, r, r4):
                dve.wait_ge(s["z_dense_ready"], k + 1)
                if known(k, 2):
                    dve.wait_ge(s[f"out_dense_saved{r}"], dma_uses(k - 2, r, 32))
                for b in range(2):
                    c = slice(b * T, (b + 1) * T)
                    last = dve.tensor_tensor(OD[:, r, c, :].rearrange("p t d -> p (t d)"),
                                             XD[:, r4, c, :].rearrange("p t d -> p (t d)"),
                                             TD[:, r, b, :], ALU.add)
                    if b == 0:
                        yield
                last.then_inc(s["out_dense_done"], 1)
                yield

            def mean1(k, r):
                def before_state():
                    if known(k, 2):
                        dve.wait_ge(s[f"state_saved{r}"], dma_uses(k - 2, r))

                yield from aggregate(dve, k, r, k, H[:, r, 0:T, :], H[:, r, T:2 * T, :], True, before_state)
                if known(k, 2):
                    dve.wait_ge(s["h1_turned"], k - 1)
                dve.tensor_tensor(H1[:, r, :, :], tmpf[:, 0, :, :], tmpf[:, 1, :, :], ALU.add
                                  ).then_inc(s["h1_ready"], 1)
                yield

            def turn(k, r4):
                r = r4 % 2
                late = isinstance(k, int) and k >= U
                if not late:
                    row_stats(k, r, r4)
                chains = [] if late else [norm_chain(k, r), edge_attrs(k, r)]
                if known(k, 2):
                    chains.append(mean1(k - 2, r))
                weave(*chains)
                chains = []
                if not late:
                    dve.wait_ge(s["stats_step"], k * LN_STEPS + LN_STEPS)
                    chains.append(edge_rows(k, r))
                if known(k, 1) and not (late and k - 1 >= U):
                    chains.append(chain([None] * 2, softmax_logits(dve, k - 1, 1 - r, k - 1)))
                if known(k, 2):
                    chains.append(chain([None] * 4, out_dense(k - 2, r, (r4 + 2) % 4)))
                weave(*chains)

            def norm_nodes():
                dve.wait_ge(s["node_in"], 16)
                mean = lnb[:, 0, 0:1]
                link(dve, "seam", dve.bn_stats(stats[:, 0, :], xh[:, :]))
                link(dve, "seam", dve.tensor_tensor(lnb[:, 0, 0:1], stats[:, 0, 1:2], stats[:, 0, 4:5], ALU.add))
                link(dve, "seam", dve.tensor_tensor(lnb[:, 1, 0:1], stats[:, 0, 1:2], stats[:, 0, 4:5], ALU.subtract))
                link(dve, "seam", dve.tensor_tensor(lnb[:, 2, 0:1], stats[:, 0, 2:3], stats[:, 0, 5:6], ALU.add))
                link(dve, "seam", dve.scalar_tensor_tensor(out=lnb[:, 3, 0:1], in0=lnb[:, 1, 0:1], scalar=0.25, in1=lnb[:, 1, 0:1],
                                         op0=ALU.mult, op1=ALU.mult))
                link(dve, "seam", dve.tensor_scalar(lnb[:, 4, 0:1], lnb[:, 2, 0:1], 1.0 / D, EPS, ALU.mult, ALU.add))
                link(dve, "seam", dve.tensor_scalar(lnb[:, 7, 0:1], mean, 0.5, None, ALU.mult))
                v = lnb[:, 5, 0:1]
                y = lnb[:, 6, 0:1]
                link(dve, "seam", dve.tensor_tensor(v, lnb[:, 3, 0:1], lnb[:, 4, 0:1], ALU.add))
                link(dve, "seam", dve.tensor_scalar(y.bitcast(I32), v.bitcast(I32), 1, None,
                                                    ALU.logical_shift_right))
                link(dve, "seam", dve.tensor_scalar(y.bitcast(I32), y.bitcast(I32), -1.0, RSQRT_MAGIC,
                                                    ALU.mult, ALU.add))
                for _ in range(3):
                    link(dve, "seam", dve.scalar_tensor_tensor(out=lnb[:, 0, 0:1], in0=y, scalar=-0.5, in1=y,
                                                               op0=ALU.mult, op1=ALU.mult))
                    link(dve, "seam", dve.tensor_tensor(lnb[:, 1, 0:1], lnb[:, 0, 0:1], v, ALU.mult))
                    link(dve, "seam", dve.scalar_tensor_tensor(out=y, in0=lnb[:, 1, 0:1], scalar=1.5, in1=y,
                                                               op0=ALU.add, op1=ALU.mult))
                link(dve, "seam", dve.tensor_scalar(hh[:, :], xh[:, :], lnb[:, 7, 0:1], y, ALU.subtract, ALU.mult))
                link(dve, "seam", dve.tensor_scalar(hh[:, :], hh[:, :], 0.0, None, ALU.max))

            def runs():
                link(dve, "setup", dve.tensor_scalar(lastm[:, :], notlast[:, :], -1.0, 1.0, ALU.mult, ALU.add))
                link(dve, "setup", dve.tensor_scalar(tmpd[:, :], eq0[:, :], sm[:, 0:1], None, ALU.mult))
                link(dve, "setup", dve.tensor_scalar(tmpc[:, :], same[:, 1:C + 1], -1.0, 1.0, ALU.mult, ALU.add))
                link(dve, "setup", dve.tensor_scalar(tmpd[:, :], tmpd[:, :], -1.0, 1.0, ALU.mult, ALU.add))
                link(dve, "setup", dve.tensor_tensor(hend[:, :], eq0[:, :], tmpc[:, :], ALU.mult))
                link(dve, "setup", dve.tensor_tensor(tmpd[:, :], tmpd[:, :], lastm[:, :], ALU.mult))
                link(dve, "setup", dve.scalar_tensor_tensor(out=tmpd[:, :], in0=dext[:, 1:C + 1], scalar=SKIP,
                                                            in1=tmpd[:, :], op0=ALU.subtract, op1=ALU.mult))
                link(dve, "setup", dve.tensor_scalar(sca_i[:, :], tmpd[:, :], SKIP, None, ALU.add))
                dve.wait_ge(s["iotas"], 2)
                link(dve, "setup", dve.tensor_tensor(tmpc[:, :], hend[:, :], iota_c[:, :], ALU.mult))
                link(dve, "setup", dve.tensor_reduce(sm[:, 2:3], tmpc[:, :], AX_X, ALU.add))
                link(dve, "setup", dve.tensor_tensor(tmpc[:, :], hend[:, :], lastm[:, :], ALU.mult))
                link(dve, "setup", dve.tensor_reduce(sm[:, 3:4], tmpc[:, :], AX_X, ALU.add))
                link(dve, "setup", dve.tensor_copy(smi[:, 5:6], sm[:, 2:3]))
                link(dve, "setup", dve.tensor_scalar(smi[:, 0:1], smi[:, 5:6], 3, None, ALU.logical_shift_right))
                link(dve, "setup", dve.tensor_copy(sm[:, 4:5], smi[:, 0:1]))
                link(dve, "setup", dve.scalar_tensor_tensor(out=sm[:, 5:6], in0=sm[:, 4:5], scalar=-float(T),
                                                            in1=sm[:, 2:3], op0=ALU.mult, op1=ALU.add))
                link(dve, "setup", dve.tensor_scalar(mask8[:, :], iota_c[:, 0:T], sm[:, 5:6], None, ALU.is_equal))
                link(dve, "setup", dve.scalar_tensor_tensor(out=sm[:, 6:7], in0=sm[:, 4:5], scalar=float(P),
                                                            in1=iota_p[:, :], op0=ALU.mult, op1=ALU.add))
                link(dve, "setup", dve.tensor_copy(smi[:, 0:1], sm[:, 6:7]))
                link(dve, "setup", dve.scalar_tensor_tensor(out=sm[:, 7:8], in0=sm[:, 6:7], scalar=float(T), in1=sm[:, 5:6],
                                         op0=ALU.mult, op1=ALU.add))
                link(dve, "setup", dve.tensor_tensor(sm[:, 8:9], sm[:, 3:4], sm[:, 0:1], ALU.mult))
                link(dve, "setup", dve.scalar_tensor_tensor(out=sm[:, 9:10], in0=dext[:, 1:2], scalar=SKIP,
                                                            in1=sm[:, 8:9], op0=ALU.subtract, op1=ALU.mult))
                link(dve, "setup", dve.tensor_scalar(smi[:, 2:3], sm[:, 9:10], SKIP, None, ALU.add))
                link(dve, "setup", dve.scalar_tensor_tensor(out=sm[:, 9:10], in0=sm[:, 7:8], scalar=SKIP,
                                                            in1=sm[:, 8:9], op0=ALU.subtract, op1=ALU.mult))
                link(dve, "setup", dve.tensor_scalar(smi[:, 3:4], sm[:, 9:10], SKIP, None, ALU.add))
                link(dve, "setup", dve.tensor_scalar(smi[:, 1:2], dext[:, 1:2], float(N - 1), None, ALU.min))
                link(dve, "setup", dve.tensor_scalar(smi[:, 4:5], dext[:, C:C + 1], float(N - 1), None, ALU.min))
                link(dve, "setup", dve.tensor_tensor(sm[:, 10:11], sm[:, 0:1], sm[:, 1:2], ALU.mult))
                link(dve, "setup", dve.tensor_scalar(sm[:, 11:12], sm[:, 10:11], 1.0, -FAR, ALU.subtract, ALU.mult))
                link(dve, "setup", dve.tensor_scalar(sm[:, 12:13], sm[:, 0:1], 1.0, -FAR, ALU.subtract, ALU.mult), s["head_idx"], 1)

            turns(dve, 0, 4, U - 1, turn, 4)
            turn(U - 1, 0)
            runs()
            turn(U, 1)
            turn(U + 1, 2)

            def spread_tails(layer, rT, width):
                link(dve, "seam", dve.tensor_copy(TS[:, 0:width], ST[:, rT, 0:width, T - 1]))
                link(dve, "seam", dve.tensor_copy(TS[:, W:W + 1], den_all[:, C:C + 1]))
                if layer == 0:
                    link(dve, "seam", dve.tensor_copy(TS[:, W + 1:W + 2], cnt[:, C - 1:C]))
                link(dve, "seam", dve.tensor_copy(sm[:, 14:15], m_all[:, C:C + 1]))
                dve.sem_inc(s["tails_ready"], 1)
                link(dve, "seam", dve.tensor_tensor(tmpc[:, :], hend[:, :], m_all[:, 1:C + 1], ALU.mult))
                link(dve, "seam", dve.tensor_reduce(sm[:, 13:14], tmpc[:, :], AX_X, ALU.add))
                link(dve, "seam", dve.tensor_tensor(tmpd[:, :], hend[:, :], den_all[:, 1:C + 1], ALU.mult))
                link(dve, "seam", dve.tensor_reduce(HS[:, W:W + 1], tmpd[:, :], AX_X, ALU.add))
                if layer == 0:
                    link(dve, "seam", dve.tensor_tensor(tmpc[:, :], hend[:, :], cnt[:, :], ALU.mult))
                    link(dve, "seam", dve.tensor_reduce(HS[:, W + 1:W + 2], tmpc[:, :], AX_X, ALU.add))

            def spread_heads(layer, width):
                dve.wait_ge(s["head_in"], 16 * (layer + 1))
                hb = HB[:, 0:width * T].rearrange("p (f t) -> p f t", t=T)
                link(dve, "seam", dve.tensor_tensor(V[:, 0:width, :], hb,
                                                    mask8[:, :].unsqueeze(1).to_broadcast([P, width, T]), ALU.mult))
                link(dve, "seam", dve.tensor_reduce(HS[:, 0:width], V[:, 0:width, :], AX_X, ALU.add))

            def seam(layer, rT):
                width = W if layer == 0 else D
                spread_tails(layer, rT, width)
                dve.wait_ge(s["rows_turned"], layer + 1)
                link(dve, "seam", dve.tensor_copy(row[:, 2:5, 0:P], pS[0:1, 0:3 * P].rearrange("p (a b) -> p a b", a=3)))
                link(dve, "seam", dve.tensor_tensor_scan(row[:, 1, 1:P + 1], row[:, 3, 0:P], row[:, 2, 0:P], FAR,
                                                         ALU.add, ALU.max))
                link(dve, "seam", dve.tensor_tensor(row[:, 5, 0:P], row[:, 2, 0:P], row[:, 1, 1:P + 1], ALU.subtract))
                link(dve, "seam", dve.tensor_tensor(row[:, 6, 0:P], row[:, 1, 0:P], row[:, 3, 0:P], ALU.add))
                link(dve, "seam", dve.tensor_tensor(row[:, 6, 0:P], row[:, 6, 0:P], row[:, 1, 1:P + 1], ALU.subtract))
                dve.sem_inc(s["row_exps_asked"], 1)
                if layer == 0:
                    norm_nodes()
                spread_heads(layer, width)
                dve.wait_ge(s["decay_spread"], layer + 1)
                link(dve, "seam", dve.tensor_copy(QT[0:W + 2, :], pM[0:W + 2, 0:P]))
                dve.wait_ge(s["tails_turned"], layer + 1)
                link(dve, "seam", dve.tensor_tensor(QT[0:W + 2, :], QT[0:W + 2, :], pT[0][0:W + 2, 0:P], ALU.mult))
                link(dve, "seam", dve.tensor_tensor_scan(OT[0:W + 2, 1:P + 1], pM[0:W + 2, P:2 * P], QT[0:W + 2, :], 0.0,
                                                         ALU.mult, ALU.add))
                dve.sem_inc(s["carries_made"], 1)
                dve.wait_ge(s["carries_turned"], layer + 1)
                link(dve, "seam", dve.tensor_copy(CS[:, 0:W + 2], pT[1][:, 0:W + 2]))
                link(dve, "seam", dve.tensor_scalar(sm[:, 15:16], pS[:, 3 * P:3 * P + 1], sm[:, 12:13], None, ALU.add))
                link(dve, "seam", dve.tensor_tensor(sm[:, 16:17], sm[:, 15:16], sm[:, 13:14], ALU.max))
                link(dve, "seam", dve.tensor_tensor(sm[:, 17:18], sm[:, 13:14], sm[:, 16:17], ALU.subtract))
                link(dve, "seam", dve.tensor_tensor(sm[:, 18:19], sm[:, 15:16], sm[:, 16:17], ALU.subtract))
                dve.sem_inc(s["seam_exps_asked"], 1)
                dve.wait_ge(s["seam_exps"], 2 * layer + 1)
                for a, b in ((0, D), (W, W + 1)):
                    link(dve, "seam", dve.tensor_scalar(HS[:, a:b], HS[:, a:b], sm[:, 19:20], None, ALU.mult))
                    link(dve, "seam", dve.scalar_tensor_tensor(out=HS[:, a:b], in0=CS[:, a:b], scalar=sm[:, 20:21],
                                                               in1=HS[:, a:b], op0=ALU.mult, op1=ALU.add))
                if layer == 0:
                    for a, b in ((D, W), (W + 1, W + 2)):
                        link(dve, "seam", dve.scalar_tensor_tensor(out=HS[:, a:b], in0=CS[:, a:b], scalar=sm[:, 0:1],
                                                                   in1=HS[:, a:b], op0=ALU.mult, op1=ALU.add))
                    link(dve, "seam", dve.reciprocal(sm[:, 21:22], HS[:, W + 1:W + 2]))
                    link(dve, "seam", dve.tensor_scalar(loopm[:, :], HS[:, D:W], sm[:, 21:22], None, ALU.mult))
                node = hh if layer == 0 else zh
                if layer == 1:
                    dve.wait_ge(s["zh_in"], 16)
                else:
                    dve.sem_inc(s["node_ready"], 1)
                dve.wait_ge(s["loop_logit"], layer + 1)
                ls = pL[:, 4 * T:4 * T + 1]
                link(dve, "seam", dve.tensor_tensor(sm[:, 15:16], ls, sm[:, 16:17], ALU.max))
                link(dve, "seam", dve.tensor_tensor(sm[:, 17:18], sm[:, 16:17], sm[:, 15:16], ALU.subtract))
                link(dve, "seam", dve.tensor_tensor(sm[:, 18:19], ls, sm[:, 15:16], ALU.subtract))
                dve.sem_inc(s["seam_exps_asked"], 1)
                dve.wait_ge(s["seam_exps"], 2 * layer + 2)
                link(dve, "seam", dve.scalar_tensor_tensor(out=sm[:, 21:22], in0=HS[:, W:W + 1], scalar=sm[:, 19:20],
                                                           in1=sm[:, 20:21], op0=ALU.mult, op1=ALU.add))
                link(dve, "seam", dve.reciprocal(sm[:, 22:23], sm[:, 21:22]))
                link(dve, "seam", dve.tensor_scalar(sm[:, 19:21], sm[:, 19:21], sm[:, 22:23], None, ALU.mult))
                link(dve, "seam", dve.tensor_scalar(fixv[:, 0, :], HS[:, 0:D], sm[:, 19:20], None, ALU.mult))
                link(dve, "seam", dve.scalar_tensor_tensor(out=fixv[:, 1, :], in0=node[:, :], scalar=sm[:, 20:21],
                                                           in1=fixv[:, 0, :], op0=ALU.mult, op1=ALU.add))

            seam(0, 0)
            dve.sem_inc(s["fixv_ready"], 1)
            dve.wait_ge(s["zfix_made"], 1)
            link(dve, "seam", dve.tensor_tensor(zfix[:, :], pM[:, 0:D], cb[:, :], ALU.add), s["zfix_ready"], 1)
            link(dve, "seam", dve.memset(m_all[:, 0:1], FAR))

            dve.wait_ge(s["tail_in"], 16)

            def turn2(k, r4):
                r = r4 % 2
                u = (U - 1) - k
                a = bass.ds(u * T, T)
                base = k * (T + 1)
                if isinstance(k, int) and k >= U - AHEAD:
                    back = ZT[k - (U - AHEAD)]
                    wait(dve, s["z_tail_back"], 16 * AHEAD, s["dve_went_on"])
                else:
                    back = ZL[r4]
                    wait(dve, s[f"z_back{r4}"], dma_uses(k, r4, 16, 4), s["dve_went_on"])
                if known(k, 2):
                    wait(dve, s[f"zd_saved{r}"], dma_uses(k - 2, r), s["dve_went_on"])
                dve.tensor_tensor(ZB[:, r, :, :], back, bc(lastm[:, a], D), ALU.mult
                                  ).then_inc(s["back_step"], 1)
                for n, t in enumerate(reversed(range(T))):
                    prev = ZB[:, r, t + 1, :] if t + 1 < T else (ZB[:, 1 - r, 0, :] if known(k, 1) else tailc[:, :])
                    wait(dve, s["back_step"], base + n + 1, s["dve_went_on"])
                    ins = dve.scalar_tensor_tensor(out=ZB[:, r, t, :], in0=prev,
                                                   scalar=notlast[:, bass.ds(u * T + t, 1)], in1=ZB[:, r, t, :],
                                                   op0=ALU.mult, op1=ALU.add).then_inc(s["back_step"], 1)
                wait(dve, s["back_step"], base + T + 1, s["dve_went_on"])
                dve.sem_inc(s["zd_ready"], 1)

            turns(dve, 0, 5, U - AHEAD, turn2, 4)
            for k in range(U - AHEAD, U):
                turn2(k, k % 4)

            def turn3(k, r4):
                r = r4 % 2
                n = k + U
                dve.wait_ge(s[f"dst2_in{r}"], dma_uses(k, r, 48))
                weave(softmax_logits(dve, k, r, n))

                def before_state():
                    if known(k, 2):
                        dve.wait_ge(s[f"state2_saved{r}"], dma_uses(k - 2, r))

                weave(aggregate(dve, k, r, n, ZS[r4], ZD[:, r, :, :], False, before_state))
                dve.tensor_tensor(tmpf[:, 0, :, :], tmpf[:, 0, :, :], tmpf[:, 1, :, :], ALU.add
                                  ).then_inc(s["mean2_ready"], 1)
                dve.wait_ge(s["mean2_ready"], k + 1)
                if known(k, 4):
                    dve.wait_ge(s[f"out_scattered{r4}"], by_four(k - 4, r4))
                dve.tensor_tensor(OE[r4], tmpf[:, 0, :, :], XR[:, r, :, :], ALU.add
                                  ).then_inc(s["agg2_done"], 1)

            turns(dve, 0, 5, U, turn3, 4)
            seam(1, 0)
            dve.tensor_tensor(zfix[:, :], fixv[:, 1, :], xh[:, :], ALU.add).then_inc(s["outfix_ready"], 1)

        @block.scalar
        def _(act):
            def exps(k, q, n):
                act.wait_ge(s["soft_step"], n * SM_STEPS + SM_STEPS)
                act.activation(EX[:, q, :], DX[:, q, :], ACT.Exp).then_inc(s["exps_ready"], 1)
                act.wait_ge(s["exps_ready"], n + 1)
                if known(n, 1):
                    act.wait_ge(s["agg_step"], (n - 1) * AG_STEPS + 5)
                act.activation(RM[:, 0:D, 1:T], EX[:, q, 1:T].unsqueeze(1).to_broadcast([P, D, T - 1]),
                               ACT.Copy).then_inc(s["decay_ready"], 1)

            def leaky_rows(n, layer, done_m, done_s):
                for i, (ps_i, made) in enumerate(((pM, "rows_m"), (pS, "rows_s"))):
                    act.wait_ge(s[made], n + 1)
                    if known(n, 1):
                        act.wait_ge(s["logits_ready"], n)
                    act.activation(mz[:, 2 * i, :], ps_i[:, :], ACT.Relu, bias=zb[:, layer:layer + 1])
                    act.activation(mz[:, 2 * i + 1, :], ps_i[:, :], ACT.Identity, bias=zb[:, layer:layer + 1]
                                   ).then_inc(s[(done_m, done_s)[i]], 1)

            def mask(k):
                if known(k, 1):
                    act.wait_ge(s["attr_step"], (k - 1) * AT_STEPS + 3)
                act.activation(RM[:, D:W, 1:T],
                               same[:, bass.ds(k * T + 1, T - 1)].unsqueeze(1).to_broadcast([P, DE, T - 1]),
                               ACT.Copy).then_inc(s["mask_spread"], 1)

            def dense_rows(k, r, r4, b):
                if b == 0:
                    act.wait_ge(s["stats_step"], k * LN_STEPS + LN_STEPS)
                    if known(k, 2):
                        act.wait_ge(s["dense1_turned"], k - 1)
                for t in range(b * T, (b + 1) * T):
                    c = slice(2 * T + t, 2 * T + t + 1)
                    last = act.activation(HD[:, r, t, :], XD[:, r4, t, :], ACT.Relu,
                                          bias=nmr[:, r, c], scale=rstd[:, r, c])
                last.then_inc(s["dense0_normed" if b == 0 else "dense_normed"], 1)

            def first_part(k, r, r4):
                dense_rows(k, r, r4, 0)
                for b, nm in enumerate(("hs", "hd")):
                    act.wait_ge(s[f"{nm}_turned"], k + 1)
                    if known(k, 1):
                        act.wait_ge(s["rows_s"], k)
                    act.activation(hts[:, b, :], pT[b][:, :], ACT.Relu).then_inc(s[f"{nm}_out"], 1)

            def second_part(k, r, r4):
                act.wait_ge(s["ea_turned"], k + 1)
                if known(k, 2):
                    act.wait_ge(s[f"el_saved{r}"], dma_uses(k - 2, r))
                    act.wait_ge(s["rows_s"], k - 1)
                act.activation(EL[:, r, :], pT[0][:, :], ACT.Copy).then_inc(s["el_ready"], 1)
                if not isinstance(k, int) or k + 1 < U:
                    mask(k + 1)
                dense_rows(k, r, r4, 1)

            def z_dense_out(k, r):
                act.wait_ge(s["z_dense_made"], k + 1)
                if known(k, 2):
                    act.wait_ge(s[f"z_dense_saved{r}"], dma_uses(k - 2, r, 32))
                    act.wait_ge(s["out_dense_done"], k - 1)
                act.activation(TD[:, r, :, :].rearrange("p b f -> p (b f)"), pY[:, :, :].rearrange("p b f -> p (b f)"),
                               ACT.Copy).then_inc(s["z_dense_ready"], 1)

            def third_part(k, r):
                leaky_rows(k, 0, "mz_m", "mz_s")
                for b in range(2):
                    act.wait_ge(s[f"dense{b}_turned"], k + 1)
                    if known(k, 1):
                        act.wait_ge(s["z_dense_made"], k)
                    act.activation(htd[:, b, :], pT[1 - b][:, :], ACT.Copy).then_inc(s[f"dense{b}_out"], 1)

            def means_out(k):
                act.wait_ge(s["h1_turned"], k + 1)
                if known(k, 1):
                    act.wait_ge(s["z_edge_made"], k)
                act.activation(h1t[:, :], pT[1][:, :], ACT.Copy).then_inc(s["h1t_ready"], 1)

            def z_edges_out(k, r):
                act.wait_ge(s["z_edge_made"], k + 1)
                if known(k, 2):
                    act.wait_ge(s[f"z_edge_saved{r}"], dma_uses(k - 2, r))
                act.activation(ZE[:, r, :], pZ[:, :], ACT.Copy).then_inc(s["z_edge_ready"], 1)

            def rows_to_gather(k, r, layer=0):
                if layer == 0:
                    act.activation(gidx[:, r, :], gat_i[:, bass.ds(k, 1), :, :].rearrange("p u s t -> p (u s t)"),
                                   ACT.Copy).then_inc(s["gidx_ready"], 1)
                else:
                    act.activation(gidx4[r], gat_i[:, bass.ds(k, 1), 0, :].rearrange("p u t -> p (u t)"),
                                   ACT.Copy).then_inc(s["gidx_ready"], 1)

            def rows_to_scatter(u, r):
                act.activation(sidx[:, r, :], sca_i[:, bass.ds(u * T, T)], ACT.Copy).then_inc(s["sidx_ready"], 1)

            act.wait_ge(s["gat_i_ready"], 1)
            for k in range(2):
                rows_to_gather(k, k)
            act.wait_ge(s["consts_ready"], 1)
            mask(0)

            def turn(k, r4):
                r = r4 % 2
                late = isinstance(k, int) and k >= U
                before = known(k, 1) and not (late and k - 1 >= U)
                if not isinstance(k, int) or k + 2 < U:
                    act.wait_ge(s[f"gathered{r}"], gathered(k, r))
                    rows_to_gather(k + 2, r)
                if not late:
                    first_part(k, r, r4)
                if before and not late:
                    exps(k - 1, 1 - r, k - 1)
                if known(k, 3):
                    z_edges_out(k - 3, 1 - r)
                if not late:
                    second_part(k, r, r4)
                if before:
                    z_dense_out(k - 1, 1 - r)
                if not late:
                    third_part(k, r)
                if isinstance(k, int) and k == U - 1:
                    exps(k, r, k)
                if known(k, 2) and not (late and k - 2 >= U):
                    means_out(k - 2)

            turns(act, 0, 4, U - 2, turn, 4)
            for k in range(U - 2, U + 3):
                turn(k, k % 4)

            def loop_rows_out(layer):
                act.wait_ge(s["node_turned"], layer + 1)
                if layer == 0:
                    act.activation(lpt[:, :], pT[0][0:DE, P:2 * P], ACT.Copy)
                act.activation(hht[0:D, :], pT[0][0:D, 0:P], ACT.Copy).then_inc(s["node_out"], 1)
                act.wait_ge(s["loop_rows"], layer + 1)
                act.activation(srz[:, 0, :], pM[0:D, 0:P], ACT.Relu, bias=zb[0:D, layer:layer + 1])
                act.activation(srz[:, 1, :], pM[0:D, 0:P], ACT.Identity, bias=zb[0:D, layer:layer + 1]
                               ).then_inc(s["loop_leaky"], 1)

            def seam(layer):
                act.wait_ge(s["row_exps_asked"], layer + 1)
                act.activation(row[:, 7:9, 0:P], row[:, 5:7, 0:P], ACT.Exp).then_inc(s["row_exps"], 1)
                act.wait_ge(s["seam_exps_asked"], 2 * layer + 1)
                act.activation(sm[:, 19:21], sm[:, 17:19], ACT.Exp).then_inc(s["seam_exps"], 1)
                if layer == 0:
                    loop_rows_out(0)
                act.wait_ge(s["seam_exps_asked"], 2 * layer + 2)
                act.activation(sm[:, 19:21], sm[:, 17:19], ACT.Exp).then_inc(s["seam_exps"], 1)

            seam(0)
            act.wait_ge(s["fix_turned"], 1)
            act.activation(fixt[:, :], pT[0][0:D, 0:P], ACT.Copy).then_inc(s["fixt_ready"], 1)

            def turn2(k, r):
                if known(k, 4):
                    act.wait_ge(s[f"z_scattered{r}"], by_four(k, r))
                rows_to_scatter((U - 1) - k, r)

            turns(act, 0, 5, U - AHEAD, turn2, 4)
            loop_rows_out(1)

            for k in range(4):
                rows_to_gather(k, k, 1)
            for r in range(4):
                act.wait_ge(s[f"z_scattered{r}"], 16 * T * ((U + 3 - r) // 4))

            def scatter_rows(k, r):
                if known(k, 4):
                    act.wait_ge(s[f"out_scattered{r}"], by_four(k - 4, r))
                rows_to_scatter(k, r)

            def turn3(k, r):
                n = k + U
                leaky_rows(n, 1, "mz_m", "mz_s")
                exps(k, r % 2, n)
                if not isinstance(k, int) or k + 4 < U:
                    act.wait_ge(s[f"src2_in{r}"], by_four(k, r))
                    rows_to_gather(k + 4, r, 1)
                if known(k, 1):
                    scatter_rows(k - 1, (r - 1) % 4)

            turns(act, 0, 5, U - 4, turn3, 4)
            for k in range(U - 4, U):
                turn3(k, k % 4)
            scatter_rows(U - 1, (U - 1) % 4)
            seam(1)

        @block.tensor
        def _(pe):
            def turned(to, tile, signal):
                for j in range(F // P):
                    last = pe.transpose(to[:, j * P:(j + 1) * P], tile[:, j * P:(j + 1) * P], ident[:, :])
                last.then_inc(signal, 1)

            def flat(ap):
                return ap.rearrange("p t d -> p (t d)")

            def logits(n, q, layer):
                for i, ready in enumerate(("mz_m", "mz_s")):
                    pe.wait_ge(s[ready], n + 1)
                    if i == 0 and known(n, 1):
                        pe.wait_ge(s["soft_step"], (n - 1) * SM_STEPS + SM_STEPS)
                    for j in range(T // 2):
                        c = q * 2 * T + i * T + 2 * j
                        for h in range(2):
                            last = pe.matmul(pL[:, c:c + 2], mz[:, 2 * i + h, j * P:(j + 1) * P], attr[:, layer, h, :],
                                             start=(h == 0), stop=(h == 1))
                last.then_inc(s["logits_ready"], 1)

            pe.wait_ge(s["falls_counted"], 1)
            pe.matmul(pL[0:1, 0:1], unsorted[:, :], ones[:, 0:1], start=True, stop=True).then_inc(s["falls_summed"], 1)
            pe.wait_ge(s["weights_made"], 1)
            pe.transpose(pT[0][:, 0:P], w1d[:, :], ident[:, :]).then_inc(s["w1_turned"], 1)
            pe.wait_ge(s["w1t_ready"], 1)
            pe.matmul(pS[:, 0:D], vrep[0:D, :], w2d[0:D, 0:D], start=True, stop=True)
            pe.matmul(pT[1][:, 0:P], w1t[:, :], w2d[:, :], start=True, stop=True).then_inc(s["w12_made"], 1)
            pe.wait_ge(s["consts_ready"], 1)

            def z_dense(k, b):
                if b == 0 and known(k, 1):
                    pe.wait_ge(s["z_dense_ready"], k)
                pe.wait_ge(s[f"dense{b}_out"], k + 1)
                for j in range(T // 2):
                    pe.matmul(pY[:, b, j * P:(j + 1) * P], htd[:, b, j * P:(j + 1) * P], w12[:, :],
                              start=(j == 0), stop=True, skip_group_check=True)
                last = pe.matmul(pY[:, b, :], ones_h[:, :], cb3[:, :], start=False, stop=True, skip_group_check=True)
                if b == 1:
                    last.then_inc(s["z_dense_made"], 1)

            def turn_src(k, r):
                pe.wait_ge(s["edges_step"], k * 4 + 2)
                if known(k, 1):
                    pe.wait_ge(s["dense1_out"], k)
                turned(pT[0], flat(H[:, r, 0:T, :]), s["hs_turned"])

            def turn_dst(k, r):
                pe.wait_ge(s["edges_step"], k * 4 + 4)
                if known(k, 3):
                    pe.wait_ge(s["h1t_ready"], k - 2)
                elif known(k, 1):
                    pe.wait_ge(s["dense0_out"], k)
                turned(pT[1], flat(H[:, r, T:2 * T, :]), s["hd_turned"])
                pe.wait_ge(s["attr_step"], k * AT_STEPS + AT_STEPS)
                pe.wait_ge(s["hs_out"], k + 1)
                for i, tile in enumerate((EA, LA)):
                    tile = flat(tile[:, r, :, :])
                    for j in range(2):
                        last = pe.transpose(pT[0][:, (2 * i + j) * P:(2 * i + j + 1) * P],
                                            tile[:, j * P:(j + 1) * P], ident[:, :])
                last.then_inc(s["ea_turned"], 1)

            def logit_rows(k, r):
                pe.wait_ge(s["hd_out"], k + 1)
                if known(k, 1):
                    pe.wait_ge(s["mz_m"], k)
                pe.matmul(pM[:, :], w1d[:, :], hts[:, 0, :], start=True, stop=False)
                pe.matmul(pM[:, :], w1d[:, :], hts[:, 1, :], start=False, stop=True)
                pe.wait_ge(s["el_ready"], k + 1)
                for j in range(T // 2):
                    last = pe.matmul(pM[:, j * P:(j + 1) * P], we[:, 0, j % 2, :],
                                     EL[:, r, j // 2 * P:(j // 2 + 1) * P], start=False, stop=True,
                                     skip_group_check=True)
                last.then_inc(s["rows_m"], 1)
                if known(k, 1):
                    pe.wait_ge(s["mz_s"], k)
                pe.matmul(pS[:, :], w1d2[:, :], hts[:, 1, :], start=True, stop=True)
                for j in range(T // 2):
                    last = pe.matmul(pS[:, j * P:(j + 1) * P], we[:, 0, j % 2, :],
                                     EL[:, r, (2 + j // 2) * P:(3 + j // 2) * P], start=False,
                                     stop=True, skip_group_check=True)
                last.then_inc(s["rows_s"], 1)

            def turn_edges(k, r, dense_ahead):
                pe.wait_ge(s["h1_ready"], k + 1)
                if dense_ahead:
                    pe.wait_ge(s["dense0_out"], k + 3)
                elif k == U - 1:
                    pe.wait_ge(s["h1t_ready"], k)
                turned(pT[1], flat(H1[:, r, :, :]), s["h1_turned"])

            def z_edges(k):
                pe.wait_ge(s["h1t_ready"], k + 1)
                if known(k, 1):
                    pe.wait_ge(s["z_edge_ready"], k)
                for j in range(T // 2):
                    pe.matmul(pZ[:, j * P:(j + 1) * P], h1t[:, j * P:(j + 1) * P], w12[:, :],
                              start=(j == 0), stop=True, skip_group_check=True)
                last = pe.matmul(pZ[:, :], ones_h[:, :], cb3[:, :], start=False, stop=True, skip_group_check=True)
                last.then_inc(s["z_edge_made"], 1)

            def turn(k, r):
                late = isinstance(k, int) and k >= U
                before = known(k, 1) and not late
                if not late:
                    turn_src(k, r)
                if before:
                    z_dense(k - 1, 0)
                if not late:
                    turn_dst(k, r)
                if before:
                    z_dense(k - 1, 1)
                if not late:
                    logit_rows(k, r)
                    pe.wait_ge(s["dense0_normed"], k + 1)
                    turned(pT[1], flat(HD[:, r, 0:T, :]), s["dense0_turned"])
                    pe.wait_ge(s["dense_normed"], k + 1)
                    turned(pT[0], flat(HD[:, r, T:2 * T, :]), s["dense1_turned"])
                    logits(k, r, 0)
                if isinstance(k, int) and k == U - 1:
                    z_dense(k, 0)
                    z_dense(k, 1)
                if known(k, 2):
                    turn_edges(k - 2, r, not late)
                    z_edges(k - 2)

            turns(pe, 0, 4, U - 1, turn)
            for k in range(U - 1, U + 2):
                turn(k, k % 2)

            def loop_logit(layer):
                pe.wait_ge(*((s["node_ready"], 1) if layer == 0 else (s["zh_in"], 16)))
                node = hh if layer == 0 else zh
                if layer == 0:
                    pe.transpose(pT[0][0:DE, P:2 * P], loopm[:, :], ident[:, :])
                pe.transpose(pT[0][0:D, 0:P], node[:, :], ident[:, :]).then_inc(s["node_turned"], 1)
                pe.wait_ge(s["node_out"], layer + 1)
                wn = w1d2 if layer == 0 else ident2
                pe.matmul(pM[0:D, 0:P], wn[0:D, 0:D], hht[0:D, :], start=True, stop=False)
                pe.matmul(pM[0:D, 0:P], we[0:DE, layer, 0, 0:D], lpt[:, :], start=False, stop=True
                          ).then_inc(s["loop_rows"], 1)
                pe.wait_ge(s["loop_leaky"], layer + 1)
                for h in range(2):
                    last = pe.matmul(pL[:, 4 * T:4 * T + 1], srz[:, h, :], attr[0:D, layer, h, 0:1],
                                     start=(h == 0), stop=(h == 1))
                last.then_inc(s["loop_logit"], 1)

            def seam(layer):
                pe.wait_ge(s["tails_ready"], layer + 1)
                for i, c in enumerate((14, 11, 10)):
                    last = pe.transpose(pS[0:1, i * P:(i + 1) * P], sm[:, c:c + 1], ident[:, :])
                last.then_inc(s["rows_turned"], 1)
                pe.transpose(pT[0][0:W + 2, 0:P], TS[:, :], ident[:, :]).then_inc(s["tails_turned"], 1)
                pe.wait_ge(s["row_exps"], layer + 1)
                pe.matmul(pM[:, 0:P], sel[:, 0, :], row[:, 7, 0:P], start=True, stop=False)
                pe.matmul(pM[:, 0:P], sel[:, 1, :], ones[0:1, :], start=False, stop=True)
                pe.matmul(pM[:, P:2 * P], sel[:, 0, :], row[:, 8, 0:P], start=True, stop=False)
                pe.matmul(pM[:, P:2 * P], sel[:, 1, :], row[:, 4, 0:P], start=False, stop=True
                          ).then_inc(s["decay_spread"], 1)
                pe.wait_ge(s["carries_made"], layer + 1)
                pe.transpose(pT[1][:, 0:W + 2], OT[0:W + 2, 0:P], ident[0:W + 2, 0:W + 2])
                pe.transpose(pS[:, 3 * P:3 * P + 1], row[:, 1, 0:P], ident[0:1, 0:1]).then_inc(s["carries_turned"], 1)
                if layer == 0:
                    loop_logit(0)

            seam(0)
            pe.wait_ge(s["fixv_ready"], 1)
            pe.transpose(pT[0][0:D, 0:P], fixv[:, 1, :], ident[:, :]).then_inc(s["fix_turned"], 1)
            pe.wait_ge(s["fixt_ready"], 1)
            pe.matmul(pM[:, 0:D], fixt[:, :], w12[0:D, 0:D], start=True, stop=True).then_inc(s["zfix_made"], 1)
            pe.wait_ge(s["zfix_ready"], 1)
            loop_logit(1)

            def turn3(k, r4):
                r = r4 % 2
                n = k + U
                pe.wait_ge(s[f"src2_in{r4}"], by_four(k, r4))
                pe.wait_ge(s[f"dst2_in{r}"], dma_uses(k, r, 48))
                pe.wait_ge(s["mz_m"], n)
                zs, zd = flat(ZS[r4]), flat(ZD[:, r, :, :])
                for j in range(T // 2):
                    c = slice(j * P, (j + 1) * P)
                    pe.matmul(pM[:, c], zs[:, c], ident[:, :], start=True, stop=False)
                    pe.matmul(pM[:, c], zd[:, c], ident[:, :], start=False, stop=False)
                    last = pe.matmul(pM[:, c], we[:, 1, j % 2, :], EL[:, r, j // 2 * P:(j // 2 + 1) * P],
                                     start=False, stop=True)
                last.then_inc(s["rows_m"], 1)
                pe.wait_ge(s["mz_s"], n)
                for j in range(T // 2):
                    c = slice(j * P, (j + 1) * P)
                    pe.matmul(pS[:, c], zd[:, c], ident2[:, :], start=True, stop=False)
                    last = pe.matmul(pS[:, c], we[:, 1, j % 2, :], EL[:, r, (2 + j // 2) * P:(3 + j // 2) * P],
                                     start=False, stop=True)
                last.then_inc(s["rows_s"], 1)
                pe.wait_ge(s["rows_s"], n + 1)
                pe.nop().then_inc(s["rows2_done"], 1)
                logits(n, r, 1)

            turns(pe, 0, 5, U, turn3, 4)
            seam(1)


_INS = ["x", "src", "dst", "edge_attr_32"] + [f"L0_gnn_{n}" for n in
        ("W1", "b1", "We1", "att1", "bias1", "W2", "b2", "We2", "att2", "bias2")]


def kernel(**inputs):
    import numpy as np
    import concourse.bacc as bacc
    from concourse.bass_utils import run_bass_kernel_spmd

    nc = bacc.Bacc("TRN2", target_bir_lowering=False, num_devices=1)
    arrays, args = {}, []
    for name in _INS:
        a = np.ascontiguousarray(inputs[name])
        arrays[f"in_{name}"] = a
        args.append(nc.dram_tensor(f"in_{name}", a.shape, mybir.dt.from_np(a.dtype), kind="ExternalInput").ap())
    out = nc.dram_tensor("out_0", tuple(inputs["x"].shape), F32, kind="ExternalOutput").ap()
    gnn_kernel(nc, *args, out)
    r = run_bass_kernel_spmd(nc, [arrays], core_ids=[0])
    return r.results[0]["out_0"]
```
